# Optimizing a Trainium2 kernel written in Bass

```python
import numpy as np
import jax
import jax.numpy as jnp

def _softmax(x, axis=-1):
    return jax.nn.softmax(x, axis=axis)

def _gelu(x):
    return jax.nn.gelu(x, approximate=True)

def _silu(x):
    return jax.nn.silu(x)

def _sigmoid(x):
    return jax.nn.sigmoid(x)

def _layernorm(x, axis=-1, eps=1e-05):
    m = jnp.mean(x, axis=axis, keepdims=True)
    v = jnp.var(x, axis=axis, keepdims=True)
    return (x - m) / jnp.sqrt(v + eps)

def _scatter_add(tgt, idx, src, axis=0):
    return tgt.at[idx].add(src)

def _segment_sum(src, seg, n):
    return jax.ops.segment_sum(src, seg, n)
kernel_name = 'mk_prb_d1_jaxref_r4_9ba0bd'

def setup_inputs(seed: int=0):
    np.random.seed(seed)
    _w = jnp.asarray

    def _L0_attn_setup():
        import jax, jax.numpy as jnp
        import numpy as np
        B, T, HIDDEN = (2, 1024, 512)
        NUM_HEADS, HEAD_K, HEAD_V = (6, 64, 128)
        KEY_DIM, VALUE_DIM = (NUM_HEADS * HEAD_K, NUM_HEADS * HEAD_V)
        CONV_K, CHUNK, EPS = (4, 64, 1e-05)

        def short_conv(x, w):
            K = w.shape[1]
            xp = jnp.pad(x, ((0, 0), (K - 1, 0), (0, 0)))
            y = sum((xp[:, i:i + x.shape[1], :] * w[:, i] for i in range(K)))
            return jax.nn.silu(y)

        def l2norm(x):
            return x * jax.lax.rsqrt(jnp.sum(x * x, -1, keepdims=True))

        def _step(S, xs):
            qt, kt, vt, gt, bt = xs
            S = S * jnp.exp(gt)[..., None, None]
            pred = jnp.einsum('bhk,bhkv->bhv', kt, S)
            delta = (vt - pred) * bt[..., None]
            S = S + jnp.einsum('bhk,bhv->bhkv', kt, delta)
            return (S, jnp.einsum('bhk,bhkv->bhv', qt, S))

        def _chunk(S, xs):
            return jax.lax.scan(_step, S, xs)
        _chunk_ckpt = jax.checkpoint(_chunk)

        def gated_delta_rule(q, k, v, g, beta):
            b, t, h, dk = q.shape
            dv = v.shape[-1]
            q = l2norm(q) * dk ** (-0.5)
            k = l2norm(k)
            nc = t // CHUNK

            def to_scan(x):
                x = x.reshape(b, nc, CHUNK, *x.shape[2:])
                return jnp.moveaxis(x, 0, 2)
            xs = tuple(map(to_scan, (q, k, v, g, beta)))
            S0 = jnp.zeros((b, h, dk, dv), q.dtype)
            _, o = jax.lax.scan(_chunk_ckpt, S0, xs)
            return jnp.moveaxis(o, 2, 0).reshape(b, t, h, dv)
        key = jax.random.key(seed)
        ks = jax.random.split(key, 14)

        def lin(k, fi, fo):
            return jax.random.normal(k, (fi, fo), jnp.float32) / np.sqrt(fi)
        A = jax.random.uniform(ks[11], (NUM_HEADS,), minval=0.001, maxval=16.0)
        dt = jnp.exp(jax.random.uniform(ks[12], (NUM_HEADS,)) * (np.log(0.1) - np.log(0.001)) + np.log(0.001))
        dt = jnp.clip(dt, 0.0001)
        return {'hidden_states': jax.random.normal(ks[0], (B, T, HIDDEN), jnp.float32), 'Wq': lin(ks[1], HIDDEN, KEY_DIM), 'Wk': lin(ks[2], HIDDEN, KEY_DIM), 'Wv': lin(ks[3], HIDDEN, VALUE_DIM), 'Wa': lin(ks[4], HIDDEN, NUM_HEADS), 'Wb': lin(ks[5], HIDDEN, NUM_HEADS), 'Wg': lin(ks[6], HIDDEN, VALUE_DIM), 'Wo': lin(ks[7], VALUE_DIM, HIDDEN), 'conv_wq': jax.random.normal(ks[8], (KEY_DIM, CONV_K), jnp.float32) / np.sqrt(CONV_K), 'conv_wk': jax.random.normal(ks[9], (KEY_DIM, CONV_K), jnp.float32) / np.sqrt(CONV_K), 'conv_wv': jax.random.normal(ks[10], (VALUE_DIM, CONV_K), jnp.float32) / np.sqrt(CONV_K), 'A_log': jnp.log(A), 'dt_bias': dt + jnp.log(-jnp.expm1(-dt)), 'norm_weight': jnp.ones((HEAD_V,), jnp.float32)}
    _L0_attn_in = _L0_attn_setup()

    def _L0_ffn_setup():
        import jax, jax.numpy as jnp
        import numpy as np
        HIDDEN = 512
        INTER = 2048
        COMPRESSION = 128.9

        def _n_ctrl(out_size, in_size):
            return max(16, int(out_size * in_size / COMPRESSION))

        def _catmull_rom_grid(n_ctrl, n_samples):
            t = np.linspace(0.0, n_ctrl - 1.0, n_samples, dtype=np.float64)
            i = np.clip(np.floor(t).astype(np.int64), 0, n_ctrl - 2)
            f = (t - i).astype(np.float32)
            idx = np.stack([np.clip(i + k, 0, n_ctrl - 1) for k in (-1, 0, 1, 2)], axis=0)
            return (jnp.asarray(idx.astype(np.int32)), jnp.asarray(f))

        def spline_reconstruct(control_points, out_size, in_size):
            n = out_size * in_size
            idx, f = _catmull_rom_grid(control_points.shape[0], n)
            p0, p1, p2, p3 = (control_points[idx[0]], control_points[idx[1]], control_points[idx[2]], control_points[idx[3]])
            f2 = f * f
            f3 = f2 * f
            w = 0.5 * (2.0 * p1 + (p2 - p0) * f + (2.0 * p0 - 5.0 * p1 + 4.0 * p2 - p3) * f2 + (3.0 * p1 - p0 - 3.0 * p2 + p3) * f3)
            return w.reshape(out_size, in_size)
        key = jax.random.key(seed)
        k0, k1, k2, k3 = jax.random.split(key, 4)
        hidden_states = jax.random.normal(k0, (4, 512, HIDDEN), dtype=jnp.float32)
        gate_cp = jax.random.normal(k1, (_n_ctrl(INTER, HIDDEN),), dtype=jnp.float32) * 0.02
        up_cp = jax.random.normal(k2, (_n_ctrl(INTER, HIDDEN),), dtype=jnp.float32) * 0.02
        down_cp = jax.random.normal(k3, (_n_ctrl(HIDDEN, INTER),), dtype=jnp.float32) * 0.02
        return {'hidden_states': hidden_states, 'gate_cp': gate_cp, 'up_cp': up_cp, 'down_cp': down_cp}
    _L0_ffn_in = _L0_ffn_setup()
    _d = {'L0_attn_hidden_states': _L0_attn_in['hidden_states'], 'L0_attn_Wq': _L0_attn_in['Wq'], 'L0_attn_Wk': _L0_attn_in['Wk'], 'L0_attn_Wv': _L0_attn_in['Wv'], 'L0_attn_Wa': _L0_attn_in['Wa'], 'L0_attn_Wb': _L0_attn_in['Wb'], 'L0_attn_Wg': _L0_attn_in['Wg'], 'L0_attn_Wo': _L0_attn_in['Wo'], 'L0_attn_conv_wq': _L0_attn_in['conv_wq'], 'L0_attn_conv_wk': _L0_attn_in['conv_wk'], 'L0_attn_conv_wv': _L0_attn_in['conv_wv'], 'L0_attn_A_log': _L0_attn_in['A_log'], 'L0_attn_dt_bias': _L0_attn_in['dt_bias'], 'L0_attn_norm_weight': _L0_attn_in['norm_weight'], 'L0_ffn_gate_cp': _L0_ffn_in['gate_cp'], 'L0_ffn_up_cp': _L0_ffn_in['up_cp'], 'L0_ffn_down_cp': _L0_ffn_in['down_cp']}
    _x0 = _d['L0_attn_hidden_states']
    _d['L0_attn_hidden_states'] = jax.random.normal(jax.random.fold_in(jax.random.key(seed), 1), (1, 2048, 512), dtype=_x0.dtype)
    del _x0
    return _d

def reference(L0_attn_hidden_states, L0_attn_Wq, L0_attn_Wk, L0_attn_Wv, L0_attn_Wa, L0_attn_Wb, L0_attn_Wg, L0_attn_Wo, L0_attn_conv_wq, L0_attn_conv_wk, L0_attn_conv_wv, L0_attn_A_log, L0_attn_dt_bias, L0_attn_norm_weight, L0_ffn_gate_cp, L0_ffn_up_cp, L0_ffn_down_cp):

    def _L0_attn_ref(hidden_states, Wq, Wk, Wv, Wa, Wb, Wg, Wo, conv_wq, conv_wk, conv_wv, A_log, dt_bias, norm_weight):
        import jax, jax.numpy as jnp
        import numpy as np
        B, T, HIDDEN = (2, 1024, 512)
        NUM_HEADS, HEAD_K, HEAD_V = (6, 64, 128)
        KEY_DIM, VALUE_DIM = (NUM_HEADS * HEAD_K, NUM_HEADS * HEAD_V)
        CONV_K, CHUNK, EPS = (4, 64, 1e-05)

        def short_conv(x, w):
            K = w.shape[1]
            xp = jnp.pad(x, ((0, 0), (K - 1, 0), (0, 0)))
            y = sum((xp[:, i:i + x.shape[1], :] * w[:, i] for i in range(K)))
            return jax.nn.silu(y)

        def l2norm(x):
            return x * jax.lax.rsqrt(jnp.sum(x * x, -1, keepdims=True))

        def _step(S, xs):
            qt, kt, vt, gt, bt = xs
            S = S * jnp.exp(gt)[..., None, None]
            pred = jnp.einsum('bhk,bhkv->bhv', kt, S)
            delta = (vt - pred) * bt[..., None]
            S = S + jnp.einsum('bhk,bhv->bhkv', kt, delta)
            return (S, jnp.einsum('bhk,bhkv->bhv', qt, S))

        def _chunk(S, xs):
            return jax.lax.scan(_step, S, xs)
        _chunk_ckpt = jax.checkpoint(_chunk)

        def gated_delta_rule(q, k, v, g, beta):
            b, t, h, dk = q.shape
            dv = v.shape[-1]
            q = l2norm(q) * dk ** (-0.5)
            k = l2norm(k)
            nc = t // CHUNK

            def to_scan(x):
                x = x.reshape(b, nc, CHUNK, *x.shape[2:])
                return jnp.moveaxis(x, 0, 2)
            xs = tuple(map(to_scan, (q, k, v, g, beta)))
            S0 = jnp.zeros((b, h, dk, dv), q.dtype)
            _, o = jax.lax.scan(_chunk_ckpt, S0, xs)
            return jnp.moveaxis(o, 2, 0).reshape(b, t, h, dv)
        b, t, _ = hidden_states.shape
        q = short_conv(hidden_states @ Wq, conv_wq).reshape(b, t, NUM_HEADS, HEAD_K)
        k = short_conv(hidden_states @ Wk, conv_wk).reshape(b, t, NUM_HEADS, HEAD_K)
        v = short_conv(hidden_states @ Wv, conv_wv).reshape(b, t, NUM_HEADS, HEAD_V)
        beta = jax.nn.sigmoid(hidden_states @ Wb)
        g = -jnp.exp(A_log) * jax.nn.softplus(hidden_states @ Wa + dt_bias)
        o = gated_delta_rule(q, k, v, g, beta)
        gate = (hidden_states @ Wg).reshape(b, t, NUM_HEADS, HEAD_V)
        o = o * jax.lax.rsqrt(jnp.mean(o * o, -1, keepdims=True) + EPS) * norm_weight
        o = o * jax.nn.silu(gate)
        return o.reshape(b, t, VALUE_DIM) @ Wo

    def _L0_ffn_ref(hidden_states, gate_cp, up_cp, down_cp):
        import jax, jax.numpy as jnp
        import numpy as np
        HIDDEN = 512
        INTER = 2048
        COMPRESSION = 128.9

        def _n_ctrl(out_size, in_size):
            return max(16, int(out_size * in_size / COMPRESSION))

        def _catmull_rom_grid(n_ctrl, n_samples):
            t = np.linspace(0.0, n_ctrl - 1.0, n_samples, dtype=np.float64)
            i = np.clip(np.floor(t).astype(np.int64), 0, n_ctrl - 2)
            f = (t - i).astype(np.float32)
            idx = np.stack([np.clip(i + k, 0, n_ctrl - 1) for k in (-1, 0, 1, 2)], axis=0)
            return (jnp.asarray(idx.astype(np.int32)), jnp.asarray(f))

        def spline_reconstruct(control_points, out_size, in_size):
            n = out_size * in_size
            idx, f = _catmull_rom_grid(control_points.shape[0], n)
            p0, p1, p2, p3 = (control_points[idx[0]], control_points[idx[1]], control_points[idx[2]], control_points[idx[3]])
            f2 = f * f
            f3 = f2 * f
            w = 0.5 * (2.0 * p1 + (p2 - p0) * f + (2.0 * p0 - 5.0 * p1 + 4.0 * p2 - p3) * f2 + (3.0 * p1 - p0 - 3.0 * p2 + p3) * f3)
            return w.reshape(out_size, in_size)
        gate_w = spline_reconstruct(gate_cp, INTER, HIDDEN)
        up_w = spline_reconstruct(up_cp, INTER, HIDDEN)
        down_w = spline_reconstruct(down_cp, HIDDEN, INTER)
        gate = jnp.einsum('bsh,ih->bsi', hidden_states, gate_w)
        up = jnp.einsum('bsh,ih->bsi', hidden_states, up_w)
        inter = jax.nn.silu(gate) * up
        return jnp.einsum('bsi,hi->bsh', inter, down_w)
    x = L0_attn_hidden_states
    xn = _layernorm(x, axis=-1)
    x = x + _L0_attn_ref(xn, L0_attn_Wq, L0_attn_Wk, L0_attn_Wv, L0_attn_Wa, L0_attn_Wb, L0_attn_Wg, L0_attn_Wo, L0_attn_conv_wq, L0_attn_conv_wk, L0_attn_conv_wv, L0_attn_A_log, L0_attn_dt_bias, L0_attn_norm_weight) + _L0_ffn_ref(xn, L0_ffn_gate_cp, L0_ffn_up_cp, L0_ffn_down_cp)
    return x

_drawn_inputs = setup_inputs


def setup_inputs(seed=0):
    import zlib

    import numpy as np

    out = dict(_drawn_inputs(seed))
    spreads = {'L0_attn_norm_weight': (1.0, 0.2)}
    factors = {}
    for name, (base, spread) in spreads.items():
        noise = np.random.default_rng([zlib.crc32(name.encode()), seed]).standard_normal(out[name].shape)
        drawn = base * np.exp(spread * noise) if base else spread * noise
        out[name] = jnp.asarray(drawn.astype(out[name].dtype))
    for name, factor in factors.items():
        out[name] = (out[name] * factor).astype(out[name].dtype)
    return out
```

```python
import concourse.bass as bass
from concourse import mybir
from contextlib import ExitStack
import numpy as np

F32 = mybir.dt.float32
F16 = mybir.dt.float16
BF16 = mybir.dt.bfloat16
U8 = mybir.dt.uint8
ALU = mybir.AluOpType
ACT = mybir.ActivationFunctionType

T_ALL, D = 2048, 512
HB = D // 128
ST = 512
NST = T_ALL // ST
CH = 128
NCH = ST // CH
NH, DK, DV = 6, 64, 128
NPAIR = NH // 2
KD, VD = NH * DK, NH * DV
TAPS = 4
NQK = 2 * KD // 128
NV = VD // 128
NBLK = NQK + NV
WCOLS = 2 * KD + 2 * VD
EPS = 1e-5
INTER = 2048
IB = INTER // 128
SUB = 32
NSUB = CH // SUB
NINST = NSUB * NCH * NH
W_SCALE = 64.0
NCP = max(16, int(INTER * D / 128.9))
NCOL = INTER * D // 128
NCR = NCOL // 128
HALF = NH // 2 * 128
KQ_HEADS = ((0, 2), (1, 3), (4,), (5,))


def spline_shapes():
    n = NCOL * 128
    t = np.linspace(0.0, NCP - 1.0, n, dtype=np.float64)
    i = np.clip(np.floor(t).astype(np.int64), 0, NCP - 2)
    first = i.reshape(NCOL, 128)[:, 0]
    knot = (i.reshape(NCOL, 128) == first[:, None]).sum(axis=1)
    frac = (t.reshape(NCOL, 128)[:, 0] - first).astype(np.float32).reshape(128, NCR)
    step = (NCP - 1.0) / (n - 1)
    powers = np.stack([(np.arange(128) * step) ** k for k in range(4)])
    hi = powers.astype(np.float16)
    lo = (powers - hi).astype(np.float16)
    shift = np.arange(NCOL) - first
    cuts = [0] + [int(c) for c in np.nonzero(np.diff(shift))[0] + 1] + [NCOL]
    runs = [(a, b, int(first[a])) for a, b in zip(cuts[:-1], cuts[1:])]
    rows = np.arange(128, dtype=np.float32).reshape(128, 1)
    return runs, frac, knot.astype(np.float32), rows, np.concatenate([hi, lo, hi]).astype(np.float32)


class At:

    def __init__(self, reg, off):
        self.reg, self.off = reg, off

    def val(self, per, n):
        assert self.first() or self.off * per + n > 0
        return self.off * per + n if self.reg is None else self.reg * per + (self.off * per + n)

    def idx(self):
        return self.off if self.reg is None else self.reg + self.off

    def first(self):
        return self.reg is None and self.off == 0


class Steps:

    def __init__(self, per):
        self.per, self.n = per, 0

    def start(self, at):
        assert self.n in (0, self.per), (self.n, self.per)
        self.at, self.n = at, 0

    def next(self):
        self.n += 1
        return self.at.val(self.per, self.n)


def bank_uses():
    order = []
    ring = [("ln", t) for t in range(NCH)] + [("ab",)]
    ring += [("gate", c, h) for c in range(NCH) for h in range(2)]
    ring += [("blk", n) for n in range(NQK)] + [("sums",)] + [("ktr", c) for c in range(NCH)]
    ring += [("blk", NQK + n) for n in range(NV)] + [("vtr", n) for n in range(NV)]
    order += [(i % 2, u) for i, u in enumerate(ring)]
    for c in range(NCH):
        order += [(2, ("D", c, 0)), (3, ("D", c, 1))] + [(4 + p, ("KQ", c, p)) for p in range(len(KQ_HEADS))]
    for k in range(NCH + 3):
        if k < NCH:
            order += [(2, ("X", k, 0)), (3, ("X", k, 1))]
        if 0 <= k - 1 < NCH:
            order += [(4, ("Y", k - 1)), (5, ("Z", k - 1, 0)), (6, ("Z", k - 1, 1))]
        if 0 <= k - 2 < NCH:
            order += [(7, ("X2", k - 2))]
        if 0 <= k - 3 < NCH:
            order += [(4, ("Z2", k - 3))]
    for c in range(NCH + 1):
        if c < NCH:
            order += [(2, ("KS", c, 0)), (3, ("KS", c, 1)), (6, ("QS", c, 0)), (7, ("QS", c, 1)),
                      (4, ("U", c, 0)), (5, ("U", c, 1)), (4, ("dS", c)),
                      (2, ("AU", c, 0)), (3, ("AU", c, 1))]
        if c >= 1:
            order += [(5, ("OT", c - 1, 0)), (6, ("OT", c - 1, 1)), (7, ("WO", c - 1))]
    per, table = [0] * 8, {}
    for bank, u in order:
        table[u] = (bank, per[bank])
        per[bank] += 1
    return table, per


def prepare(nc, A, scr, P):
    runs = A.runs
    with ExitStack() as ctx:
        def sb(name, shape, dt=F32):
            return ctx.enter_context(nc.sbuf_tensor(name, shape, dt))

        def sem(name):
            return ctx.enter_context(nc.semaphore(name))

        NSTG = 4
        stage = sb("w_stage", [128, NSTG, HB * 384])
        ab_stage = sb("ab_stage", [128, HB, 2 * NH])
        nw = sb("nw", [128, 1])
        nw_s = sb("nw_s", [128, 1])
        ctrl = sb("ctrl", [128, 3, 5, NCR])
        frac = sb("frac", [128, NCR])
        frac1 = sb("frac1", [128, NCR])
        co = sb("co", [128, 4, 3, NCR])
        t1 = sb("sp_t1", [128, 3, NCR])
        t2 = sb("sp_t2", [128, 3, NCR])
        dcf = sb("dcf", [128, 2, 4, 3, NCR])
        dsp = sb("dsp", [128, 2, 2, 4, 3, NCR], F16)
        staged = [sem(f"staged{i}") for i in range(NSTG)]
        small_in, hi_done, lo_done = sem("small_in"), sem("hi_done"), sem("lo_done")
        const_made, padded, gathered = sem("const_made"), sem("padded"), sem("gathered")
        ctrl_in, sp_step, coef_hi, coef_out = sem("ctrl_in"), sem("sp_step"), sem("coef_hi"), sem("coef_out")
        nw_ready, coef_lo = sem("nw_ready"), sem("coef_lo")
        block = ctx.enter_context(nc.Block())

        pieces = [(A.Wk, 0, 0), (A.Wq, 0, KD)]
        pieces += [(A.Wv, 384 * i, 2 * KD + 384 * i) for i in range(2)]
        pieces += [(A.Wg, 384 * i, 2 * KD + VD + 384 * i) for i in range(2)]
        wo_v = A.Wo.rearrange("(h p) n -> p h n", p=128)
        NP_ = len(pieces) + 2

        def parts(i):
            if i < len(pieces):
                col = pieces[i][2]
                return (stage[:, i % NSTG, :].rearrange("p (b n) -> p b n", b=HB),
                        P.w_hi[:, :, col:col + 384], P.w_lo[:, :, col:col + 384])
            h0 = 3 * (i - len(pieces))
            return (stage[:, i % NSTG, :].rearrange("p (h n) -> p h n", h=3),
                    P.wo_hi[:, h0:h0 + 3, :], P.wo_lo[:, h0:h0 + 3, :])

        @block.sync
        def _(sp):
            cps = (A.gate_cp, A.up_cp, A.down_cp)
            for m, cp in enumerate(cps):
                row = cp.rearrange("(a n) -> a n", a=1)
                sp.dma_start(scr.pad[m:m + 1, 1:1 + NCP], row).then_inc(padded, 16)
                sp.dma_start(scr.pad[m:m + 1, 0:1], row[:, 0:1]).then_inc(padded, 16)
                for e in range(2):
                    sp.dma_start(scr.pad[m:m + 1, 1 + NCP + e:2 + NCP + e], row[:, NCP - 1:NCP]).then_inc(padded, 16)
            sp.dma_start(nw[:], A.nw.rearrange("(p a) -> p a", a=1)).then_inc(small_in, 16)
            ab = ab_stage[:]
            sp.dma_start(ab[:, :, 0:NH], A.Wa.rearrange("(b p) n -> p b n", p=128)).then_inc(small_in, 16)
            sp.dma_start(ab[:, :, NH:2 * NH], A.Wb.rearrange("(b p) n -> p b n", p=128)).then_inc(small_in, 16)
            sp.dma_start(frac[:], A.frac).then_inc(small_in, 16)
            for b in range(NPAIR):
                for which, w in enumerate((A.cwk, A.cwq)):
                    sp.dma_start(P.taps[:, NPAIR * which + b, :], w[128 * b:128 * b + 128, :]).then_inc(small_in, 16)
            sp.dma_start(P.taps[:, NQK:NBLK, :], A.cwv.rearrange("(b p) t -> p b t", p=128)).then_inc(small_in, 16)
            sp.dma_start(P.dtb[:], A.dt_bias.partition_broadcast(128)).then_inc(small_in, 16)
            sp.dma_start(P.nega[:], A.A_log.partition_broadcast(128)).then_inc(small_in, 16)
            sp.wait_ge(padded, 12 * 16)
            for c0, c1, j0 in runs:
                src = bass.AP(tensor=scr.pad.tensor, offset=scr.pad.offset + j0,
                              ap=[[NCP + 3, 3], [1, 5], [1, c1 - c0]])
                sp.dma_start(scr.ctrl[:, :, c0:c1], src, allow_slow_non_contiguous=c1 - c0 == 1).then_inc(gathered, 16)
            sp.wait_ge(gathered, 16 * len(runs))
            for m in range(3):
                sp.dma_start(ctrl[:, m, :, :], scr.ctrl[m].rearrange("k (q r) -> q k r", r=NCR)).then_inc(ctrl_in, 16)
            sp.wait_ge(coef_lo, 1)
            for a in range(2):
                for part in range(2):
                    for m in range(3):
                        sp.dma_start(scr.coef[part, :, m, a, :].rearrange("k (q r) -> q k r", r=NCR),
                                     dsp[:, a, part, :, m, :]).then_inc(coef_out, 16)
            sp.wait_ge(coef_out, 12 * 16)

        @block.scalar
        def _(act):
            def load(i):
                dst = parts(i)[0]
                if i < len(pieces):
                    w, c0, _ = pieces[i]
                    src = w.rearrange("(b p) n -> p b n", p=128)[:, :, c0:c0 + 384]
                else:
                    h0 = 3 * (i - len(pieces))
                    src = wo_v[:, h0:h0 + 3, :]
                act.dma_start(dst, src).then_inc(staged[i % NSTG], 16)

            for i in range(NSTG):
                load(i)
            for i in range(NP_):
                act.wait_ge(staged[i % NSTG], 16 * (i // NSTG + 1))
                src, hi, _ = parts(i)
                if i == len(pieces):
                    act.wait_ge(small_in, 16 * 13)
                    nc.scalar.activation(nw_s[:], nw[:], ACT.Copy, scale=W_SCALE).then_inc(nw_ready, 1)
                    act.wait_ge(nw_ready, 1)
                scale = W_SCALE if i < len(pieces) else nw_s[:]
                nc.scalar.activation(hi, src, ACT.Copy, scale=scale).then_inc(hi_done, 1)
                if i >= 1 and i - 1 + NSTG < NP_:
                    act.wait_ge(lo_done, i)
                    load(i - 1 + NSTG)
            nc.scalar.activation(P.wab_hi[:], ab_stage[:], ACT.Copy, scale=W_SCALE).then_inc(hi_done, 1)
            nc.scalar.activation(P.nega[:], P.nega[:], ACT.Exp).then_inc(nw_ready, 1)
            act.wait_ge(nw_ready, 2)
            nc.scalar.activation(P.nega[:], P.nega[:], ACT.Copy, scale=-1.0).then_inc(nw_ready, 1)
            act.wait_ge(sp_step, 1 + 2 * 20)
            nc.scalar.activation(dsp[:, :, 0, :, :, :], dcf[:], ACT.Copy, scale=W_SCALE).then_inc(coef_hi, 1)

        @block.vector
        def _(dve):
            for i in range(NP_):
                dve.wait_ge(hi_done, i + 1)
                src, hi, lo = parts(i)
                scale = W_SCALE if i < len(pieces) else nw_s[:]
                nc.vector.scalar_tensor_tensor(out=lo, in0=src, scalar=scale, in1=hi,
                                               op0=ALU.mult, op1=ALU.subtract).then_inc(lo_done, 1)
            dve.wait_ge(hi_done, NP_ + 1)
            nc.vector.scalar_tensor_tensor(out=P.wab_lo[:], in0=ab_stage[:], scalar=W_SCALE, in1=P.wab_hi[:],
                                           op0=ALU.mult, op1=ALU.subtract).then_inc(lo_done, 1)
            step = [0]

            def link(ins):
                step[0] += 1
                ins.then_inc(sp_step, 1)
                dve.wait_ge(sp_step, step[0])

            dve.wait_ge(small_in, 16 * 13)
            link(nc.vector.tensor_scalar(frac1[:], frac[:], -1.0, None, ALU.add))
            dve.wait_ge(ctrl_in, 48)
            stt = nc.vector.scalar_tensor_tensor
            for a in range(2):
                p0, p1, p2, p3 = (ctrl[:, :, a + k, :] for k in range(4))
                u = (frac if a == 0 else frac1)[:, :].unsqueeze(1).broadcast_to([128, 3, NCR])
                c1, c2, c3 = (co[:, k, :, :] for k in range(1, 4))
                link(nc.vector.tensor_tensor(t1[:], p1, p2, ALU.subtract))
                link(nc.vector.tensor_tensor(t2[:], p3, p0, ALU.subtract))
                link(nc.vector.tensor_scalar(t2[:], t2[:], 0.5, None, ALU.mult))
                link(stt(out=c3, in0=t1[:], scalar=1.5, in1=t2[:], op0=ALU.mult, op1=ALU.add))
                link(nc.vector.tensor_tensor(t2[:], p2, p0, ALU.subtract))
                link(nc.vector.tensor_scalar(c1, t2[:], 0.5, None, ALU.mult))
                link(stt(out=t1[:], in0=p1, scalar=-2.5, in1=p0, op0=ALU.mult, op1=ALU.add))
                link(stt(out=t1[:], in0=p2, scalar=2.0, in1=t1[:], op0=ALU.mult, op1=ALU.add))
                link(stt(out=c2, in0=p3, scalar=-0.5, in1=t1[:], op0=ALU.mult, op1=ALU.add))
                link(nc.vector.tensor_tensor(t1[:], c3, u, ALU.mult))
                link(stt(out=dcf[:, a, 2, :, :], in0=t1[:], scalar=3.0, in1=c2, op0=ALU.mult, op1=ALU.add))
                link(nc.vector.tensor_tensor(t2[:], dcf[:, a, 2, :, :], c2, ALU.add))
                link(nc.vector.tensor_tensor(t2[:], t2[:], u, ALU.mult))
                link(nc.vector.tensor_tensor(dcf[:, a, 1, :, :], t2[:], c1, ALU.add))
                link(nc.vector.tensor_tensor(t1[:], t1[:], c2, ALU.add))
                link(nc.vector.tensor_tensor(t1[:], t1[:], u, ALU.mult))
                link(nc.vector.tensor_tensor(t1[:], t1[:], c1, ALU.add))
                last = nc.vector.tensor_copy(dcf[:, a, 3, :, :], c3)
                link(last)
                link(nc.vector.tensor_tensor(t1[:], t1[:], u, ALU.mult))
                link(nc.vector.tensor_tensor(dcf[:, a, 0, :, :], t1[:], p1, ALU.add))
            dve.wait_ge(coef_hi, 1)
            nc.vector.scalar_tensor_tensor(
                out=dsp[:, :, 1, :, :, :].rearrange("p a k m r -> p a (k m r)"),
                in0=dcf[:].rearrange("p a k m r -> p a (k m r)"), scalar=W_SCALE,
                in1=dsp[:, :, 0, :, :, :].rearrange("p a k m r -> p a (k m r)"),
                op0=ALU.mult, op1=ALU.subtract).then_inc(coef_lo, 1)

        @block.gpsimd
        def _(pool):
            n = [0]

            def made(ins):
                n[0] += 1
                ins.then_inc(const_made, 1)
                pool.wait_ge(const_made, n[0])

            g = nc.gpsimd
            made(g.memset(P.ident[:], 0.0))
            made(g.affine_select(out=P.ident[:], in_=P.ident[:], compare_op=ALU.not_equal, fill=1.0, base=0,
                                 pattern=[[-1, 128]], channel_multiplier=1))
            made(g.memset(P.ones[:], 1.0))
            made(g.affine_select(out=P.after[:], in_=P.ones[:], compare_op=ALU.is_gt, fill=0.0, base=0,
                                 pattern=[[-1, 128]], channel_multiplier=1))
            made(g.affine_select(out=P.upto[:], in_=P.ones[:], compare_op=ALU.is_ge, fill=0.0, base=0,
                                 pattern=[[1, 128]], channel_multiplier=-1))
            made(g.memset(P.level32[:], 0.0))
            for b in (1, 3):
                made(g.memset(P.level32[SUB * b:SUB * b + SUB, SUB * (b - 1):SUB * b], 1.0))
            made(g.memset(P.pair[:], 0.0))
            for b in range(2):
                made(g.memset(P.pair[DK * b:DK * b + DK, b:b + 1], 1.0))
            made(g.memset(P.mhalf[:], -0.5))
            made(g.memset(P.phalf[:], 0.5))
            made(g.memset(P.S[:], 0.0))
            made(g.memset(P.halo[:], 0.0))
            made(g.memset(P.zeros[:], 0.0))


def attend(nc, A, scr, P, nst=NST):
    uses, per = bank_uses()
    with ExitStack() as ctx:
        def sb(name, shape, dt=F32):
            return ctx.enter_context(nc.sbuf_tensor(name, shape, dt))

        def sem(name):
            return ctx.enter_context(nc.semaphore(name))

        NCHH = NCH * NH
        xb = sb("xb", [128, NCH, D])
        x_hi = sb("x_hi", [128, HB, ST], F16)
        x_lo = sb("x_lo", [128, HB, ST], F16)
        raw = sb("raw", [128, 3, ST + TAPS - 1])
        cv = sb("cv", [128, 2, ST])
        kq = sb("kq", [128, NPAIR, 2, ST])
        vT = sb("vT", [128, 3, ST])
        V = sb("V", [128, NCH, NH, DV])
        gate = sb("gate", [128, NCH, VD])
        ktok = sb("ktok", [128, NCH, KD])
        BA = sb("BA", [128, 2, NCHH, CH])
        eg = sb("eg", [128, 2, NH, CH])
        Tbd = sb("Tbd", [128, NCHH, CH])
        W = sb("W", [128, NCHH, CH])
        T1 = sb("T1", [64, 2, NH, 64])
        X2s = sb("X2s", [128, 2, NH, 64])
        og_hi = sb("og_hi", [128, NH, CH], F16)
        og_lo = sb("og_lo", [128, NH, CH], F16)
        xr = sb("xr", [128, 2, D])
        junk = sb("junk", [128, NH, DV], BF16)
        bin_ = sb("bin", [NINST, SUB * SUB])
        tin = sb("tin", [NINST, SUB * SUB])
        tmp = sb("tmp", [NINST, 256])
        mv = sb("mv", [128, NCH, 2])
        stats = sb("stats", [128, NCH, 6])
        rstd = sb("rstd", [128, NCH])
        ln_d = sb("ln_d", [128, NCH])
        ab = sb("ab", [128, NCH, 2 * NH])
        z, az, nb, e1, ln1, beta, g = (sb(n, [128, NCH, NH]) for n in ("z", "az", "nb", "e1", "ln1", "beta", "g"))
        eb = sb("eb", [128, NCH, NH])
        sums = sb("sums", [128, 5 * NCHH])
        rk2, cj, eq, nk, gam, ngam, suf, ks = (sb(n, [128, NCHH]) for n in
                                               ("rk2", "cj", "eq", "nk", "gam", "ngam", "suf", "ks"))
        gC = sb("gC", [128, NCH, NPAIR])
        ss = sb("ss", [128, 2, NH])
        t6 = sb("t6", [128, 2, NH])
        rn = sb("rn", [128, 2, NH])
        rb = BA[:, 0, :, :]
        Rr, U = rb[:, 0:NH, :], rb[:, NH:2 * NH, :]
        O = rb[:, 2 * NH:4 * NH, :].rearrange("p (r h) d -> p r h d", r=2)
        sq = BA[:, 1, :, :].rearrange("p (n a) c -> p n (a c)", n=NQK)
        E, gm = eg[:, 0], eg[:, 1]
        bank = [ctx.enter_context(nc.psum_tensor(f"bank{i}", [128, 512], F32)) for i in range(8)]
        full = [sem(f"full{i}") for i in range(8)]
        done = [sem(f"done{i}") for i in range(8)]
        x_in, ln_step, ln_stats, ln_rstd, xn_ready = sem("x_in"), sem("ln_step"), sem("ln_stats"), sem("ln_rstd"), sem("xn_ready")
        xhi_ready, spilled = sem("xhi_ready"), sem("spilled")
        ab_ready, ab_exp, ab_ln, g_ready = sem("ab_ready"), sem("ab_exp"), sem("ab_ln"), sem("g_ready")
        dve_step, t32_step = sem("dve_step"), sem("t32_step")
        halo_used, raw_ready, cv_ready, silu_done, sq_ready = (
            sem("halo_used"), sem("raw_ready"), sem("cv_ready"), sem("silu_done"), sem("sq_ready"))
        dec_ready, ssq_ready, nk_ready, ks_ready = sem("dec_ready"), sem("ssq_ready"), sem("nk_ready"), sem("ks_ready")
        gm_ready, e_ready = sem("gm_ready"), sem("e_ready")
        b_out, b_in, t_out, tt_out, tw_in = sem("b_out"), sem("b_in"), sem("t_out"), sem("tt_out"), sem("tw_in")
        ss_ready, t6_ready, rn_ready, og_ready, oghi_ready = (
            sem("ss_ready"), sem("t6_ready"), sem("rn_ready"), sem("og_ready"), sem("oghi_ready"))
        xr_in = [sem(f"xr_in{i}") for i in range(2)]
        y_out = [sem(f"y_out{i}") for i in range(2)]
        block = ctx.enter_context(nc.Block())

        x_v = A.x.rearrange("(s t p) d -> s p t d", t=NCH, p=128)
        y_v = scr.y.rearrange("(s t p) d -> s t p d", t=NCH, p=128)
        xr_v = A.x.rearrange("(s t p) d -> s t p d", t=NCH, p=128)

        def filled(eng, u, s):
            b, n = uses[u]
            eng.wait_ge(full[b], s.val(per[b], n + 1))

        def ready(eng, u, s):
            b, n = uses[u]
            eng.wait_ge(done[b], s.val(per[b], n + 1))

        def out_of(u):
            return bank[uses[u][0]], done[uses[u][0]]

        def ch(c, h):
            return NH * c + h

        @block.tensor
        def _(pe):
            def claim(u, s):
                b, n = uses[u]
                if not (s.first() and n == 0):
                    pe.wait_ge(done[b], s.val(per[b], n))
                return bank[b], full[b]

            def split_product(out, w_hi, w_lo, x_hi_, x_lo_, swap, first=True, last=True):
                todo = ((w_hi, x_hi_), (w_hi, x_lo_), (w_lo, x_hi_))
                for i, (w, xx) in enumerate(todo):
                    a, b = (xx, w) if swap else (w, xx)
                    ins = nc.tensor.matmul(out, a, b, start=first and i == 0, stop=last and i == 2)
                return ins

            def ln_transposes(s):
                for t in range(NCH):
                    pe.wait_ge(xn_ready, s.val(NCH, t + 1))
                    ps, f = claim(("ln", t), s)
                    for hb in range(HB):
                        ins = nc.tensor.transpose(ps[:, 128 * hb:128 * hb + 128], xb[:, t, 128 * hb:128 * hb + 128], P.ident[:])
                    ins.then_inc(f, 1)

            def decay_products(s):
                ps, f = claim(("ab",), s)
                for t in (NCH - 2, NCH - 1):
                    ready(pe, ("ln", t), s)
                for c in range(NCH):
                    for hb in range(HB):
                        ins = split_product(ps[:, 2 * NH * c:2 * NH * (c + 1)], P.wab_hi[:, hb, :], P.wab_lo[:, hb, :],
                                            x_hi[:, hb, CH * c:CH * c + CH], x_lo[:, hb, CH * c:CH * c + CH], True,
                                            hb == 0, hb == HB - 1)
                ins.then_inc(f, 1)

            def gate_products(s, c):
                for h in range(2):
                    ps, f = claim(("gate", c, h), s)
                    col = 2 * KD + VD + 384 * h
                    for hb in range(HB):
                        ins = split_product(ps[:, 0:384], P.w_hi[:, hb, col:col + 384], P.w_lo[:, hb, col:col + 384],
                                            x_hi[:, hb, CH * c:CH * c + CH], x_lo[:, hb, CH * c:CH * c + CH], True,
                                            hb == 0, hb == HB - 1)
                    ins.then_inc(f, 1)

            def block_products(s, n):
                ps, f = claim(("blk", n), s)
                for hb in range(HB):
                    ins = split_product(ps[:], P.w_hi[:, hb, 128 * n:128 * n + 128], P.w_lo[:, hb, 128 * n:128 * n + 128],
                                        x_hi[:, hb, :], x_lo[:, hb, :], False, hb == 0, hb == HB - 1)
                ins.then_inc(f, 1)

            def token_sums(s):
                ps, f = claim(("sums",), s)
                pe.wait_ge(g_ready, s.val(1, 1))
                gv = g[:].rearrange("p c h -> p (c h)")
                for i, mask in enumerate((P.upto, P.after, P.ones)):
                    nc.tensor.matmul(ps[:, NCHH * i:NCHH * (i + 1)], mask[:], gv, start=True, stop=True)
                for n in range(NQK):
                    pe.wait_ge(sq_ready, s.val(NQK, n + 1))
                    for c in range(NCH):
                        col = 3 * NCHH + 2 * NQK * c + 2 * n
                        ins = nc.tensor.matmul(ps[:, col:col + 2], sq[:, n, CH * c:CH * c + CH], P.pair[:], start=True, stop=True)
                ins.then_inc(f, 1)

            def k_transposes(s, c):
                ps, f = claim(("ktr", c), s)
                pe.wait_ge(silu_done, s.val(NBLK, NQK))
                for b in range(NPAIR):
                    ins = nc.tensor.transpose(ps[:, 128 * b:128 * b + 128], kq[:, b, 0, CH * c:CH * c + CH], P.ident[:])
                ins.then_inc(f, 1)

            def chunk_scores(s, c):
                pe.wait_ge(gm_ready, s.val(NCH, c + 1))
                for hf in range(2):
                    ps, f = claim(("D", c, hf), s)
                    nc.tensor.matmul(ps[:, 0:HALF], P.after[:], gm[:, hf:NH:2, :], start=True, stop=True).then_inc(f, 1)
                for p, heads in enumerate(KQ_HEADS):
                    ps, f = claim(("KQ", c, p), s)
                    for k, h in enumerate(heads):
                        rows = slice(DK * (h % 2), DK * (h % 2) + DK)
                        ins = nc.tensor.matmul(ps[:, 256 * k:256 * k + 256], kq[rows, h // 2, 0, CH * c:CH * c + CH],
                                               kq[rows, h // 2, :, CH * c:CH * c + CH], start=True, stop=True)
                    ins.then_inc(f, 1)

            def v_transposes(s, n):
                ps, f = claim(("vtr", n), s)
                pe.wait_ge(silu_done, s.val(NBLK, NQK + n + 1))
                for c in range(NCH):
                    ins = nc.tensor.transpose(ps[:, 128 * c:128 * c + 128], vT[:, n % 3, CH * c:CH * c + CH], P.ident[:])
                ins.then_inc(f, 1)

            def solve(s):
                pe.wait_ge(tw_in, s.val(128, 128))
                for k in range(NCH + 3):
                    if k < NCH:
                        for hf in range(2):
                            ps, f = claim(("X", k, hf), s)
                            for h in range(3):
                                i = ch(k, 2 * h + hf)
                                ins = nc.tensor.matmul(ps[:, 128 * h:128 * h + 128], BA[:, 0, i, :], Tbd[:, i, :], start=True, stop=True)
                            ins.then_inc(f, 1)
                    c = k - 1
                    if 0 <= c < NCH:
                        ps, f = claim(("Y", c), s)
                        for hf in range(2):
                            ready(pe, ("X", c, hf), s)
                        for h in range(NH):
                            ins = nc.tensor.matmul(ps[0:64, 64 * h:64 * h + 64], W[:, ch(c, h), 0:64],
                                                   eg[:, c % 2, h, 0:64], start=True, stop=True)
                        ins.then_inc(f, 1)
                        for hf in range(2):
                            ps, f = claim(("Z", c, hf), s)
                            for h in range(3):
                                i = 2 * h + hf
                                ins = nc.tensor.matmul(ps[:, 128 * h:128 * h + 128], eg[:, c % 2, i, :], W[:, ch(c, i), :], start=True, stop=True)
                            ins.then_inc(f, 1)
                    c = k - 2
                    if 0 <= c < NCH:
                        ps, f = claim(("X2", c), s)
                        ready(pe, ("Y", c), s)
                        for h in range(NH):
                            ins = nc.tensor.matmul(ps[:, 64 * h:64 * h + 64], BA[0:64, 0, ch(c, h), :],
                                                   T1[:, c % 2, h, :], start=True, stop=True)
                        ins.then_inc(f, 1)
                    c = k - 3
                    if 0 <= c < NCH:
                        ps, f = claim(("Z2", c), s)
                        ready(pe, ("X2", c), s)
                        for hf in range(2):
                            ready(pe, ("Z", c, hf), s)
                        for h in range(NH):
                            ins = nc.tensor.matmul(ps[0:64, 64 * h:64 * h + 64], X2s[:, c % 2, h, :],
                                                   W[:, ch(c, h), 64:128], start=True, stop=True)
                        ins.then_inc(f, 1)

            def recur(s, c):
                rows = [slice(DK * (h % 2), DK * (h % 2) + DK) for h in range(NH)]
                tok = slice(CH * c, CH * c + CH)
                if c >= 1:
                    ready(pe, ("dS", c - 1), s)
                for name, which in (("KS", 0), ("QS", 1)):
                    for hf in range(2):
                        ps, f = claim((name, c, hf), s)
                        for h in range(hf, NH, 2):
                            ins = nc.tensor.matmul(ps[:, 128 * (h // 2):128 * (h // 2) + 128], kq[rows[h], h // 2, which, tok],
                                                   P.S[rows[h], h // 2, :], start=True, stop=True)
                        ins.then_inc(f, 1)
                ready(pe, ("Z2", c), s)
                for hf in range(2):
                    ps, f = claim(("U", c, hf), s)
                    ready(pe, ("KS", c, hf), s)
                    for h in range(hf, NH, 2):
                        ins = nc.tensor.matmul(ps[:, 128 * (h // 2):128 * (h // 2) + 128], W[:, ch(c, h), :], Rr[:, h, :], start=True, stop=True)
                    ins.then_inc(f, 1)

            def recur_out(s, c):
                ps, f = claim(("dS", c), s)
                for hf in range(2):
                    ready(pe, ("U", c, hf), s)
                for h in range(NH):
                    r = DK * (h % 2)
                    ins = nc.tensor.matmul(ps[r:r + DK, 128 * (h // 2):128 * (h // 2) + 128], ktok[:, c, DK * h:DK * h + DK],
                                           U[:, h, :], start=True, stop=True)
                ins.then_inc(f, 1)
                for hf in range(2):
                    ps, f = claim(("AU", c, hf), s)
                    for h in range(hf, NH, 2):
                        ins = nc.tensor.matmul(ps[:, 128 * (h // 2):128 * (h // 2) + 128], BA[:, 1, ch(c, h), :], U[:, h, :], start=True, stop=True)
                    ins.then_inc(f, 1)

            def project_out(s, c):
                pe.wait_ge(og_ready, s.val(NCH, c + 1))
                for hf in range(2):
                    ps, f = claim(("OT", c, hf), s)
                    for h in range(3):
                        ins = nc.tensor.transpose(ps[:, 128 * h:128 * h + 128], O[:, c % 2, 2 * h + hf, :], P.ident[:])
                    ins.then_inc(f, 1)
                ps, f = claim(("WO", c), s)
                for hf in range(2):
                    ready(pe, ("OT", c, hf), s)
                for h in range(NH):
                    ins = split_product(ps[:], P.wo_hi[:, h, :], P.wo_lo[:, h, :], og_hi[:, h, :], og_lo[:, h, :], True,
                                        h == 0, h == NH - 1)
                ins.then_inc(f, 1)

            def local(s):
                for n in range(NQK):
                    block_products(s, n)
                token_sums(s)
                for c in range(NCH):
                    k_transposes(s, c)
                for c in range(NCH):
                    chunk_scores(s, c)
                for n in range(NV):
                    block_products(s, NQK + n)
                for n in range(NV):
                    v_transposes(s, n)
                solve(s)

            s0 = At(None, 0)
            ln_transposes(s0)
            decay_products(s0)
            for c in range(NCH):
                gate_products(s0, c)
            local(s0)
            with pe.Fori(0, nst - 1) as r:
                s, b = At(r, 1), At(r, 0)
                recur(b, 0)
                ln_transposes(s)
                decay_products(s)
                recur_out(b, 0)
                for c in range(1, NCH):
                    recur(b, c)
                    gate_products(s, c - 1)
                    recur_out(b, c)
                    project_out(b, c - 1)
                gate_products(s, NCH - 1)
                project_out(b, NCH - 1)
                local(s)
            b = At(None, nst - 1)
            for c in range(NCH):
                recur(b, c)
                recur_out(b, c)
                if c:
                    project_out(b, c - 1)
            project_out(b, NCH - 1)

        @block.vector
        def _(dve):
            steps = Steps(DVE_STEPS)
            t32 = Steps(T32_STEPS)
            v = nc.vector

            def layer_norm(s):
                dve.wait_ge(x_in, s.val(16, 16))
                for t in range(NCH):
                    v.bn_stats(stats[:, t, :], xb[:, t, :]).then_inc(ln_step, 1)
                dve.wait_ge(ln_step, s.val(LN_STEPS, NCH))

                def link_ln(ins, n):
                    ins.then_inc(ln_step, 1)
                    dve.wait_ge(ln_step, s.val(LN_STEPS, NCH + n))
                link_ln(v.tensor_tensor(mv[:, :, 0], stats[:, :, 1], stats[:, :, 4], ALU.add), 1)
                link_ln(v.tensor_tensor(ln_d[:], stats[:, :, 1], stats[:, :, 4], ALU.subtract), 2)
                link_ln(v.tensor_tensor(mv[:, :, 1], stats[:, :, 2], stats[:, :, 5], ALU.add), 3)
                link_ln(v.tensor_scalar(mv[:, :, 0], mv[:, :, 0], 0.5, None, ALU.mult), 4)
                link_ln(v.tensor_tensor(ln_d[:], ln_d[:], ln_d[:], ALU.mult), 5)
                link_ln(v.tensor_scalar(mv[:, :, 1], mv[:, :, 1], 1.0 / D, EPS, ALU.mult, ALU.add), 6)
                v.scalar_tensor_tensor(out=mv[:, :, 1], in0=ln_d[:], scalar=0.25, in1=mv[:, :, 1],
                                       op0=ALU.mult, op1=ALU.add).then_inc(ln_stats, 1)
                dve.wait_ge(ln_rstd, s.val(1, 1))
                for t in range(NCH):
                    v.tensor_scalar(xb[:, t, :], xb[:, t, :], mv[:, t, 0:1], rstd[:, t:t + 1],
                                    ALU.subtract, ALU.mult).then_inc(xn_ready, 1)

            def xn_parts(s):
                for t in range(NCH):
                    ps, d = out_of(("ln", t))
                    dve.wait_ge(xhi_ready, s.val(NCH, t + 1))
                    cols = slice(CH * t, CH * t + CH)
                    v.tensor_tensor(x_lo[:, :, cols], ps[:].rearrange("p (b c) -> p b c", b=HB), x_hi[:, :, cols],
                                    ALU.subtract).then_inc(d, 1)

            def link(ins):
                n = steps.next()
                ins.then_inc(dve_step, 1)
                dve.wait_ge(dve_step, n)

            def decays(s):
                filled(dve, ("ab",), s)
                ps, d = out_of(("ab",))
                v.tensor_copy(ab[:].rearrange("p c n -> p (c n)"), ps[:, 0:2 * NCHH]).then_inc(d, 1)
                ready(dve, ("ab",), s)
                link(v.scalar_tensor_tensor(out=z[:], in0=ab[:, :, 0:NH], scalar=1.0 / W_SCALE,
                                            in1=P.dtb[:].unsqueeze(1).broadcast_to([128, NCH, NH]), op0=ALU.mult, op1=ALU.add))
                link(v.tensor_scalar(nb[:], ab[:, :, NH:2 * NH], -1.0 / W_SCALE, None, ALU.mult))
                v.scalar_tensor_tensor(out=az[:], in0=z[:], scalar=-1.0, in1=z[:], op0=ALU.mult, op1=ALU.max).then_inc(ab_ready, 1)
                dve.wait_ge(ab_exp, s.val(2, 2))
                link(v.tensor_scalar(eb[:], eb[:], 1.0, None, ALU.add))
                link(v.reciprocal(beta[:], eb[:]))
                dve.wait_ge(ab_ln, s.val(1, 1))
                link(v.scalar_tensor_tensor(out=z[:], in0=z[:], scalar=0.0, in1=ln1[:], op0=ALU.max, op1=ALU.add))
                v.tensor_tensor(g[:], z[:], P.nega[:].unsqueeze(1).broadcast_to([128, NCH, NH]), ALU.mult).then_inc(g_ready, 1)

            def convolve(s, blocks):
                for i in range(TAPS):
                    for n in blocks:
                        if i == 0:
                            dve.wait_ge(raw_ready, s.val(NBLK, n + 1))
                            if not (s.first() and n < 2):
                                dve.wait_ge(silu_done, s.val(NBLK, n - 1))
                        src = raw[:, n % 3, i:i + ST]
                        out = cv[:, n % 2, :]
                        w = P.taps[:, n, i:i + 1]
                        if i == 0:
                            ins = v.tensor_scalar(out, src, w, None, ALU.mult)
                        else:
                            dve.wait_ge(dve_step, last[n])
                            ins = v.scalar_tensor_tensor(out=out, in0=src, scalar=w, in1=out, op0=ALU.mult, op1=ALU.add)
                        if i < TAPS - 1:
                            last[n] = steps.next()
                            ins.then_inc(dve_step, 1)
                        else:
                            ins.then_inc(cv_ready, 1)

            last = {}

            def token_scales(s):
                filled(dve, ("sums",), s)
                ps, d = out_of(("sums",))
                v.tensor_copy(sums[:], ps[:, 0:5 * NCHH]).then_inc(d, 1)
                ready(dve, ("sums",), s)
                sq_v = sums[:, 3 * NCHH:5 * NCHH].rearrange("p (c k h) -> p c k h", c=NCH, k=2)

                def by_chunk(t):
                    return t[:].rearrange("p (c h) -> p c h", c=NCH)
                v.tensor_scalar(by_chunk(eq), sq_v[:, :, 1, :], DK * EPS / W_SCALE ** 2, None, ALU.mult).then_inc(ssq_ready, 1)
                link(v.reciprocal(by_chunk(rk2), sq_v[:, :, 0, :]))
                link(v.tensor_tensor(cj[:], rk2[:], beta[:].rearrange("p c h -> p (c h)"), ALU.mult))
                dve.wait_ge(dec_ready, s.val(4, 4))
                v.tensor_scalar(ngam[:], gam[:], -1.0, None, ALU.mult).then_inc(ks_ready, 1)
                v.tensor_tensor(ks[:], cj[:], suf[:], ALU.mult).then_inc(ks_ready, 1)
                dve.wait_ge(ks_ready, s.val(2, 2))

            def k_tokens(s, c):
                filled(dve, ("ktr", c), s)
                ps, d = out_of(("ktr", c))
                v.tensor_tensor(ktok[:, c, :].rearrange("p (h k) -> p h k", h=NH), ps[:, 0:KD].rearrange("p (h k) -> p h k", h=NH),
                                ks[:, NH * c:NH * c + NH].unsqueeze(2).broadcast_to([128, NH, DK]), ALU.mult).then_inc(d, 1)

            def scores(s, c):
                dve.wait_ge(e_ready, s.val(NCH, c + 1))
                for p, heads in enumerate(KQ_HEADS):
                    u = ("KQ", c, p)
                    filled(dve, u, s)
                    ps, d = out_of(u)
                    for k, h in enumerate(heads):
                        ins = v.scalar_tensor_tensor(out=BA[:, :, ch(c, h), :],
                                                     in0=ps[:, 256 * k:256 * k + 256].rearrange("p (k c) -> p k c", k=2),
                                                     scalar=cj[:, ch(c, h):ch(c, h) + 1],
                                                     in1=E[:, h, :].unsqueeze(1).broadcast_to([128, 2, CH]),
                                                     op0=ALU.mult, op1=ALU.mult)
                    ins.then_inc(d, 1)

            def invert_blocks(s):
                t32.start(s)

                def chain(ins):
                    n = t32.next()
                    ins.then_inc(t32_step, 1)
                    dve.wait_ge(t32_step, n)

                if not s.first():
                    dve.wait_ge(t_out, s.val(16, 0))
                    dve.wait_ge(tt_out, s.val(16, 0))
                chain(v.memset(tin[:], 0.0))
                chain(v.memset(tin[:, 0:SUB * SUB:SUB + 1], 1.0))
                dve.wait_ge(b_in, s.val(16, 16))
                tv = tin[:].rearrange("p (i c) -> p i c", i=SUB)
                for j in range(SUB - 1):
                    n, m = SUB - 1 - j, j + 1
                    prod = tmp[:, 0:n * m].rearrange("p (i c) -> p i c", i=n)
                    chain(v.tensor_tensor(prod, bin_[:, SUB * j + j + 1:SUB * j + SUB].unsqueeze(2).broadcast_to([NINST, n, m]),
                                          tv[:, j, 0:m].unsqueeze(1).broadcast_to([NINST, n, m]), ALU.mult))
                    chain(v.tensor_tensor(tv[:, j + 1:SUB, 0:m], tv[:, j + 1:SUB, 0:m], prod, ALU.subtract))
                chain(v.tensor_copy(bin_[:].rearrange("p (c i) -> p c i", c=SUB), tin[:].rearrange("p (i c) -> p c i", i=SUB)))

            def v_tokens(s, n):
                filled(dve, ("vtr", n), s)
                ps, d = out_of(("vtr", n))
                if n == 0:
                    dve.wait_ge(nk_ready, s.val(1, 1))
                nkv = nk[:].rearrange("p (c h) -> p c h", c=NCH)[:, :, n:n + 1].broadcast_to([128, NCH, DV])
                v.tensor_tensor(V[:, :, n, :], ps[:].rearrange("p (c d) -> p c d", c=NCH), nkv, ALU.mult).then_inc(d, 1)

            def heads3(ps):
                return ps[:, 0:HALF].rearrange("p (h d) -> p h d", h=3)

            def heads64(ps, lo_):
                return ps[lo_:lo_ + 64, 0:64 * NH].rearrange("p (h d) -> p h d", h=NH)

            def solve(s):
                for k in range(NCH + 3):
                    if k < NCH:
                        for hf in range(2):
                            filled(dve, ("X", k, hf), s)
                            ps, d = out_of(("X", k, hf))
                            v.tensor_tensor(eg[:, k % 2, hf:NH:2, :], heads3(ps),
                                            P.level32[:].unsqueeze(1).broadcast_to([128, 3, CH]), ALU.mult).then_inc(d, 1)
                    c = k - 1
                    if 0 <= c < NCH:
                        filled(dve, ("Y", c), s)
                        ps, d = out_of(("Y", c))
                        v.tensor_tensor(T1[:, c % 2, :, :], Tbd[0:64, NH * c:NH * c + NH, 0:64], heads64(ps, 0),
                                        ALU.subtract).then_inc(d, 1)
                        for hf in range(2):
                            filled(dve, ("Z", c, hf), s)
                            ps, d = out_of(("Z", c, hf))
                            ws = W[:, NH * c + hf:NH * c + NH:2, :]
                            v.tensor_tensor(ws, ws, heads3(ps), ALU.subtract).then_inc(d, 1)
                    c = k - 3
                    if 0 <= c < NCH:
                        filled(dve, ("Z2", c), s)
                        ps, d = out_of(("Z2", c))
                        for hf in range(2):
                            ready(dve, ("Z", c, hf), s)
                        w = W[0:64, NH * c:NH * c + NH, 64:128]
                        v.tensor_tensor(w, w, heads64(ps, 0), ALU.subtract).then_inc(d, 1)

            def right_sides(s, c):
                for hf in range(2):
                    u = ("KS", c, hf)
                    filled(dve, u, s)
                    ps, d = out_of(u)
                    for h in range(hf, NH, 2):
                        ins = v.scalar_tensor_tensor(out=Rr[:, h, :], in0=ps[:, 128 * (h // 2):128 * (h // 2) + 128],
                                                     scalar=ngam[:, ch(c, h):ch(c, h) + 1], in1=V[:, c, h, :],
                                                     op0=ALU.mult, op1=ALU.add)
                    ins.then_inc(d, 1)

            def state(s, c):
                u = ("dS", c)
                filled(dve, u, s)
                ps, d = out_of(u)
                for b in range(NPAIR):
                    ins = v.scalar_tensor_tensor(out=P.S[:, b, :], in0=P.S[:, b, :], scalar=gC[:, c, b:b + 1],
                                                 in1=ps[:, 128 * b:128 * b + 128], op0=ALU.mult, op1=ALU.add)
                ins.then_inc(d, 1)

            def outputs(s, c):
                for hf in range(2):
                    ready(dve, ("QS", c, hf), s)
                    u = ("AU", c, hf)
                    filled(dve, u, s)
                    ps, d = out_of(u)
                    o = O[:, c % 2, hf:NH:2, :]
                    v.tensor_tensor(o, heads3(ps), o, ALU.add).then_inc(d, 1)

            def mean_squares(s, c):
                dve.wait_ge(ss_ready, s.val(NCH, c + 1))
                v.scalar_tensor_tensor(out=t6[:, c % 2, :], in0=ss[:, c % 2, :], scalar=1.0 / (DV * W_SCALE ** 2),
                                       in1=eq[:, NH * c:NH * c + NH], op0=ALU.mult, op1=ALU.add).then_inc(t6_ready, 1)

            def gated(s, c):
                dve.wait_ge(rn_ready, s.val(NCH, c + 1))
                for h in range(NH):
                    o = O[:, c % 2, h, :]
                    ins = v.scalar_tensor_tensor(out=o, in0=o, scalar=rn[:, c % 2, h:h + 1],
                                                 in1=gate[:, c, DV * h:DV * h + DV], op0=ALU.mult, op1=ALU.mult)
                ins.then_inc(og_ready, 1)

            def og_part(s, c):
                for hf in range(2):
                    dve.wait_ge(oghi_ready, s.val(2 * NCH, 2 * c + hf + 1))
                    ps, d = out_of(("OT", c, hf))
                    hs = slice(hf, NH, 2)
                    v.tensor_tensor(og_lo[:, hs, :], heads3(ps), og_hi[:, hs, :], ALU.subtract).then_inc(d, 1)

            def residual(s, c):
                u = ("WO", c)
                filled(dve, u, s)
                ps, d = out_of(u)
                dve.wait_ge(xr_in[c % 2], s.val(16 * NCH // 2, 16 * (c // 2 + 1)))
                v.scalar_tensor_tensor(out=xr[:, c % 2, :], in0=ps[:], scalar=W_SCALE ** -2, in1=xr[:, c % 2, :],
                                       op0=ALU.mult, op1=ALU.add).then_inc(d, 1)

            def local(s):
                for n in range(0, NQK, 2):
                    convolve(s, (n, n + 1))
                token_scales(s)
                for c in range(NCH):
                    k_tokens(s, c)
                for c in range(NCH):
                    scores(s, c)
                convolve(s, (NQK, NQK + 1))
                invert_blocks(s)
                for n in range(NQK + 2, NBLK, 2):
                    convolve(s, (n, n + 1))
                for n in range(NV):
                    v_tokens(s, n)
                solve(s)

            def finish(b, c):
                og_part(b, c)
                residual(b, c)

            s0 = At(None, 0)
            steps.start(s0)
            layer_norm(s0)
            xn_parts(s0)
            decays(s0)
            local(s0)
            with dve.Fori(0, nst - 1) as r:
                s, b = At(r, 1), At(r, 0)
                steps.start(s)
                layer_norm(s)
                right_sides(b, 0)
                xn_parts(s)
                decays(s)
                state(b, 0)
                outputs(b, 0)
                for c in range(1, NCH):
                    right_sides(b, c)
                    mean_squares(b, c - 1)
                    gated(b, c - 1)
                    state(b, c)
                    outputs(b, c)
                    finish(b, c - 1)
                mean_squares(b, NCH - 1)
                gated(b, NCH - 1)
                finish(b, NCH - 1)
                local(s)
            b = At(None, nst - 1)
            for c in range(NCH):
                right_sides(b, c)
                if c:
                    mean_squares(b, c - 1)
                    gated(b, c - 1)
                state(b, c)
                outputs(b, c)
                if c:
                    finish(b, c - 1)
            mean_squares(b, NCH - 1)
            gated(b, NCH - 1)
            finish(b, NCH - 1)

        @block.scalar
        def _(act):
            sc = nc.scalar

            def xn_high(s):
                if not s.first():
                    act.wait_ge(spilled, s.val(32, 0))
                for t in range(NCH):
                    filled(act, ("ln", t), s)
                    ps, _ = out_of(("ln", t))
                    sc.activation(x_hi[:, :, CH * t:CH * t + CH], ps[:].rearrange("p (b c) -> p b c", b=HB),
                                  ACT.Copy).then_inc(xhi_ready, 1)

            def decays(s):
                act.wait_ge(ab_ready, s.val(1, 1))
                sc.activation(e1[:], az[:], ACT.Exp, scale=-1.0).then_inc(ab_exp, 1)
                sc.activation(eb[:], nb[:], ACT.Exp).then_inc(ab_exp, 1)
                act.wait_ge(ab_exp, s.val(2, 1))
                sc.activation(ln1[:], e1[:], ACT.Ln, bias=P.ones[:, 0:1]).then_inc(ab_ln, 1)

            def gates(s, c, b):
                if b is not None:
                    act.wait_ge(og_ready, b.val(NCH, c + 1))
                for h in range(2):
                    u = ("gate", c, h)
                    filled(act, u, s)
                    ps, d = out_of(u)
                    sc.activation(gate[:, c, 384 * h:384 * h + 384], ps[:, 0:384], ACT.Silu, scale=1.0 / W_SCALE).then_inc(d, 1)

            def raw_out(s, n):
                u = ("blk", n)
                filled(act, u, s)
                ps, d = out_of(u)
                if not (s.first() and n < 3):
                    act.wait_ge(cv_ready, s.val(NBLK, n - 2))
                    act.wait_ge(raw_ready, s.val(NBLK, n - 2))
                sc.activation(raw[:, n % 3, TAPS - 1:], ps[:], ACT.Copy, scale=1.0 / W_SCALE).then_inc(d, 1)

            def silu(s, n):
                act.wait_ge(cv_ready, s.val(NBLK, n + 1))
                if n < NQK:
                    dst = kq[:, n % NPAIR, n // NPAIR, :]
                else:
                    dst = vT[:, n % 3, :]
                    if n - NQK >= 3:
                        filled(act, ("vtr", n - NQK - 3), s)
                sc.activation(dst, cv[:, n % 2, :], ACT.Silu).then_inc(silu_done, 1)

            def decay_exps(s):
                ready(act, ("sums",), s)
                tot = sums[:, 2 * NCHH:3 * NCHH].rearrange("p (c b r) -> p c b r", c=NCH, r=2)
                sc.activation(gam[:], sums[:, 0:NCHH], ACT.Exp).then_inc(dec_ready, 1)
                sc.activation(suf[:], sums[:, NCHH:2 * NCHH], ACT.Exp).then_inc(dec_ready, 1)
                for r in range(2):
                    rows = slice(DK * r, DK * r + DK)
                    sc.activation(gC[rows, :, :], tot[rows, :, :, r], ACT.Exp).then_inc(dec_ready, 1)

            def pair_exps(s, c):
                if c:
                    for p in range(len(KQ_HEADS)):
                        ready(act, ("KQ", c - 1, p), s)
                for hf in range(2):
                    u = ("D", c, hf)
                    filled(act, u, s)
                    ps, d = out_of(u)
                    sc.activation(E[:, hf:NH:2, :], ps[:, 0:HALF].rearrange("p (h c) -> p h c", h=3), ACT.Exp).then_inc(d, 1)

            def local(s):
                for n in range(NQK + 2):
                    if n < NQK:
                        raw_out(s, n)
                    if n >= 2:
                        silu(s, n - 2)
                decay_exps(s)
                for c in range(NCH):
                    pair_exps(s, c)
                for n in range(NQK, NBLK + 2):
                    if n < NBLK:
                        raw_out(s, n)
                    if n >= NQK + 2:
                        silu(s, n - 2)
                for c in range(NCH):
                    u = ("X2", c)
                    filled(act, u, s)
                    ps, d = out_of(u)
                    sc.activation(X2s[:, c % 2, :, :], ps[:, 0:64 * NH].rearrange("p (h c) -> p h c", h=NH), ACT.Copy).then_inc(d, 1)

            def q_state(s, c):
                for hf in range(2):
                    u = ("QS", c, hf)
                    filled(act, u, s)
                    ps, d = out_of(u)
                    for h in range(hf, NH, 2):
                        ins = sc.activation(O[:, c % 2, h, :], ps[:, 128 * (h // 2):128 * (h // 2) + 128], ACT.Copy,
                                            scale=gam[:, ch(c, h):ch(c, h) + 1])
                    ins.then_inc(d, 1)

            def updates(s, c):
                for hf in range(2):
                    u = ("U", c, hf)
                    filled(act, u, s)
                    ps, d = out_of(u)
                    sc.activation(U[:, hf:NH:2, :], ps[:, 0:HALF].rearrange("p (h d) -> p h d", h=3), ACT.Copy).then_inc(d, 1)

            def squares(s, c):
                if c:
                    act.wait_ge(ss_ready, s.val(NCH, c))
                for h in range(NH):
                    if h < 2:
                        ready(act, ("AU", c, h), s)
                    ins = sc.activation(junk[:, h, :], O[:, c % 2, h, :], ACT.Square, accum_out=ss[:, c % 2, h:h + 1])
                ins.then_inc(ss_ready, 1)

            def og_high(s, c):
                for hf in range(2):
                    u = ("OT", c, hf)
                    filled(act, u, s)
                    ps, _ = out_of(u)
                    sc.activation(og_hi[:, hf:NH:2, :], ps[:, 0:HALF].rearrange("p (h c) -> p h c", h=3),
                                  ACT.Copy).then_inc(oghi_ready, 1)

            s0 = At(None, 0)
            xn_high(s0)
            decays(s0)
            for c in range(NCH):
                gates(s0, c, None)
            local(s0)
            with act.Fori(0, nst - 1) as r:
                s, b = At(r, 1), At(r, 0)
                q_state(b, 0)
                updates(b, 0)
                xn_high(s)
                decays(s)
                squares(b, 0)
                for c in range(1, NCH):
                    q_state(b, c)
                    updates(b, c)
                    gates(s, c - 1, b)
                    squares(b, c)
                    og_high(b, c - 1)
                gates(s, NCH - 1, b)
                act.wait_ge(ss_ready, b.val(NCH, NCH))
                og_high(b, NCH - 1)
                local(s)
            b = At(None, nst - 1)
            for c in range(NCH):
                q_state(b, c)
                updates(b, c)
                squares(b, c)
                if c:
                    og_high(b, c - 1)
            og_high(b, NCH - 1)

        @block.gpsimd
        def _(pool):
            g_ = nc.gpsimd

            def ln_scale(s):
                pool.wait_ge(ln_stats, s.val(1, 1))
                g_.tensor_tensor(out=rstd[:], in0=mv[:, :, 1], in1=P.mhalf[:, 0:NCH], op=ALU.pow).then_inc(ln_rstd, 1)

            def spill(s):
                for t in (NCH - 2, NCH - 1):
                    ready(pool, ("ln", t), s)
                pool.dma_start(scr.xh[s.idx()], x_hi[:].rearrange("p b c -> p (b c)")).then_inc(spilled, 16)
                pool.dma_start(scr.xl[s.idx()], x_lo[:].rearrange("p b c -> p (b c)")).then_inc(spilled, 16)

            def norm_scale(s, c):
                pool.wait_ge(t6_ready, s.val(NCH, c + 1))
                g_.tensor_tensor(out=rn[:, c % 2, :], in0=t6[:, c % 2, :], in1=P.mhalf[:, 0:NH], op=ALU.pow).then_inc(rn_ready, 1)

            def halo(s, n):
                ready(pool, ("blk", n), s)
                g_.tensor_tensor(out=raw[:, n % 3, 0:TAPS - 1], in0=P.halo[:, n, :], in1=P.zeros[:], op=ALU.add).then_inc(halo_used, 1)
                pool.wait_ge(halo_used, s.val(NBLK, n + 1))
                g_.tensor_tensor(out=P.halo[:, n, :], in0=raw[:, n % 3, ST:ST + TAPS - 1], in1=P.zeros[:], op=ALU.add).then_inc(raw_ready, 1)

            def square(s, n):
                pool.wait_ge(silu_done, s.val(NBLK, n + 1))
                src = kq[:, n % NPAIR, n // NPAIR, :]
                g_.tensor_tensor(out=sq[:, n, :], in0=src, in1=src, op=ALU.mult).then_inc(sq_ready, 1)

            def masked_g(s, c):
                if c:
                    filled(pool, ("D", c - 1, 1), s)
                g_.tensor_tensor(out=gm[:], in0=P.upto[:].unsqueeze(1).broadcast_to([128, NH, CH]),
                                 in1=g[:, c, :].unsqueeze(2).broadcast_to([128, NH, CH]), op=ALU.mult).then_inc(gm_ready, 1)

            def mask_decays(s, c):
                for hf in range(2):
                    ready(pool, ("D", c, hf), s)
                g_.tensor_tensor(out=E[:], in0=E[:], in1=P.upto[:].unsqueeze(1).broadcast_to([128, NH, CH]),
                                 op=ALU.mult).then_inc(e_ready, 1)

            def local(s):
                for n in range(NQK):
                    halo(s, n)
                    if n >= 2:
                        square(s, n - 2)
                square(s, NQK - 2)
                square(s, NQK - 1)
                pool.wait_ge(g_ready, s.val(1, 1))
                masked_g(s, 0)
                pool.wait_ge(ssq_ready, s.val(1, 1))
                g_.tensor_tensor(out=nk[:].rearrange("p (c h) -> p c h", c=NCH),
                                 in0=sums[:, 3 * NCHH:5 * NCHH].rearrange("p (c k h) -> p c k h", c=NCH, k=2)[:, :, 0, :],
                                 in1=P.phalf[:, 0:NCHH].rearrange("p (c h) -> p c h", c=NCH), op=ALU.pow).then_inc(nk_ready, 1)
                for c in range(NCH):
                    if c + 1 < NCH:
                        masked_g(s, c + 1)
                    mask_decays(s, c)
                for n in range(NQK, NBLK):
                    halo(s, n)

            s0 = At(None, 0)
            ln_scale(s0)
            g_.memset(Tbd[:], 0.0)
            g_.memset(W[:], 0.0)
            spill(s0)
            local(s0)
            with pool.Fori(0, nst - 1) as r:
                s, b = At(r, 1), At(r, 0)
                ln_scale(s)
                spill(s)
                for c in range(NCH):
                    norm_scale(b, c)
                g_.memset(W[:], 0.0)
                local(s)
            b = At(None, nst - 1)
            for c in range(NCH):
                norm_scale(b, c)

        @block.sync
        def _(sp):
            def load_x(s, b):
                if b is not None:
                    filled(sp, ("ln", NCH - 1), b)
                sp.dma_start(xb[:], x_v[s.idx()]).then_inc(x_in, 16)

            def load_residual(s, c):
                if not (s.first() and c < 2):
                    sp.wait_ge(y_out[c % 2], s.val(16 * NCH // 2, 16 * (c // 2)))
                sp.dma_start(xr[:, c % 2, :], xr_v[s.idx(), c]).then_inc(xr_in[c % 2], 16)

            def store_y(s, c):
                ready(sp, ("WO", c), s)
                sp.dma_start(y_v[s.idx(), c], xr[:, c % 2, :]).then_inc(y_out[c % 2], 16)

            def store_all(s):
                for c in range(NCH):
                    store_y(s, c)
                    if c + 2 < NCH:
                        load_residual(s, c + 2)

            def exchange(s):
                ready(sp, ("KQ", NCH - 1, len(KQ_HEADS) - 1), s)
                for q in range(NSUB):
                    rows = slice(SUB * q, SUB * q + SUB)
                    sp.dma_start(scr.b[q].rearrange("c j i -> j c i"), BA[rows, 0, :, rows]).then_inc(b_out, 16)
                sp.wait_ge(b_out, s.val(16 * NSUB, 16 * NSUB))
                sp.dma_start(bin_[:], scr.b.rearrange("q c j i -> (q c) (j i)")).then_inc(b_in, 16)
                sp.wait_ge(t32_step, s.val(T32_STEPS, T32_STEPS - 1))
                sp.dma_start(scr.t.rearrange("q c i k -> (q c) (i k)"), tin[:]).then_inc(t_out, 16)
                sp.wait_ge(t32_step, s.val(T32_STEPS, T32_STEPS))
                sp.dma_start(scr.tt.rearrange("q c k i -> (q c) (k i)"), bin_[:]).then_inc(tt_out, 16)
                sp.wait_ge(t_out, s.val(16, 16))
                for q in range(NSUB):
                    rows = slice(SUB * q, SUB * q + SUB)
                    sp.dma_start(Tbd[rows, :, rows], scr.t[q].rearrange("c i k -> i c k")).then_inc(tw_in, 16)
                sp.wait_ge(tt_out, s.val(16, 16))
                for q in range(NSUB):
                    rows = slice(SUB * q, SUB * q + SUB)
                    sp.dma_start(W[rows, :, rows], scr.tt[q].rearrange("c k i -> k c i")).then_inc(tw_in, 16)

            s0 = At(None, 0)
            load_x(s0, None)
            load_residual(s0, 0)
            load_residual(s0, 1)
            exchange(s0)
            with sp.Fori(0, nst - 1) as r:
                s, b = At(r, 1), At(r, 0)
                load_x(s, b)
                store_all(b)
                exchange(s)
                load_residual(s, 0)
                load_residual(s, 1)
            store_all(At(None, nst - 1))
            for i in range(2):
                sp.wait_ge(y_out[i], 16 * NCH // 2 * nst)
            sp.wait_ge(spilled, 32 * nst)


DVE_STEPS = 3 * NBLK + 5 + 2
LN_STEPS = NCH + 6
T32_STEPS = 3 + 2 * (SUB - 1)


def feed(nc, A, scr, nst=NST):
    with ExitStack() as ctx:
        def sb(name, shape, dt=F32):
            return ctx.enter_context(nc.sbuf_tensor(name, shape, dt))

        def sem(name):
            return ctx.enter_context(nc.semaphore(name))

        NM = 3
        GC = NCOL // IB
        gu_hi = sb("gu_hi", [128, 2, HB, INTER], F16)
        gu_lo = sb("gu_lo", [128, 2, HB, INTER], F16)
        d_hi = sb("d_hi", [128, IB, D], F16)
        d_lo = sb("d_lo", [128, IB, D], F16)
        x_hi = sb("fx_hi", [128, HB, ST], F16)
        x_lo = sb("fx_lo", [128, HB, ST], F16)
        it_hi = sb("it_hi", [128, IB, ST], F16)
        it_lo = sb("it_lo", [128, IB, ST], F16)
        sg = sb("sg", [128, 2, ST])
        hh = sb("hh", [128, 2, ST])
        yr = sb("yr", [128, 2, D])
        wt = sb("wt", [128, 2, GC])
        knot = sb("knot", [128, 2, GC])
        rows = sb("rows", [128, 1])
        later = sb("later", [128, 2, GC], U8)
        pow_in = sb("pow_in", [12, 128])
        coef = sb("coef", [12, 2, 2 * NM, GC], F16)
        powers = sb("powers", [12, 128], F16)
        pg = [ctx.enter_context(nc.psum_tensor(f"pg{i}", [128, 512], F32)) for i in range(2)]
        pu = [ctx.enter_context(nc.psum_tensor(f"pu{i}", [128, 512], F32)) for i in range(2)]
        pw = [ctx.enter_context(nc.psum_tensor(f"pw{i}", [128, 512], F32)) for i in range(4)]
        const_in, x_in, y_in, y_out = sem("const_in"), sem("fx_in"), [sem(f"y_in{i}") for i in range(2)], [sem(f"out{i}") for i in range(2)]
        coef_in = [sem(f"coef_in{i}") for i in range(2)]
        poly_made, first_copied, picked, w_hi_made, w_made = (
            sem("poly_made"), sem("first_copied"), sem("picked"), sem("w_hi_made"), sem("w_made"))
        gate_made, up_made, sg_ready, h_ready, hi_ready, it_ready = (
            sem("gate_made"), sem("up_made"), sem("sg_ready"), sem("h_ready"), sem("hi_ready"), sem("it_ready"))
        down_made, down_read = sem("down_made"), sem("down_read")
        later_made, powers_ready = sem("later_made"), sem("powers_ready")
        block = ctx.enter_context(nc.Block())
        y_v = scr.y.rearrange("(s t p) d -> s t p d", t=NCH, p=128)
        o_v = A.out.rearrange("(n p) d -> n p d", p=128)

        def weight_block(part, m, i):
            if m < 2:
                return (gu_hi, gu_lo)[part][:, m, :, 128 * i:128 * i + 128]
            n = GC // IB
            return (d_hi, d_lo)[part][:, :, n * i:n * i + n]

        def by_block(t, m):
            nb = HB if m < 2 else IB
            return t.rearrange("p (o b) -> p b o", b=nb)

        @block.sync
        def _(sp):
            sp.dma_start(pow_in[:], A.powers).then_inc(const_in, 16)
            sp.dma_start(rows[:], A.rows).then_inc(const_in, 16)

            def load_coef(i):
                if i >= 2:
                    sp.wait_ge(poly_made, NM * (i - 1))
                    sp.wait_ge(later_made, i - 1)
                sp.dma_start(knot[:, i % 2, :], A.knot[GC * i:GC * i + GC].partition_broadcast(128)).then_inc(coef_in[i % 2], 16)
                for row, part in ((0, 0), (4, 0), (8, 1)):
                    sp.dma_start(coef[row:row + 4, i % 2, :, :],
                                 scr.coef[part, :, :, :, GC * i:GC * i + GC].rearrange("k m a c -> k (m a) c")
                                 ).then_inc(coef_in[i % 2], 16)

            def load_x(s):
                if not s.first():
                    sp.wait_ge(up_made, s.val(IB, 0))
                sp.dma_start(x_hi[:].rearrange("p b c -> p (b c)"), scr.xh[s.idx()]).then_inc(x_in, 16)
                sp.dma_start(x_lo[:].rearrange("p b c -> p (b c)"), scr.xl[s.idx()]).then_inc(x_in, 16)

            def store(s):
                for t in range(NCH):
                    sp.wait_ge(down_read, s.val(NCH, t + 1))
                    sp.dma_start(o_v[s.val(NCH, t)], yr[:, t % 2, :]).then_inc(y_out[t % 2], 16)

            s0 = At(None, 0)
            load_coef(0)
            load_x(s0)
            for i in range(1, IB):
                load_coef(i)
            store(s0)
            with sp.Fori(0, nst - 1) as r:
                load_x(At(r, 1))
                store(At(r, 1))
            for i in range(2):
                sp.wait_ge(y_out[i], 16 * NCH // 2 * nst)

        @block.gpsimd
        def _(pool):
            def load_y(s, t):
                if not (s.first() and t < 2):
                    pool.wait_ge(y_out[t % 2], s.val(16 * NCH // 2, 16 * (t // 2)))
                pool.dma_start(yr[:, t % 2, :], y_v[s.idx(), t]).then_inc(y_in[t % 2], 16)

            for t in range(NCH):
                load_y(At(None, 0), t)
            with pool.Fori(0, nst - 1) as r:
                for t in range(NCH):
                    load_y(At(r, 1), t)

        @block.tensor
        def _(pe):
            def polynomials(i):
                pe.wait_ge(coef_in[i % 2], 64 * (i // 2 + 1))
                for m in range(NM):
                    q = NM * i + m
                    if q >= 2:
                        pe.wait_ge(picked, q - 1)
                    for a in range(2):
                        ins = nc.tensor.matmul(pw[2 * (q % 2) + a][:], powers[:], coef[:, i % 2, 2 * m + a, :], start=True, stop=True)
                    ins.then_inc(poly_made, 1)

            def gate_up(s, i):
                if not (s.first() and i < 2):
                    pe.wait_ge(sg_ready, s.val(IB, i - 1))
                    pe.wait_ge(h_ready, s.val(IB, i - 1))
                for m, ps, made in ((0, pg[i % 2], gate_made), (1, pu[i % 2], up_made)):
                    for hb in range(HB):
                        w_h, w_l = (t[:, m, hb, 128 * i:128 * i + 128] for t in (gu_hi, gu_lo))
                        nc.tensor.matmul(ps[:], w_h, x_hi[:, hb, :], start=hb == 0, stop=False)
                        nc.tensor.matmul(ps[:], w_h, x_lo[:, hb, :], start=False, stop=False)
                        ins = nc.tensor.matmul(ps[:], w_l, x_hi[:, hb, :], start=False, stop=hb == HB - 1)
                    ins.then_inc(made, 1)

            def down(s, t):
                if not (s.first() and t < 2):
                    pe.wait_ge(down_read, s.val(NCH, t - 1))
                ps, tok = pw[t % 2], slice(CH * t, CH * t + CH)
                for i in range(IB):
                    nc.tensor.matmul(ps[:], it_hi[:, i, tok], d_hi[:, i, :], start=i == 0, stop=False)
                    nc.tensor.matmul(ps[:], it_hi[:, i, tok], d_lo[:, i, :], start=False, stop=False)
                    ins = nc.tensor.matmul(ps[:], it_lo[:, i, tok], d_hi[:, i, :], start=False, stop=i == IB - 1)
                ins.then_inc(down_made, 1)

            s0 = At(None, 0)
            pe.wait_ge(powers_ready, 1)
            polynomials(0)
            pe.wait_ge(x_in, 32)
            for i in range(IB):
                if i + 1 < IB:
                    polynomials(i + 1)
                pe.wait_ge(w_made, NM * i + 2)
                gate_up(s0, i)
            pe.wait_ge(w_made, NM * IB)
            pe.wait_ge(it_ready, IB)
            for t in range(NCH):
                down(s0, t)
            with pe.Fori(0, nst - 1) as r:
                s = At(r, 1)
                pe.wait_ge(x_in, s.val(32, 32))
                for i in range(IB):
                    gate_up(s, i)
                pe.wait_ge(it_ready, s.val(IB, IB))
                for t in range(NCH):
                    down(s, t)

        @block.scalar
        def _(act):
            sc = nc.scalar

            def first_cubic(q):
                act.wait_ge(poly_made, q + 1)
                if q >= 2:
                    act.wait_ge(w_made, q - 1)
                sc.activation(wt[:, q % 2, :], pw[2 * (q % 2)][:], ACT.Copy).then_inc(first_copied, 1)

            def weight_hi(q):
                act.wait_ge(picked, q + 1)
                i, m = q // NM, q % NM
                sc.activation(weight_block(0, m, i), by_block(wt[:, q % 2, :], m), ACT.Copy).then_inc(w_hi_made, 1)

            def gated(s, i):
                act.wait_ge(gate_made, s.val(IB, i + 1))
                if not (s.first() and i < 2):
                    act.wait_ge(h_ready, s.val(IB, i - 1))
                sc.activation(sg[:, i % 2, :], pg[i % 2][:], ACT.Silu, scale=1.0 / W_SCALE).then_inc(sg_ready, 1)

            def inter_hi(s, i):
                act.wait_ge(h_ready, s.val(IB, i + 1))
                sc.activation(it_hi[:, i, :], hh[:, i % 2, :], ACT.Copy).then_inc(hi_ready, 1)

            s0 = At(None, 0)
            for q in range(NM):
                first_cubic(q)
                weight_hi(q)
            for i in range(IB):
                if i + 1 < IB:
                    for q in range(NM * (i + 1), NM * (i + 2)):
                        first_cubic(q)
                        weight_hi(q)
                gated(s0, i)
                inter_hi(s0, i)
            with act.Fori(0, nst - 1) as r:
                s = At(r, 1)
                for i in range(IB):
                    gated(s, i)
                    inter_hi(s, i)

        @block.vector
        def _(dve):
            v = nc.vector

            def pick(q):
                dve.wait_ge(first_copied, q + 1)
                i = q // NM
                if q % NM == 0:
                    dve.wait_ge(coef_in[i % 2], 64 * (i // 2 + 1))
                    if i >= 2:
                        dve.wait_ge(picked, NM * (i - 1))
                    v.tensor_scalar(later[:, i % 2, :], knot[:, i % 2, :], rows[:, 0:1], None, ALU.is_le).then_inc(later_made, 1)
                    dve.wait_ge(later_made, i + 1)
                v.copy_predicated(wt[:, q % 2, :], later[:, i % 2, :], pw[2 * (q % 2) + 1][:]).then_inc(picked, 1)

            def weight_lo(q):
                dve.wait_ge(w_hi_made, q + 1)
                i, m = q // NM, q % NM
                v.tensor_tensor(weight_block(1, m, i), by_block(wt[:, q % 2, :], m), weight_block(0, m, i), ALU.subtract).then_inc(w_made, 1)

            def product(s, i):
                dve.wait_ge(sg_ready, s.val(IB, i + 1))
                dve.wait_ge(up_made, s.val(IB, i + 1))
                if not (s.first() and i < 2):
                    dve.wait_ge(it_ready, s.val(IB, i - 1))
                v.tensor_tensor(hh[:, i % 2, :], sg[:, i % 2, :], pu[i % 2][:], ALU.mult).then_inc(h_ready, 1)

            def inter_lo(s, i):
                dve.wait_ge(hi_ready, s.val(IB, i + 1))
                v.tensor_tensor(it_lo[:, i, :], hh[:, i % 2, :], it_hi[:, i, :], ALU.subtract).then_inc(it_ready, 1)

            def finish(s, t):
                dve.wait_ge(down_made, s.val(NCH, t + 1))
                dve.wait_ge(y_in[t % 2], s.val(16 * NCH // 2, 16 * (t // 2 + 1)))
                v.scalar_tensor_tensor(out=yr[:, t % 2, :], in0=pw[t % 2][:], scalar=W_SCALE ** -2, in1=yr[:, t % 2, :],
                                       op0=ALU.mult, op1=ALU.add).then_inc(down_read, 1)

            s0 = At(None, 0)
            dve.wait_ge(const_in, 32)
            v.tensor_copy(powers[:], pow_in[:]).then_inc(powers_ready, 1)
            for q in range(NM):
                pick(q)
                weight_lo(q)
            for i in range(IB):
                if i + 1 < IB:
                    for q in range(NM * (i + 1), NM * (i + 2)):
                        pick(q)
                        weight_lo(q)
                product(s0, i)
                inter_lo(s0, i)
            for t in range(NCH):
                finish(s0, t)
            with dve.Fori(0, nst - 1) as r:
                s = At(r, 1)
                for i in range(IB):
                    product(s, i)
                    inter_lo(s, i)
                for t in range(NCH):
                    finish(s, t)


class Arrays:

    def __init__(self, aps, out, runs):
        self.x = aps["x"].rearrange("a t d -> (a t) d")
        self.out = out.rearrange("a t d -> (a t) d")
        self.Wq, self.Wk, self.Wv, self.Wg, self.Wo = (aps[n] for n in ("Wq", "Wk", "Wv", "Wg", "Wo"))
        self.Wa, self.Wb, self.A_log, self.dt_bias, self.nw = (aps[n] for n in ("Wa", "Wb", "A_log", "dt_bias", "nw"))
        self.cwq, self.cwk, self.cwv = (aps[n] for n in ("cwq", "cwk", "cwv"))
        self.gate_cp, self.up_cp, self.down_cp = (aps[n] for n in ("gate_cp", "up_cp", "down_cp"))
        self.frac, self.knot, self.rows, self.powers = (aps[n] for n in ("frac", "knot", "rows", "powers"))
        self.runs = runs


class Scratch:

    def __init__(self, dram):
        self.pad, self.ctrl = dram("pad", [3, NCP + 3]), dram("ctrl_cols", [3, 5, NCOL])
        self.coef = dram("coef_rows", [2, 4, 3, 2, NCOL], F16)
        self.y = dram("y_attn", [T_ALL, D])
        self.xh, self.xl = dram("xn_hi", [NST, 128, HB * ST], F16), dram("xn_lo", [NST, 128, HB * ST], F16)
        self.b, self.t, self.tt = (dram(n, [NSUB, NCH * NH, SUB, SUB]) for n in ("b_blocks", "t_blocks", "tt_blocks"))


class Persistent:

    def __init__(self, sb):
        self.w_hi, self.w_lo = sb("w_hi", [128, HB, WCOLS], F16), sb("w_lo", [128, HB, WCOLS], F16)
        self.wo_hi, self.wo_lo = sb("wo_hi", [128, NH, D], F16), sb("wo_lo", [128, NH, D], F16)
        self.wab_hi, self.wab_lo = sb("wab_hi", [128, HB, 2 * NH], F16), sb("wab_lo", [128, HB, 2 * NH], F16)
        self.taps, self.dtb, self.nega = sb("taps", [128, NBLK, TAPS]), sb("dtb", [128, NH]), sb("nega", [128, NH])
        self.ident, self.ones, self.after, self.upto, self.level32 = (
            sb(n, [128, 128]) for n in ("ident", "ones", "after", "upto", "level32"))
        self.pair = sb("pair", [128, 2])
        self.mhalf, self.phalf = sb("mhalf", [128, NCH * NH]), sb("phalf", [128, NCH * NH])
        self.S, self.halo, self.zeros = (
            sb("S", [128, NPAIR, DV]), sb("halo", [128, NBLK, TAPS - 1]), sb("zeros", [128, TAPS - 1]))


def build(nc, A, nst=NST):
    def dram(name, shape, dt=F32):
        return nc.dram_tensor(name, shape, dt, kind="Internal").ap()

    scr = Scratch(dram)
    with ExitStack() as ctx:
        def sb(name, shape, dt=F32):
            return ctx.enter_context(nc.sbuf_tensor(name, shape, dt))

        P = Persistent(sb)
        prepare(nc, A, scr, P)
        attend(nc, A, scr, P, nst)
    feed(nc, A, scr, nst)


_INS = dict(x="L0_attn_hidden_states", Wq="L0_attn_Wq", Wk="L0_attn_Wk", Wv="L0_attn_Wv", Wa="L0_attn_Wa",
            Wb="L0_attn_Wb", Wg="L0_attn_Wg", Wo="L0_attn_Wo", cwq="L0_attn_conv_wq", cwk="L0_attn_conv_wk",
            cwv="L0_attn_conv_wv", A_log="L0_attn_A_log", dt_bias="L0_attn_dt_bias", nw="L0_attn_norm_weight",
            gate_cp="L0_ffn_gate_cp", up_cp="L0_ffn_up_cp", down_cp="L0_ffn_down_cp")


def kernel(**inputs):
    import concourse.bacc as bacc
    from concourse.bass_utils import run_bass_kernel_spmd

    nc = bacc.Bacc("TRN2", target_bir_lowering=False, num_devices=1)
    arrays = {short: np.ascontiguousarray(inputs[name]) for short, name in _INS.items()}
    runs, arrays["frac"], arrays["knot"], arrays["rows"], arrays["powers"] = spline_shapes()
    aps = {n: nc.dram_tensor(f"in_{n}", a.shape, mybir.dt.from_np(a.dtype), kind="ExternalInput").ap()
           for n, a in arrays.items()}
    out = nc.dram_tensor("out", [1, T_ALL, D], F32, kind="ExternalOutput").ap()
    build(nc, Arrays(aps, out, runs))
    r = run_bass_kernel_spmd(nc, [{f"in_{n}": a for n, a in arrays.items()}], core_ids=[0])
    return r.results[0]["out"]
```

```python
import concourse.bass as bass
from concourse import mybir
from contextlib import ExitStack
import numpy as np

F32 = mybir.dt.float32
F16 = mybir.dt.float16
BF16 = mybir.dt.bfloat16
U8 = mybir.dt.uint8
ALU = mybir.AluOpType
ACT = mybir.ActivationFunctionType

T_ALL, D = 2048, 512
HB = D // 128
ST = 512
NST = T_ALL // ST
CH = 128
NCH = ST // CH
NH, DK, DV = 6, 64, 128
NPAIR = NH // 2
KD, VD = NH * DK, NH * DV
TAPS = 4
NQK = 2 * KD // 128
NV = VD // 128
NBLK = NQK + NV
WCOLS = 2 * KD + 2 * VD
EPS = 1e-5
INTER = 2048
IB = INTER // 128
SUB = 32
NSUB = CH // SUB
NINST = NSUB * NCH * NH
W_SCALE = 64.0
NCP = max(16, int(INTER * D / 128.9))
NCOL = INTER * D // 128
NCR = NCOL // 128
HALF = NH // 2 * 128
NSTG = 4
KQ_HEADS = ((0, 2), (1, 3), (4,), (5,))


def spline_shapes():
    n = NCOL * 128
    t = np.linspace(0.0, NCP - 1.0, n, dtype=np.float64)
    i = np.clip(np.floor(t).astype(np.int64), 0, NCP - 2)
    first = i.reshape(NCOL, 128)[:, 0]
    knot = (i.reshape(NCOL, 128) == first[:, None]).sum(axis=1)
    frac = (t.reshape(NCOL, 128)[:, 0] - first).astype(np.float32).reshape(128, NCR)
    step = (NCP - 1.0) / (n - 1)
    powers = np.stack([(np.arange(128) * step) ** k for k in range(4)])
    hi = powers.astype(np.float16)
    lo = (powers - hi).astype(np.float16)
    shift = np.arange(NCOL) - first
    cuts = [0] + [int(c) for c in np.nonzero(np.diff(shift))[0] + 1] + [NCOL]
    runs = [(a, b, int(first[a])) for a, b in zip(cuts[:-1], cuts[1:])]
    rows = np.arange(128, dtype=np.float32).reshape(128, 1)
    return runs, frac, knot.astype(np.float32), rows, np.concatenate([hi, lo, hi]).astype(np.float32)


class At:

    def __init__(self, reg, off):
        self.reg, self.off = reg, off

    def val(self, per, n):
        assert self.first() or self.off * per + n > 0
        return self.off * per + n if self.reg is None else self.reg * per + (self.off * per + n)

    def idx(self):
        return self.off if self.reg is None else self.reg + self.off

    def first(self):
        return self.reg is None and self.off == 0


class Steps:

    def __init__(self, per):
        self.per, self.n = per, 0

    def start(self, at):
        assert self.n in (0, self.per), (self.n, self.per)
        self.at, self.n = at, 0

    def next(self):
        self.n += 1
        return self.at.val(self.per, self.n)


def bank_uses():
    order = []
    ring = [("ln", t) for t in range(NCH)]
    gates = [("gate", c, h) for c in range(NCH) for h in range(2)]
    ring += [("blk", n) for n in range(NQK)] + gates[:2] + [("ktr", c) for c in range(NCH)]
    for n in range(NV):
        ring += [("blk", NQK + n)] + gates[2 + n:3 + n]
    ring += [("vtr", n) for n in range(NV)]
    order += [(i % 2, u) for i, u in enumerate(ring)] + [(2, ("sums",)), (4, ("ab",))]
    for c in range(NCH):
        order += [(2, ("D", c, 0)), (3, ("D", c, 1))] + [(4 + p, ("KQ", c, p)) for p in range(len(KQ_HEADS))]
    order += [(2, ("qsums",))]
    for k in range(NCH + 3):
        if k < NCH:
            order += [(2, ("X", k, 0)), (3, ("X", k, 1))]
        if 0 <= k - 1 < NCH:
            order += [(4, ("Y", k - 1)), (5, ("Z", k - 1, 0)), (6, ("Z", k - 1, 1))]
        if 0 <= k - 2 < NCH:
            order += [(7, ("X2", k - 2))]
        if 0 <= k - 3 < NCH:
            order += [(4, ("Z2", k - 3))]
    for c in range(NCH + 2):
        if c < NCH:
            order += [(2, ("KS", c, 0)), (3, ("KS", c, 1))]
        if 2 <= c <= NCH:
            order += [(7, ("WO", c - 2))]
        if c < NCH:
            order += [(4, ("U", c, 0)), (5, ("U", c, 1)), (6, ("QS", c, 0)), (7, ("QS", c, 1))]
        if 1 <= c <= NCH:
            order += [(5, ("OT", c - 1, 0)), (6, ("OT", c - 1, 1))]
        if c < NCH:
            order += [(4, ("dS", c)), (2, ("AU", c, 0)), (3, ("AU", c, 1))]
    per, table = [0] * 8, {}
    for bank, u in order:
        table[u] = (bank, per[bank])
        per[bank] += 1
    return table, per


class Preparation:

    def __init__(self, nc, A, scr, P, sb, sem, stage, spline, split):
        self.nc, self.A, self.scr, self.P = nc, A, scr, P
        self.stage = stage
        self.ab_stage = sb("ab_stage", [128, HB, 2 * NH])
        self.nw, self.nw_s = sb("nw", [128, 1]), sb("nw_s", [128, 1])
        n, k = 3 * NCR, 0

        def part(width):
            nonlocal k
            k += width
            return spline[:, k - width:k]
        self.ctrl = part(5 * n).rearrange("p (m k r) -> p m k r", m=3, k=5)
        self.co = part(6 * n).rearrange("p (k m a r) -> p k m a r", k=3, m=3, a=2)
        self.t1, self.t2 = (part(2 * n).rearrange("p (m a r) -> p m a r", m=3, a=2) for _ in range(2))
        self.frac = part(2 * NCR).rearrange("p (a r) -> p a r", a=2)
        self.dcf = split[:, 0:8 * n].rearrange("p (k m a r) -> p k m a r", k=4, m=3, a=2)
        self.dsp = split[:, 8 * n:16 * n].bitcast(F16).rearrange("p (h k m a r) -> p h k m a r", h=2, k=4, m=3, a=2)
        self.staged = [sem(f"staged{i}") for i in range(NSTG)]
        self.ab_in, self.small_in, self.hi_done, self.lo_done = sem("ab_in"), sem("small_in"), sem("hi_done"), sem("lo_done")
        self.const_made, self.padded, self.gathered = sem("const_made"), sem("padded"), sem("gathered")
        self.ctrl_in, self.sp_step, self.coef_out = sem("ctrl_in"), sem("sp_step"), sem("coef_out")
        self.nw_ready, self.nega_ready, self.coef_hi, self.coef_lo = (
            sem("nw_ready"), sem("nega_ready"), sem("coef_hi"), sem("coef_lo"))
        self.cleared = sem("cleared")
        self.pieces = [(A.Wk, 0, 0), (A.Wq, 0, KD)]
        self.pieces += [(A.Wg, 384 * i, 2 * KD + VD + 384 * i) for i in range(2)]
        self.pieces += [(A.Wv, 384 * i, 2 * KD + 384 * i) for i in range(2)]

    def parts(self, i):
        P = self.P
        if i < len(self.pieces):
            col = self.pieces[i][2]
            return (self.stage[i % NSTG].rearrange("p (b n) -> p b n", b=HB),
                    P.w_hi[:, :, col:col + 384], P.w_lo[:, :, col:col + 384])
        h0 = 3 * (i - len(self.pieces))
        return (self.stage[i % NSTG].rearrange("p (h n) -> p h n", h=3),
                P.wo_hi[:, h0:h0 + 3, :], P.wo_lo[:, h0:h0 + 3, :])

    @staticmethod
    def count(i):
        return i + 1 if i < 2 else i + 2

    def load_piece(self, eng, i):
        if i >= NSTG:
            eng.wait_ge(self.lo_done, self.count(i - NSTG))
        if i < len(self.pieces):
            w, c0, _ = self.pieces[i]
            src = w.rearrange("(b p) n -> p b n", p=128)[:, :, c0:c0 + 384]
        else:
            h0 = 3 * (i - len(self.pieces))
            src = self.A.Wo.rearrange("(h p) n -> p h n", p=128)[:, h0:h0 + 3, :]
        eng.dma_start(self.parts(i)[0], src).then_inc(self.staged[i % NSTG], 16)

    def load_decay_weights(self, sp):
        sp.dma_start(self.ab_stage[:, :, 0:NH], self.A.Wa.rearrange("(b p) n -> p b n", p=128)).then_inc(self.ab_in, 16)
        sp.dma_start(self.ab_stage[:, :, NH:2 * NH], self.A.Wb.rearrange("(b p) n -> p b n", p=128)).then_inc(self.ab_in, 16)

    def load_small(self, sp):
        A, P, small_in = self.A, self.P, self.small_in
        sp.dma_start(P.dtb[:], A.dt_bias.partition_broadcast(128)).then_inc(small_in, 16)
        sp.dma_start(P.nega[:], A.A_log.partition_broadcast(128)).then_inc(small_in, 16)
        for b in range(NPAIR):
            for which, w in enumerate((A.cwk, A.cwq)):
                sp.dma_start(P.taps[:, NPAIR * which + b, :], w[128 * b:128 * b + 128, :]).then_inc(small_in, 16)
        sp.dma_start(P.taps[:, NQK:NBLK, :], A.cwv.rearrange("(b p) t -> p b t", p=128)).then_inc(small_in, 16)
        sp.dma_start(self.nw[:], A.nw.rearrange("(p a) -> p a", a=1)).then_inc(small_in, 16)
        sp.dma_start(self.frac[:, 0, :], A.frac).then_inc(small_in, 16)

    SMALL = 16 * (2 + 2 * NPAIR + 3)

    def pad_control_points(self, sp):
        A, scr, padded = self.A, self.scr, self.padded
        for m, cp in enumerate((A.gate_cp, A.up_cp, A.down_cp)):
            row = cp.rearrange("(a n) -> a n", a=1)
            sp.dma_start(scr.pad[m:m + 1, 1:1 + NCP], row).then_inc(padded, 16)
            sp.dma_start(scr.pad[m:m + 1, 0:1], row[:, 0:1]).then_inc(padded, 16)
            for e in range(2):
                sp.dma_start(scr.pad[m:m + 1, 1 + NCP + e:2 + NCP + e], row[:, NCP - 1:NCP]).then_inc(padded, 16)

    def gather_control_points(self, sp):
        scr, runs = self.scr, self.A.runs
        sp.wait_ge(self.padded, 12 * 16)
        for c0, c1, j0 in runs:
            src = bass.AP(tensor=scr.pad.tensor, offset=scr.pad.offset + j0,
                          ap=[[NCP + 3, 3], [1, 5], [1, c1 - c0]])
            sp.dma_start(scr.ctrl[:, :, c0:c1], src, allow_slow_non_contiguous=c1 - c0 == 1).then_inc(self.gathered, 16)
        sp.wait_ge(self.gathered, 16 * len(runs))
        for m in range(3):
            sp.dma_start(self.ctrl[:, m, :, :], scr.ctrl[m].rearrange("k (q r) -> q k r", r=NCR)).then_inc(self.ctrl_in, 16)

    def store_coefficients(self, sp):
        sp.wait_ge(self.coef_lo, 1)
        for a in range(2):
            for part in range(2):
                for m in range(3):
                    sp.dma_start(self.scr.coef[part, :, m, a, :].rearrange("k (q r) -> q k r", r=NCR),
                                 self.dsp[:, part, :, m, a, :]).then_inc(self.coef_out, 16)

    def decay_weights_high(self, act):
        act.wait_ge(self.ab_in, 32)
        self.nc.scalar.activation(self.P.wab_hi[:], self.ab_stage[:], ACT.Copy, scale=W_SCALE).then_inc(self.hi_done, 1)

    def piece_high(self, act, i):
        act.wait_ge(self.staged[i % NSTG], 16 * (i // NSTG + 1))
        src, hi, _ = self.parts(i)
        if i == len(self.pieces):
            act.wait_ge(self.small_in, self.SMALL)
            self.nc.scalar.activation(self.nw_s[:], self.nw[:], ACT.Copy, scale=W_SCALE).then_inc(self.nw_ready, 1)
            act.wait_ge(self.nw_ready, 1)
        scale = W_SCALE if i < len(self.pieces) else self.nw_s[:]
        self.nc.scalar.activation(hi, src, ACT.Copy, scale=scale).then_inc(self.hi_done, 1)

    def decay_rates(self, act):
        P = self.P
        act.wait_ge(self.small_in, self.SMALL)
        self.nc.scalar.activation(P.nega[:], P.nega[:], ACT.Exp).then_inc(self.nega_ready, 1)
        act.wait_ge(self.nega_ready, 1)
        self.nc.scalar.activation(P.nega[:], P.nega[:], ACT.Copy, scale=-1.0).then_inc(self.nega_ready, 1)

    def decay_weights_low(self, dve):
        dve.wait_ge(self.hi_done, 3)
        self.nc.vector.scalar_tensor_tensor(out=self.P.wab_lo[:], in0=self.ab_stage[:], scalar=W_SCALE, in1=self.P.wab_hi[:],
                                            op0=ALU.mult, op1=ALU.subtract).then_inc(self.lo_done, 1)

    def piece_low(self, dve, i):
        dve.wait_ge(self.hi_done, self.count(i))
        src, hi, lo = self.parts(i)
        scale = W_SCALE if i < len(self.pieces) else self.nw_s[:]
        self.nc.vector.scalar_tensor_tensor(out=lo, in0=src, scalar=scale, in1=hi,
                                            op0=ALU.mult, op1=ALU.subtract).then_inc(self.lo_done, 1)

    def spline_coefficients(self, dve):
        nc, ctrl, co, t1, t2, dcf, dsp = self.nc, self.ctrl, self.co, self.t1, self.t2, self.dcf, self.dsp
        step = [0]

        def link(ins):
            step[0] += 1
            ins.then_inc(self.sp_step, 1)
            dve.wait_ge(self.sp_step, step[0])

        dve.wait_ge(self.small_in, self.SMALL)
        link(nc.vector.tensor_scalar(self.frac[:, 1, :], self.frac[:, 0, :], -1.0, None, ALU.add))
        dve.wait_ge(self.ctrl_in, 48)
        stt = nc.vector.scalar_tensor_tensor
        p0, p1, p2, p3 = (ctrl[:, :, k:k + 2, :] for k in range(4))
        u = self.frac.unsqueeze(1).broadcast_to([128, 3, 2, NCR])
        c1, c2, c3 = (co[:, k, :, :, :] for k in range(3))
        d0, d1, d2, d3 = (dcf[:, k, :, :, :] for k in range(4))
        link(nc.vector.tensor_tensor(t1, p1, p2, ALU.subtract))
        link(nc.vector.tensor_tensor(t2, p3, p0, ALU.subtract))
        link(nc.vector.tensor_scalar(t2, t2, 0.5, None, ALU.mult))
        link(stt(out=c3, in0=t1, scalar=1.5, in1=t2, op0=ALU.mult, op1=ALU.add))
        link(nc.vector.tensor_tensor(t2, p2, p0, ALU.subtract))
        link(nc.vector.tensor_scalar(c1, t2, 0.5, None, ALU.mult))
        link(stt(out=t1, in0=p1, scalar=-2.5, in1=p0, op0=ALU.mult, op1=ALU.add))
        link(stt(out=t1, in0=p2, scalar=2.0, in1=t1, op0=ALU.mult, op1=ALU.add))
        link(stt(out=c2, in0=p3, scalar=-0.5, in1=t1, op0=ALU.mult, op1=ALU.add))
        link(nc.vector.tensor_tensor(t1, c3, u, ALU.mult))
        link(stt(out=d2, in0=t1, scalar=3.0, in1=c2, op0=ALU.mult, op1=ALU.add))
        link(nc.vector.tensor_tensor(t2, d2, c2, ALU.add))
        link(nc.vector.tensor_tensor(t2, t2, u, ALU.mult))
        link(nc.vector.tensor_tensor(d1, t2, c1, ALU.add))
        link(nc.vector.tensor_tensor(t1, t1, c2, ALU.add))
        link(nc.vector.tensor_tensor(t1, t1, u, ALU.mult))
        link(nc.vector.tensor_tensor(t1, t1, c1, ALU.add))
        link(nc.vector.tensor_copy(d3, c3))
        link(nc.vector.tensor_tensor(t1, t1, u, ALU.mult))
        link(nc.vector.tensor_tensor(d0, t1, p1, ALU.add))
        whole = "p k m a r -> p (k m a r)"
        exact, hi, lo = dcf.rearrange(whole), dsp[:, 0].rearrange(whole), dsp[:, 1].rearrange(whole)
        nc.vector.tensor_scalar(hi, exact, W_SCALE, None, ALU.mult).then_inc(self.coef_hi, 1)
        dve.wait_ge(self.coef_hi, 1)
        stt(out=lo, in0=exact, scalar=W_SCALE, in1=hi, op0=ALU.mult, op1=ALU.subtract).then_inc(self.coef_lo, 1)

    def constants(self, pool):
        P, const_made = self.P, self.const_made
        n = [0]

        def made(ins):
            n[0] += 1
            ins.then_inc(const_made, 1)
            pool.wait_ge(const_made, n[0])

        g = self.nc.gpsimd
        made(g.memset(P.ident[:], 0.0))
        made(g.affine_select(out=P.ident[:], in_=P.ident[:], compare_op=ALU.not_equal, fill=1.0, base=0,
                             pattern=[[-1, 128]], channel_multiplier=1))
        made(g.memset(P.ones[:], 1.0))
        made(g.affine_select(out=P.after[:], in_=P.ones[:], compare_op=ALU.is_gt, fill=0.0, base=0,
                             pattern=[[-1, 128]], channel_multiplier=1))
        made(g.affine_select(out=P.upto[:], in_=P.ones[:], compare_op=ALU.is_ge, fill=0.0, base=0,
                             pattern=[[1, 128]], channel_multiplier=-1))
        made(g.memset(P.level32[:], 0.0))
        for b in (1, 3):
            made(g.memset(P.level32[SUB * b:SUB * b + SUB, SUB * (b - 1):SUB * b], 1.0))
        made(g.memset(P.pair[:], 0.0))
        for b in range(2):
            made(g.memset(P.pair[DK * b:DK * b + DK, b:b + 1], 1.0))
        made(g.memset(P.mhalf[:], -0.5))
        made(g.memset(P.phalf[:], 0.5))
        made(g.memset(P.S[:], 0.0))
        made(g.memset(P.halo[:], 0.0))
        made(g.memset(P.zeros[:], 0.0))
        assert n[0] == CONSTANTS


def attend(nc, A, scr, P, nst=NST):
    uses, per = bank_uses()
    with ExitStack() as ctx:
        def sb(name, shape, dt=F32):
            return ctx.enter_context(nc.sbuf_tensor(name, shape, dt))

        def sem(name):
            return ctx.enter_context(nc.semaphore(name))

        NCHH = NCH * NH
        xb = sb("xb", [128, NCH, D])
        x_hi = sb("x_hi", [128, HB, ST], F16)
        x_lo = sb("x_lo", [128, HB, ST], F16)
        raw = sb("raw", [128, 3, ST + TAPS - 1])
        cv = sb("cv", [128, 2, ST])
        kq = sb("kq", [128, NPAIR, 2, ST])
        vT = sb("vT", [128, 3, ST])
        V = sb("V", [128, NCH, NH, DV])
        gate = sb("gate", [128, NCH, VD])
        ktok = sb("ktok", [128, NCH, KD])
        BA = sb("BA", [128, 2, NCHH, CH])
        eg = sb("eg", [128, 2, NH, CH])
        Tbd = sb("Tbd", [128, NCHH, CH])
        W = sb("W", [128, NCHH, CH])
        T1 = sb("T1", [64, 2, NH, 64])
        X2s = sb("X2s", [128, 2, NH, 64])
        og_hi = sb("og_hi", [128, NH, CH], F16)
        og_lo = sb("og_lo", [128, NH, CH], F16)
        xr = sb("xr", [128, 2, D])
        junk = sb("junk", [128, NH, DV], BF16)
        bin_ = sb("bin", [NINST, SUB * SUB])
        tin = sb("tin", [NINST, SUB * SUB])
        tmp = sb("tmp", [NINST, 5 * SUB * SUB // 16])
        mv = sb("mv", [128, NCH, 2])
        stats = sb("stats", [128, NCH, 6])
        rstd = sb("rstd", [128, NCH])
        ln_d = sb("ln_d", [128, NCH])
        ab = sb("ab", [128, NCH, 2 * NH])
        z, az, nb, e1, ln1, beta, g = (sb(n, [128, NCH, NH]) for n in ("z", "az", "nb", "e1", "ln1", "beta", "g"))
        eb = sb("eb", [128, NCH, NH])
        sums = sb("sums", [128, 4 * NCHH])
        rk2, cj, eq, nk, gam, ngam, suf, ks = (sb(n, [128, NCHH]) for n in
                                               ("rk2", "cj", "eq", "nk", "gam", "ngam", "suf", "ks"))
        gC = sb("gC", [128, NCH, NPAIR])
        ss = sb("ss", [128, 2, NH])
        t6 = sb("t6", [128, 2, NH])
        rn = sb("rn", [128, 2, NH])
        rb = BA[:, 0, :, :]
        Rr, U = rb[:, 0:NH, :], rb[:, NH:2 * NH, :]
        O = rb[:, 2 * NH:4 * NH, :].rearrange("p (r h) d -> p r h d", r=2)
        sq = BA[:, 1, :, :].rearrange("p (n a) c -> p n (a c)", n=NQK)
        E, gm = eg[:, 0], eg[:, 1]
        tap_products = (eg[:].rearrange("p a h c -> p (a h c)").rearrange("p (t n) -> p t n", t=TAPS - 1), xb[:, 0:TAPS - 1, :])
        bank = [ctx.enter_context(nc.psum_tensor(f"bank{i}", [128, 512], F32)) for i in range(8)]
        full = [sem(f"full{i}") for i in range(8)]
        done = [sem(f"done{i}") for i in range(8)]
        x_in, ln_step, ln_stats, ln_rstd, xn_ready = sem("x_in"), sem("ln_step"), sem("ln_stats"), sem("ln_rstd"), sem("xn_ready")
        xhi_ready, spilled = sem("xhi_ready"), sem("spilled")
        ab_ready, ab_exp, ab_ln, g_ready = sem("ab_ready"), sem("ab_exp"), sem("ab_ln"), sem("g_ready")
        dve_step, t32_step = sem("dve_step"), sem("t32_step")
        halo_used, raw_ready, cv_ready, silu_done, sq_ready = (
            sem("halo_used"), sem("raw_ready"), sem("cv_ready"), sem("silu_done"), sem("sq_ready"))
        dec_ready, nk_ready, ks_ready = sem("dec_ready"), sem("nk_ready"), sem("ks_ready")
        gm_ready, a_masked = sem("gm_ready"), sem("a_masked")
        taps_ready, tap_step, v_conv = sem("taps_ready"), sem("tap_step"), sem("v_conv")
        b_out, b_in, t_out, tt_out, tbd_in, w_in = (sem(n) for n in ("b_out", "b_in", "t_out", "tt_out", "tbd_in", "w_in"))
        ss_ready, t6_ready, rn_ready, og_ready, oghi_ready = (
            sem("ss_ready"), sem("t6_ready"), sem("rn_ready"), sem("og_ready"), sem("oghi_ready"))
        xr_in = [sem(f"xr_in{i}") for i in range(2)]
        y_out = [sem(f"y_out{i}") for i in range(2)]
        prep = Preparation(nc, A, scr, P, sb, sem,
                           [BA[:, 0, NCHH // 2 * i:NCHH // 2 * (i + 1), :].rearrange("p i c -> p (i c)") for i in range(2)]
                           + [V[:, NCH // 2 * i:NCH // 2 * (i + 1), :, :].rearrange("p c h d -> p (c h d)") for i in range(2)],
                           Tbd[:].rearrange("p i c -> p (i c)"), W[:].rearrange("p i c -> p (i c)"))
        late_full, late_done = sem("late_full"), sem("late_done")
        LATE_BANK = uses[("X2", 0)][0]
        block = ctx.enter_context(nc.Block())

        def square_of(n):
            return sq[:, n, :] if n < NPAIR else xb[:, n - NPAIR, :]

        x_v = A.x.rearrange("(s t p) d -> s p t d", t=NCH, p=128)
        y_v = scr.y.rearrange("(s t p) d -> s t p d", t=NCH, p=128)
        xr_v = A.x.rearrange("(s t p) d -> s t p d", t=NCH, p=128)

        def filled(eng, u, s):
            b, n = uses[u]
            eng.wait_ge(full[b], s.val(per[b], n + 1))

        def ready(eng, u, s):
            b, n = uses[u]
            eng.wait_ge(done[b], s.val(per[b], n + 1))

        def out_of(u):
            return bank[uses[u][0]], done[uses[u][0]]

        def ch(c, h):
            return NH * c + h

        @block.tensor
        def _(pe):
            def claim(u, s):
                b, n = uses[u]
                if not (s.first() and n == 0):
                    pe.wait_ge(done[b], s.val(per[b], n))
                return bank[b], full[b]

            def split_product(out, w_hi, w_lo, x_hi_, x_lo_, swap, first=True, last=True):
                todo = ((w_hi, x_hi_), (w_hi, x_lo_), (w_lo, x_hi_))
                for i, (w, xx) in enumerate(todo):
                    a, b = (xx, w) if swap else (w, xx)
                    ins = nc.tensor.matmul(out, a, b, start=first and i == 0, stop=last and i == 2)
                return ins

            def ln_transposes(s, tiles):
                for t in tiles:
                    pe.wait_ge(xn_ready, s.val(NCH, t + 1))
                    ps, f = claim(("ln", t), s)
                    for hb in range(HB):
                        ins = nc.tensor.transpose(ps[:, 128 * hb:128 * hb + 128], xb[:, t, 128 * hb:128 * hb + 128], P.ident[:])
                    ins.then_inc(f, 1)

            def decay_products(s):
                ps, f = claim(("ab",), s)
                for c in range(NCH):
                    for hb in range(HB):
                        ins = split_product(ps[:, 2 * NH * c:2 * NH * (c + 1)], P.wab_hi[:, hb, :], P.wab_lo[:, hb, :],
                                            x_hi[:, hb, CH * c:CH * c + CH], x_lo[:, hb, CH * c:CH * c + CH], True,
                                            hb == 0, hb == HB - 1)
                ins.then_inc(f, 1)

            def gate_products(s, c, h):
                ps, f = claim(("gate", c, h), s)
                col = 2 * KD + VD + 384 * h
                for hb in range(HB):
                    ins = split_product(ps[:, 0:384], P.w_hi[:, hb, col:col + 384], P.w_lo[:, hb, col:col + 384],
                                        x_hi[:, hb, CH * c:CH * c + CH], x_lo[:, hb, CH * c:CH * c + CH], True,
                                        hb == 0, hb == HB - 1)
                ins.then_inc(f, 1)

            def block_products(s, n):
                ps, f = claim(("blk", n), s)
                if n == 0:
                    for t in (NCH - 2, NCH - 1):
                        ready(pe, ("ln", t), s)
                for hb in range(HB):
                    ins = split_product(ps[:], P.w_hi[:, hb, 128 * n:128 * n + 128], P.w_lo[:, hb, 128 * n:128 * n + 128],
                                        x_hi[:, hb, :], x_lo[:, hb, :], False, hb == 0, hb == HB - 1)
                ins.then_inc(f, 1)

            def norms(ps, col, s, which):
                for n in range(NPAIR * which, NPAIR * which + NPAIR):
                    pe.wait_ge(sq_ready, s.val(NQK, n + 1))
                    for c in range(NCH):
                        at = col + NH * c + 2 * (n % NPAIR)
                        ins = nc.tensor.matmul(ps[:, at:at + 2], square_of(n)[:, CH * c:CH * c + CH], P.pair[:], start=True, stop=True)
                return ins

            def token_sums(s):
                ps, f = claim(("sums",), s)
                pe.wait_ge(g_ready, s.val(1, 1))
                gv = g[:].rearrange("p c h -> p (c h)")
                for i, mask in enumerate((P.upto, P.after, P.ones)):
                    nc.tensor.matmul(ps[:, NCHH * i:NCHH * (i + 1)], mask[:], gv, start=True, stop=True)
                norms(ps, 3 * NCHH, s, 0).then_inc(f, 1)

            def query_sums(s):
                ps, f = claim(("qsums",), s)
                norms(ps, 0, s, 1).then_inc(f, 1)

            def k_transposes(s, c):
                ps, f = claim(("ktr", c), s)
                for b in range(NPAIR):
                    ins = nc.tensor.transpose(ps[:, 128 * b:128 * b + 128], kq[:, b, 0, CH * c:CH * c + CH], P.ident[:])
                ins.then_inc(f, 1)

            def chunk_scores(s, c):
                pe.wait_ge(gm_ready, s.val(NCH, c + 1))
                for hf in range(2):
                    ps, f = claim(("D", c, hf), s)
                    nc.tensor.matmul(ps[:, 0:HALF], P.after[:], gm[:, hf:NH:2, :], start=True, stop=True).then_inc(f, 1)
                if c == 0:
                    pe.wait_ge(silu_done, s.val(NBLK, NQK))
                for p, heads in enumerate(KQ_HEADS):
                    ps, f = claim(("KQ", c, p), s)
                    for k, h in enumerate(heads):
                        rows = slice(DK * (h % 2), DK * (h % 2) + DK)
                        ins = nc.tensor.matmul(ps[:, 256 * k:256 * k + 256], kq[rows, h // 2, 0, CH * c:CH * c + CH],
                                               kq[rows, h // 2, :, CH * c:CH * c + CH], start=True, stop=True)
                    ins.then_inc(f, 1)

            def v_transposes(s, n):
                ps, f = claim(("vtr", n), s)
                pe.wait_ge(silu_done, s.val(NBLK, NQK + n + 1))
                for c in range(NCH):
                    ins = nc.tensor.transpose(ps[:, 128 * c:128 * c + 128], vT[:, n % 3, CH * c:CH * c + CH], P.ident[:])
                ins.then_inc(f, 1)

            def solve(s):
                pe.wait_ge(tbd_in, s.val(16 * NSUB, 16 * NSUB))
                for k in range(NCH + 3):
                    if 1 <= k < NV - 1:
                        v_transposes(s, k + 1)
                    if k < NCH:
                        for hf in range(2):
                            ps, f = claim(("X", k, hf), s)
                            for h in range(3):
                                i = ch(k, 2 * h + hf)
                                ins = nc.tensor.matmul(ps[:, 128 * h:128 * h + 128], BA[:, 0, i, :], Tbd[:, i, :], start=True, stop=True)
                            ins.then_inc(f, 1)
                    c = k - 1
                    if 0 <= c < NCH:
                        if c == 0:
                            pe.wait_ge(w_in, s.val(16 * NSUB, 16 * NSUB))
                        ps, f = claim(("Y", c), s)
                        for hf in range(2):
                            ready(pe, ("X", c, hf), s)
                        for h in range(NH):
                            ins = nc.tensor.matmul(ps[0:64, 64 * h:64 * h + 64], W[:, ch(c, h), 0:64],
                                                   eg[:, c % 2, h, 0:64], start=True, stop=True)
                        ins.then_inc(f, 1)
                        for hf in range(2):
                            ps, f = claim(("Z", c, hf), s)
                            for h in range(3):
                                i = 2 * h + hf
                                ins = nc.tensor.matmul(ps[:, 128 * h:128 * h + 128], eg[:, c % 2, i, :], W[:, ch(c, i), :], start=True, stop=True)
                            ins.then_inc(f, 1)
                    c = k - 2
                    if 0 <= c < NCH:
                        if c == 0 and not s.first():
                            pe.wait_ge(late_done, s.val(1, 0))
                        ps, f = claim(("X2", c), s)
                        ready(pe, ("Y", c), s)
                        for h in range(NH):
                            ins = nc.tensor.matmul(ps[:, 64 * h:64 * h + 64], BA[0:64, 0, ch(c, h), :],
                                                   T1[:, c % 2, h, :], start=True, stop=True)
                        ins.then_inc(f, 1)
                    c = k - 3
                    if 0 <= c < NCH:
                        ps, f = claim(("Z2", c), s)
                        ready(pe, ("X2", c), s)
                        for hf in range(2):
                            ready(pe, ("Z", c, hf), s)
                        for h in range(NH):
                            ins = nc.tensor.matmul(ps[0:64, 64 * h:64 * h + 64], X2s[:, c % 2, h, :],
                                                   W[:, ch(c, h), 64:128], start=True, stop=True)
                        ins.then_inc(f, 1)

            def state_product(s, c, name, which, hf):
                ps, f = claim((name, c, hf), s)
                for h in range(hf, NH, 2):
                    rows = slice(DK * (h % 2), DK * (h % 2) + DK)
                    ins = nc.tensor.matmul(ps[:, 128 * (h // 2):128 * (h // 2) + 128], kq[rows, h // 2, which, CH * c:CH * c + CH],
                                           P.S[rows, h // 2, :], start=True, stop=True)
                ins.then_inc(f, 1)

            def recur(s, c):
                if c >= 1:
                    ready(pe, ("dS", c - 1), s)
                for hf in range(2):
                    state_product(s, c, "KS", 0, hf)
                if c >= 2:
                    project_out(s, c - 2)
                ready(pe, ("Z2", c), s)
                for hf in range(2):
                    ps, f = claim(("U", c, hf), s)
                    ready(pe, ("KS", c, hf), s)
                    for h in range(hf, NH, 2):
                        ins = nc.tensor.matmul(ps[:, 128 * (h // 2):128 * (h // 2) + 128], W[:, ch(c, h), :], Rr[:, h, :], start=True, stop=True)
                    ins.then_inc(f, 1)
                for hf in range(2):
                    state_product(s, c, "QS", 1, hf)
                if c >= 1:
                    transpose_out(s, c - 1)
                ps, f = claim(("dS", c), s)
                for hf in range(2):
                    ready(pe, ("U", c, hf), s)
                for h in range(NH):
                    r = DK * (h % 2)
                    ins = nc.tensor.matmul(ps[r:r + DK, 128 * (h // 2):128 * (h // 2) + 128], ktok[:, c, DK * h:DK * h + DK],
                                           U[:, h, :], start=True, stop=True)
                ins.then_inc(f, 1)
                pe.wait_ge(a_masked, s.val(NCH, c + 1))
                for hf in range(2):
                    ps, f = claim(("AU", c, hf), s)
                    for h in range(hf, NH, 2):
                        ins = nc.tensor.matmul(ps[:, 128 * (h // 2):128 * (h // 2) + 128], BA[:, 1, ch(c, h), :], U[:, h, :], start=True, stop=True)
                    ins.then_inc(f, 1)

            def transpose_out(s, c):
                pe.wait_ge(og_ready, s.val(NCH, c + 1))
                for hf in range(2):
                    ps, f = claim(("OT", c, hf), s)
                    for h in range(3):
                        ins = nc.tensor.transpose(ps[:, 128 * h:128 * h + 128], O[:, c % 2, 2 * h + hf, :], P.ident[:])
                    ins.then_inc(f, 1)

            def project_out(s, c):
                if c < NCH - 1:
                    ps, f = claim(("WO", c), s)
                else:
                    ps, f = bank[LATE_BANK], late_full
                for hf in range(2):
                    ready(pe, ("OT", c, hf), s)
                for h in range(NH):
                    ins = split_product(ps[:], P.wo_hi[:, h, :], P.wo_lo[:, h, :], og_hi[:, h, :], og_lo[:, h, :], True,
                                        h == 0, h == NH - 1)
                ins.then_inc(f, 1)

            def outputs_end(s, between):
                project_out(s, NCH - 2)
                between(0)
                transpose_out(s, NCH - 1)
                between(1)

            def local(s, blocks, before=None):
                for n in blocks:
                    block_products(s, n)
                if s.first():
                    pe.wait_ge(prep.lo_done, 5)
                for i in range(2):
                    gate_products(s, i // 2, i % 2)
                token_sums(s)
                for c in range(NCH):
                    chunk_scores(s, c)
                    if c < NCH // 2:
                        k_transposes(s, 2 * c)
                        k_transposes(s, 2 * c + 1)
                if s.first():
                    pe.wait_ge(prep.lo_done, 7)
                for n in range(NV):
                    block_products(s, NQK + n)
                    if n == 0:
                        query_sums(s)
                    gate_products(s, (n + 2) // 2, n % 2)
                v_transposes(s, 0)
                if before is not None:
                    ready(pe, ("KQ", NCH - 1, LATE_BANK - 4), s)
                    project_out(before, NCH - 1)
                v_transposes(s, 1)
                solve(s)

            s0 = At(None, 0)
            pe.wait_ge(prep.const_made, CONSTANTS)
            ln_transposes(s0, range(NCH))
            pe.wait_ge(prep.lo_done, 1)
            for n in range(NPAIR):
                block_products(s0, n)
            pe.wait_ge(prep.lo_done, 3)
            decay_products(s0)
            local(s0, range(NPAIR, NQK))
            pe.wait_ge(prep.lo_done, 9)
            with pe.Fori(0, nst - 1) as r:
                s, b = At(r, 1), At(r, 0)
                for c in range(NCH):
                    recur(b, c)
                    if c == 1:
                        ln_transposes(s, range(0, NCH // 2))
                    if c == 2:
                        ln_transposes(s, range(NCH // 2, NCH))
                for t in (NCH - 2, NCH - 1):
                    ready(pe, ("ln", t), s)
                decay_products(s)
                outputs_end(b, lambda n: block_products(s, n))
                local(s, range(2, NQK), b)
            b = At(None, nst - 1)
            for c in range(NCH):
                recur(b, c)
            outputs_end(b, lambda n: None)
            ready(pe, ("WO", NCH - 2), b)
            project_out(b, NCH - 1)

        @block.vector
        def _(dve):
            steps = Steps(DVE_STEPS)
            t32 = Steps(T32_STEPS)
            v = nc.vector

            def ln_tile_stats(s):
                dve.wait_ge(x_in, s.val(16, 16))
                for t in range(NCH):
                    v.bn_stats(stats[:, t, :], xb[:, t, :]).then_inc(ln_step, 1)

            def ln_moments(s):
                dve.wait_ge(ln_step, s.val(LN_STEPS, NCH))

                def link_ln(ins, n):
                    ins.then_inc(ln_step, 1)
                    dve.wait_ge(ln_step, s.val(LN_STEPS, NCH + n))
                link_ln(v.tensor_tensor(mv[:, :, 0], stats[:, :, 1], stats[:, :, 4], ALU.add), 1)
                link_ln(v.tensor_tensor(ln_d[:], stats[:, :, 1], stats[:, :, 4], ALU.subtract), 2)
                link_ln(v.tensor_tensor(mv[:, :, 1], stats[:, :, 2], stats[:, :, 5], ALU.add), 3)
                link_ln(v.tensor_scalar(mv[:, :, 0], mv[:, :, 0], 0.5, None, ALU.mult), 4)
                link_ln(v.tensor_tensor(ln_d[:], ln_d[:], ln_d[:], ALU.mult), 5)
                link_ln(v.tensor_scalar(mv[:, :, 1], mv[:, :, 1], 1.0 / D, EPS, ALU.mult, ALU.add), 6)
                v.scalar_tensor_tensor(out=mv[:, :, 1], in0=ln_d[:], scalar=0.25, in1=mv[:, :, 1],
                                       op0=ALU.mult, op1=ALU.add).then_inc(ln_stats, 1)

            def ln_apply(s):
                dve.wait_ge(ln_rstd, s.val(1, 1))
                for t in range(NCH):
                    v.tensor_scalar(xb[:, t, :], xb[:, t, :], mv[:, t, 0:1], rstd[:, t:t + 1],
                                    ALU.subtract, ALU.mult).then_inc(xn_ready, 1)

            def xn_parts(s, tiles):
                for t in tiles:
                    ps, d = out_of(("ln", t))
                    dve.wait_ge(xhi_ready, s.val(NCH, t + 1))
                    cols = slice(CH * t, CH * t + CH)
                    v.tensor_tensor(x_lo[:, :, cols], ps[:].rearrange("p (b c) -> p b c", b=HB), x_hi[:, :, cols],
                                    ALU.subtract).then_inc(d, 1)

            def link(ins):
                n = steps.next()
                ins.then_inc(dve_step, 1)
                dve.wait_ge(dve_step, n)

            def decays(s):
                filled(dve, ("ab",), s)
                ps, d = out_of(("ab",))
                v.tensor_copy(ab[:].rearrange("p c n -> p (c n)"), ps[:, 0:2 * NCHH]).then_inc(d, 1)
                ready(dve, ("ab",), s)
                link(v.scalar_tensor_tensor(out=z[:], in0=ab[:, :, 0:NH], scalar=1.0 / W_SCALE,
                                            in1=P.dtb[:].unsqueeze(1).broadcast_to([128, NCH, NH]), op0=ALU.mult, op1=ALU.add))
                link(v.tensor_scalar(nb[:], ab[:, :, NH:2 * NH], -1.0 / W_SCALE, None, ALU.mult))
                v.scalar_tensor_tensor(out=az[:], in0=z[:], scalar=-1.0, in1=z[:], op0=ALU.mult, op1=ALU.max).then_inc(ab_ready, 1)

            def decays_end(s):
                dve.wait_ge(ab_exp, s.val(2, 2))
                link(v.tensor_scalar(eb[:], eb[:], 1.0, None, ALU.add))
                link(v.reciprocal(beta[:], eb[:]))
                dve.wait_ge(ab_ln, s.val(1, 1))
                link(v.scalar_tensor_tensor(out=z[:], in0=z[:], scalar=0.0, in1=ln1[:], op0=ALU.max, op1=ALU.add))
                v.tensor_tensor(g[:], z[:], P.nega[:].unsqueeze(1).broadcast_to([128, NCH, NH]), ALU.mult).then_inc(g_ready, 1)

            def convolve(s, blocks):
                for i in range(TAPS):
                    for n in blocks:
                        if i == 0:
                            dve.wait_ge(raw_ready, s.val(NBLK, n + 1))
                            if not (s.first() and n < 2):
                                dve.wait_ge(silu_done, s.val(NBLK, n - 1))
                        src = raw[:, n % 3, i:i + ST]
                        out = cv[:, n % 2, :]
                        w = P.taps[:, n, i:i + 1]
                        if i == 0:
                            ins = v.tensor_scalar(out, src, w, None, ALU.mult)
                        else:
                            dve.wait_ge(dve_step, last[n])
                            ins = v.scalar_tensor_tensor(out=out, in0=src, scalar=w, in1=out, op0=ALU.mult, op1=ALU.add)
                        if i < TAPS - 1:
                            last[n] = steps.next()
                            ins.then_inc(dve_step, 1)
                        else:
                            ins.then_inc(cv_ready, 1)

            last = {}

            def token_scales(s):
                filled(dve, ("sums",), s)
                ps, d = out_of(("sums",))
                v.tensor_copy(sums[:], ps[:, 0:4 * NCHH]).then_inc(d, 1)
                ready(dve, ("sums",), s)
                link(v.reciprocal(rk2[:], sums[:, 3 * NCHH:4 * NCHH]))
                link(v.tensor_tensor(cj[:], rk2[:], beta[:].rearrange("p c h -> p (c h)"), ALU.mult))
                dve.wait_ge(dec_ready, s.val(4, 4))
                v.tensor_scalar(ngam[:], gam[:], -1.0, None, ALU.mult).then_inc(ks_ready, 1)
                v.tensor_tensor(ks[:], cj[:], suf[:], ALU.mult).then_inc(ks_ready, 1)
                dve.wait_ge(ks_ready, s.val(2, 2))

            def query_scales(s):
                u = ("qsums",)
                filled(dve, u, s)
                ps, d = out_of(u)
                v.tensor_scalar(eq[:], ps[:, 0:NCHH], DK * EPS / W_SCALE ** 2, None, ALU.mult).then_inc(d, 1)

            def k_tokens(s, c):
                filled(dve, ("ktr", c), s)
                ps, d = out_of(("ktr", c))
                v.tensor_tensor(ktok[:, c, :].rearrange("p (h k) -> p h k", h=NH), ps[:, 0:KD].rearrange("p (h k) -> p h k", h=NH),
                                ks[:, NH * c:NH * c + NH].unsqueeze(2).broadcast_to([128, NH, DK]), ALU.mult).then_inc(d, 1)

            def scores(s, c):
                for hf in range(2):
                    ready(dve, ("D", c, hf), s)
                for p, heads in enumerate(KQ_HEADS):
                    u = ("KQ", c, p)
                    filled(dve, u, s)
                    ps, d = out_of(u)
                    for k, h in enumerate(heads):
                        ins = v.scalar_tensor_tensor(out=BA[:, :, ch(c, h), :],
                                                     in0=ps[:, 256 * k:256 * k + 256].rearrange("p (k c) -> p k c", k=2),
                                                     scalar=cj[:, ch(c, h):ch(c, h) + 1],
                                                     in1=E[:, h, :].unsqueeze(1).broadcast_to([128, 2, CH]),
                                                     op0=ALU.mult, op1=ALU.mult)
                    ins.then_inc(d, 1)

            def invert_blocks(s):
                t32.start(s)

                def step(ins):
                    ins.then_inc(t32_step, 1)
                    return t32.next()

                if not s.first():
                    dve.wait_ge(t_out, s.val(16, 0))
                    dve.wait_ge(tt_out, s.val(16, 0))
                dve.wait_ge(t32_step, step(v.memset(tin[:], 0.0)))
                ones = step(v.memset(tin[:, 0:SUB * SUB:SUB + 1], 1.0))
                dve.wait_ge(b_in, s.val(16, 16))
                tv = tin[:].rearrange("p (i c) -> p i c", i=SUB)
                half = SUB // 2
                done_to = [ones, ones]
                for j in range(SUB - 1):
                    n = SUB - 1 - j
                    todo = []
                    for k in range(2):
                        c0, c1 = half * k, min(half * (k + 1), j + 1)
                        if c0 < c1:
                            prod = tmp[:, half * half * k:half * half * k + n * (c1 - c0)]
                            todo.append((k, c0, c1, prod.rearrange("p (i c) -> p i c", i=n)))
                    for k, c0, c1, prod in todo:
                        dve.wait_ge(t32_step, done_to[k])
                        done_to[k] = step(v.tensor_tensor(
                            prod, bin_[:, SUB * j + j + 1:SUB * j + SUB].unsqueeze(2).broadcast_to([NINST, n, c1 - c0]),
                            tv[:, j, c0:c1].unsqueeze(1).broadcast_to([NINST, n, c1 - c0]), ALU.mult))
                    for k, c0, c1, prod in todo:
                        dve.wait_ge(t32_step, done_to[k])
                        rest = tv[:, j + 1:SUB, c0:c1]
                        done_to[k] = step(v.tensor_tensor(rest, rest, prod, ALU.subtract))
                dve.wait_ge(t32_step, done_to[0])
                dve.wait_ge(t32_step, done_to[1])
                step(v.tensor_copy(bin_[:].rearrange("p (c i) -> p c i", c=SUB), tin[:].rearrange("p (i c) -> p c i", i=SUB)))

            def heads3(ps):
                return ps[:, 0:HALF].rearrange("p (h d) -> p h d", h=3)

            def heads64(ps, lo_):
                return ps[lo_:lo_ + 64, 0:64 * NH].rearrange("p (h d) -> p h d", h=NH)

            def solve(s):
                dve.wait_ge(v_conv, s.val(NV, NV - 1))
                for k in range(NCH + 3):
                    if k < NCH:
                        for hf in range(2):
                            filled(dve, ("X", k, hf), s)
                            ps, d = out_of(("X", k, hf))
                            v.tensor_tensor(eg[:, k % 2, hf:NH:2, :], heads3(ps),
                                            P.level32[:].unsqueeze(1).broadcast_to([128, 3, CH]), ALU.mult).then_inc(d, 1)
                    c = k - 1
                    if 0 <= c < NCH:
                        filled(dve, ("Y", c), s)
                        ps, d = out_of(("Y", c))
                        v.tensor_tensor(T1[:, c % 2, :, :], Tbd[0:64, NH * c:NH * c + NH, 0:64], heads64(ps, 0),
                                        ALU.subtract).then_inc(d, 1)
                        for hf in range(2):
                            filled(dve, ("Z", c, hf), s)
                            ps, d = out_of(("Z", c, hf))
                            ws = W[:, NH * c + hf:NH * c + NH:2, :]
                            v.tensor_tensor(ws, ws, heads3(ps), ALU.subtract).then_inc(d, 1)
                    c = k - 3
                    if 0 <= c < NCH:
                        filled(dve, ("Z2", c), s)
                        ps, d = out_of(("Z2", c))
                        for hf in range(2):
                            ready(dve, ("Z", c, hf), s)
                        w = W[0:64, NH * c:NH * c + NH, 64:128]
                        v.tensor_tensor(w, w, heads64(ps, 0), ALU.subtract).then_inc(d, 1)

            def right_sides(s, c):
                for hf in range(2):
                    u = ("KS", c, hf)
                    filled(dve, u, s)
                    ps, d = out_of(u)
                    for h in range(hf, NH, 2):
                        ins = v.scalar_tensor_tensor(out=Rr[:, h, :], in0=ps[:, 128 * (h // 2):128 * (h // 2) + 128],
                                                     scalar=ngam[:, ch(c, h):ch(c, h) + 1], in1=V[:, c, h, :],
                                                     op0=ALU.mult, op1=ALU.add)
                    ins.then_inc(d, 1)

            def state(s, c):
                u = ("dS", c)
                filled(dve, u, s)
                ps, d = out_of(u)
                for b in range(NPAIR):
                    ins = v.scalar_tensor_tensor(out=P.S[:, b, :], in0=P.S[:, b, :], scalar=gC[:, c, b:b + 1],
                                                 in1=ps[:, 128 * b:128 * b + 128], op0=ALU.mult, op1=ALU.add)
                ins.then_inc(d, 1)

            def outputs(s, c):
                for hf in range(2):
                    ready(dve, ("QS", c, hf), s)
                    u = ("AU", c, hf)
                    filled(dve, u, s)
                    ps, d = out_of(u)
                    o = O[:, c % 2, hf:NH:2, :]
                    v.tensor_tensor(o, heads3(ps), o, ALU.add).then_inc(d, 1)

            def mean_squares(s, c):
                dve.wait_ge(ss_ready, s.val(NCH, c + 1))
                v.scalar_tensor_tensor(out=t6[:, c % 2, :], in0=ss[:, c % 2, :], scalar=1.0 / (DV * W_SCALE ** 2),
                                       in1=eq[:, NH * c:NH * c + NH], op0=ALU.mult, op1=ALU.add).then_inc(t6_ready, 1)

            def gated(s, c):
                dve.wait_ge(rn_ready, s.val(NCH, c + 1))
                for h in range(NH):
                    o = O[:, c % 2, h, :]
                    ins = v.scalar_tensor_tensor(out=o, in0=o, scalar=rn[:, c % 2, h:h + 1],
                                                 in1=gate[:, c, DV * h:DV * h + DV], op0=ALU.mult, op1=ALU.mult)
                ins.then_inc(og_ready, 1)

            def og_part(s, c):
                for hf in range(2):
                    dve.wait_ge(oghi_ready, s.val(2 * NCH, 2 * c + hf + 1))
                    ps, d = out_of(("OT", c, hf))
                    hs = slice(hf, NH, 2)
                    v.tensor_tensor(og_lo[:, hs, :], heads3(ps), og_hi[:, hs, :], ALU.subtract).then_inc(d, 1)

            def residual(s, c):
                if c < NCH - 1:
                    filled(dve, ("WO", c), s)
                    ps, d = out_of(("WO", c))
                else:
                    dve.wait_ge(late_full, s.val(1, 1))
                    ps, d = bank[LATE_BANK], late_done
                dve.wait_ge(xr_in[c % 2], s.val(16 * NCH // 2, 16 * (c // 2 + 1)))
                v.scalar_tensor_tensor(out=xr[:, c % 2, :], in0=ps[:], scalar=W_SCALE ** -2, in1=xr[:, c % 2, :],
                                       op0=ALU.mult, op1=ALU.add).then_inc(d, 1)

            def local(s, first, before=None):
                for n in range(first, NQK, 2):
                    convolve(s, (n, n + 1))
                token_scales(s)
                for c in range(NCH):
                    scores(s, c)
                    if s.first() and c < NSTG - 1:
                        prep.piece_low(dve, NSTG + 1 + c)
                    if c < NCH // 2:
                        k_tokens(s, 2 * c)
                        k_tokens(s, 2 * c + 1)
                query_scales(s)
                if s.first():
                    prep.spline_coefficients(dve)
                invert_blocks(s)
                if before is not None:
                    residual(before, NCH - 1)
                solve(s)

            def recur(b, c, following=None):
                right_sides(b, c)
                if following is not None and c == 0:
                    ln_tile_stats(following)
                if c >= 1:
                    mean_squares(b, c - 1)
                if following is not None and c == 1:
                    ln_apply(following)
                if c >= 2:
                    residual(b, c - 2)
                if c >= 1:
                    gated(b, c - 1)
                state(b, c)
                if following is not None and c == 0:
                    ln_moments(following)
                if c >= 1:
                    og_part(b, c - 1)
                outputs(b, c)

            def outputs_end(b):
                mean_squares(b, NCH - 1)
                gated(b, NCH - 1)
                residual(b, NCH - 2)
                og_part(b, NCH - 1)

            s0 = At(None, 0)
            steps.start(s0)
            ln_tile_stats(s0)
            ln_moments(s0)
            ln_apply(s0)
            prep.piece_low(dve, 0)
            xn_parts(s0, range(NCH))
            prep.piece_low(dve, 1)
            prep.decay_weights_low(dve)
            prep.piece_low(dve, 2)
            prep.piece_low(dve, 3)
            dve.wait_ge(prep.small_in, prep.SMALL)
            dve.wait_ge(prep.nega_ready, 2)
            dve.wait_ge(prep.const_made, CONSTANTS)
            convolve(s0, (0, 1))
            decays(s0)
            convolve(s0, (2, 3))
            decays_end(s0)
            convolve(s0, (4, 5))
            prep.piece_low(dve, NSTG)
            local(s0, NQK)
            with dve.Fori(0, nst - 1) as r:
                s, b = At(r, 1), At(r, 0)
                steps.start(s)
                recur(b, 0, s)
                recur(b, 1, s)
                xn_parts(s, range(0, NCH // 2))
                recur(b, 2)
                xn_parts(s, range(NCH // 2, NCH))
                recur(b, 3)
                decays(s)
                outputs_end(b)
                convolve(s, (0, 1))
                decays_end(s)
                local(s, 2, b)
            b = At(None, nst - 1)
            for c in range(NCH):
                recur(b, c)
            outputs_end(b)
            residual(b, NCH - 1)

        @block.scalar
        def _(act):
            sc = nc.scalar

            def xn_high(s, tiles):
                if not s.first() and tiles[0] == 0:
                    act.wait_ge(spilled, s.val(32, 0))
                for t in tiles:
                    filled(act, ("ln", t), s)
                    ps, _ = out_of(("ln", t))
                    sc.activation(x_hi[:, :, CH * t:CH * t + CH], ps[:].rearrange("p (b c) -> p b c", b=HB),
                                  ACT.Copy).then_inc(xhi_ready, 1)

            def decays(s):
                act.wait_ge(ab_ready, s.val(1, 1))
                sc.activation(e1[:], az[:], ACT.Exp, scale=-1.0).then_inc(ab_exp, 1)
                sc.activation(eb[:], nb[:], ACT.Exp).then_inc(ab_exp, 1)
                act.wait_ge(ab_exp, s.val(2, 1))
                sc.activation(ln1[:], e1[:], ACT.Ln, bias=P.ones[:, 0:1]).then_inc(ab_ln, 1)

            def gates(s, c, h):
                if not s.first():
                    act.wait_ge(og_ready, s.val(NCH, 0))
                u = ("gate", c, h)
                filled(act, u, s)
                ps, d = out_of(u)
                sc.activation(gate[:, c, 384 * h:384 * h + 384], ps[:, 0:384], ACT.Silu, scale=1.0 / W_SCALE).then_inc(d, 1)

            def raw_out(s, n):
                u = ("blk", n)
                filled(act, u, s)
                ps, d = out_of(u)
                if not (s.first() and n < 3):
                    act.wait_ge(raw_ready, s.val(NBLK, n - 2))
                    if 3 <= n < NQK + 3:
                        act.wait_ge(cv_ready, s.val(NQK, n - 2))
                    else:
                        act.wait_ge(v_conv, s.val(NV, (n - 2 if n < 3 else n - NQK - 2)))
                sc.activation(raw[:, n % 3, TAPS - 1:], ps[:], ACT.Copy, scale=1.0 / W_SCALE).then_inc(d, 1)

            def v_taps(s, n):
                i = n - NQK
                act.wait_ge(raw_ready, s.val(NBLK, n + 1))
                act.wait_ge(silu_done, s.val(NBLK, n - 1))
                if i >= 2:
                    act.wait_ge(v_conv, s.val(NV, i - 1))
                else:
                    filled(act, ("D", NCH - 1, 1), s)
                    ready(act, ("KQ", NCH - 1, len(KQ_HEADS) - 1), s)
                    if i == 1:
                        filled(act, ("qsums",), s)
                for t in range(TAPS):
                    dst = cv[:, n % 2, :] if t == 0 else tap_products[i % 2][:, t - 1, :]
                    ins = sc.activation(dst, raw[:, n % 3, t:t + ST], ACT.Copy, scale=P.taps[:, n, t:t + 1])
                ins.then_inc(taps_ready, 1)

            def v_tokens(s, n):
                u = ("vtr", n)
                filled(act, u, s)
                ps, d = out_of(u)
                if n == 0:
                    act.wait_ge(nk_ready, s.val(1, 1))
                for c in range(NCH):
                    ins = sc.activation(V[:, c, n, :], ps[:, 128 * c:128 * c + 128], ACT.Copy, scale=nk[:, ch(c, n):ch(c, n) + 1])
                ins.then_inc(d, 1)

            def silu(s, n):
                if n < NQK:
                    act.wait_ge(cv_ready, s.val(NQK, n + 1))
                    dst = kq[:, n % NPAIR, n // NPAIR, :]
                else:
                    act.wait_ge(v_conv, s.val(NV, n - NQK + 1))
                    dst = vT[:, n % 3, :]
                    if n - NQK >= 3:
                        filled(act, ("vtr", n - NQK - 3), s)
                sc.activation(dst, cv[:, n % 2, :], ACT.Silu).then_inc(silu_done, 1)

            def decay_exps(s):
                ready(act, ("sums",), s)
                tot = sums[:, 2 * NCHH:3 * NCHH].rearrange("p (c b r) -> p c b r", c=NCH, r=2)
                sc.activation(gam[:], sums[:, 0:NCHH], ACT.Exp).then_inc(dec_ready, 1)
                sc.activation(suf[:], sums[:, NCHH:2 * NCHH], ACT.Exp).then_inc(dec_ready, 1)
                for r in range(2):
                    rows = slice(DK * r, DK * r + DK)
                    sc.activation(gC[rows, :, :], tot[rows, :, :, r], ACT.Exp).then_inc(dec_ready, 1)

            def pair_exps(s, c):
                if c:
                    ready(act, ("KQ", c - 1, len(KQ_HEADS) - 1), s)
                for hf in range(2):
                    u = ("D", c, hf)
                    filled(act, u, s)
                    ps, d = out_of(u)
                    sc.activation(E[:, hf:NH:2, :], ps[:, 0:HALF].rearrange("p (h c) -> p h c", h=3), ACT.Exp).then_inc(d, 1)

            def local(s):
                for n in range(NQK):
                    raw_out(s, n)
                    if n == 1 and not s.first():
                        decays(s)
                    if n == 1 and s.first():
                        prep.piece_high(act, NSTG)
                    if n >= 2:
                        silu(s, n - 2)
                    if n == 3 and s.first():
                        decays(s)
                gates(s, 0, 0)
                gates(s, 0, 1)
                silu(s, NQK - 2)
                silu(s, NQK - 1)
                decay_exps(s)
                for c in range(NCH):
                    pair_exps(s, c)
                    if s.first() and c < NSTG - 1:
                        prep.piece_high(act, NSTG + 1 + c)
                for n in range(NV):
                    raw_out(s, NQK + n)
                    if n == NV - 1:
                        silu(s, NQK + n - 2)
                    v_taps(s, NQK + n)
                    gates(s, (n + 2) // 2, n % 2)
                    if n in (1, 2, 3, NV - 1):
                        silu(s, NQK + n - 1)
                v_tokens(s, 0)
                v_tokens(s, 1)
                silu(s, NBLK - 1)
                for c in range(NCH):
                    v_tokens(s, c + 2)
                    u = ("X2", c)
                    filled(act, u, s)
                    ps, d = out_of(u)
                    sc.activation(X2s[:, c % 2, :, :], ps[:, 0:64 * NH].rearrange("p (h c) -> p h c", h=NH), ACT.Copy).then_inc(d, 1)

            def q_state(s, c):
                for hf in range(2):
                    u = ("QS", c, hf)
                    filled(act, u, s)
                    ps, d = out_of(u)
                    for h in range(hf, NH, 2):
                        ins = sc.activation(O[:, c % 2, h, :], ps[:, 128 * (h // 2):128 * (h // 2) + 128], ACT.Copy,
                                            scale=gam[:, ch(c, h):ch(c, h) + 1])
                    ins.then_inc(d, 1)

            def updates(s, c):
                for hf in range(2):
                    u = ("U", c, hf)
                    filled(act, u, s)
                    ps, d = out_of(u)
                    sc.activation(U[:, hf:NH:2, :], ps[:, 0:HALF].rearrange("p (h d) -> p h d", h=3), ACT.Copy).then_inc(d, 1)

            def squares(s, c):
                if c:
                    act.wait_ge(ss_ready, s.val(NCH, c))
                for h in range(NH):
                    if h < 2:
                        ready(act, ("AU", c, h), s)
                    ins = sc.activation(junk[:, h, :], O[:, c % 2, h, :], ACT.Square, accum_out=ss[:, c % 2, h:h + 1])
                ins.then_inc(ss_ready, 1)

            def og_high(s, c):
                for hf in range(2):
                    u = ("OT", c, hf)
                    filled(act, u, s)
                    ps, _ = out_of(u)
                    sc.activation(og_hi[:, hf:NH:2, :], ps[:, 0:HALF].rearrange("p (h c) -> p h c", h=3),
                                  ACT.Copy).then_inc(oghi_ready, 1)

            def recur(b, c):
                updates(b, c)
                q_state(b, c)
                if c >= 1:
                    og_high(b, c - 1)
                squares(b, c)

            def outputs_end(b):
                og_high(b, NCH - 1)
                act.wait_ge(ss_ready, b.val(NCH, NCH))

            s0 = At(None, 0)
            for i in range(NSTG):
                prep.load_piece(act, i)
            prep.piece_high(act, 0)
            act.wait_ge(prep.const_made, CONSTANTS)
            xn_high(s0, range(NCH))
            prep.piece_high(act, 1)
            prep.decay_weights_high(act)
            prep.piece_high(act, 2)
            prep.piece_high(act, 3)
            prep.decay_rates(act)
            local(s0)
            with act.Fori(0, nst - 1) as r:
                s, b = At(r, 1), At(r, 0)
                for c in range(NCH):
                    recur(b, c)
                    if c == 1:
                        xn_high(s, range(0, NCH // 2))
                    if c == 2:
                        xn_high(s, range(NCH // 2, NCH))
                outputs_end(b)
                local(s)
            b = At(None, nst - 1)
            for c in range(NCH):
                recur(b, c)
            outputs_end(b)

        @block.gpsimd
        def _(pool):
            g_ = nc.gpsimd

            def ln_scale(s):
                pool.wait_ge(ln_stats, s.val(1, 1))
                g_.tensor_tensor(out=rstd[:], in0=mv[:, :, 1], in1=P.mhalf[:, 0:NCH], op=ALU.pow).then_inc(ln_rstd, 1)

            def spill(s):
                for t in (NCH - 2, NCH - 1):
                    ready(pool, ("ln", t), s)
                pool.dma_start(scr.xh[s.idx()], x_hi[:].rearrange("p b c -> p (b c)")).then_inc(spilled, 16)
                pool.dma_start(scr.xl[s.idx()], x_lo[:].rearrange("p b c -> p (b c)")).then_inc(spilled, 16)

            def norm_scale(s, c):
                pool.wait_ge(t6_ready, s.val(NCH, c + 1))
                g_.tensor_tensor(out=rn[:, c % 2, :], in0=t6[:, c % 2, :], in1=P.mhalf[:, 0:NH], op=ALU.pow).then_inc(rn_ready, 1)

            def halo(s, n):
                ready(pool, ("blk", n), s)
                g_.tensor_tensor(out=raw[:, n % 3, 0:TAPS - 1], in0=P.halo[:, n, :], in1=P.zeros[:], op=ALU.add).then_inc(halo_used, 1)
                pool.wait_ge(halo_used, s.val(NBLK, n + 1))
                g_.tensor_tensor(out=P.halo[:, n, :], in0=raw[:, n % 3, ST:ST + TAPS - 1], in1=P.zeros[:], op=ALU.add).then_inc(raw_ready, 1)

            def add_taps(s, n):
                i = n - NQK
                tp, c = tap_products[i % 2], cv[:, n % 2, :]
                pool.wait_ge(taps_ready, s.val(NV, i + 1))
                g_.tensor_tensor(out=c, in0=c, in1=tp[:, 0, :], op=ALU.add).then_inc(tap_step, 1)
                g_.tensor_tensor(out=tp[:, 1, :], in0=tp[:, 1, :], in1=tp[:, 2, :], op=ALU.add).then_inc(tap_step, 1)
                pool.wait_ge(tap_step, s.val(2 * NV, 2 * i + 2))
                g_.tensor_tensor(out=c, in0=c, in1=tp[:, 1, :], op=ALU.add).then_inc(v_conv, 1)

            def square(s, n):
                pool.wait_ge(silu_done, s.val(NBLK, n + 1))
                src = kq[:, n % NPAIR, n // NPAIR, :]
                g_.tensor_tensor(out=square_of(n), in0=src, in1=src, op=ALU.mult).then_inc(sq_ready, 1)

            def masked_g(s, c):
                if c:
                    filled(pool, ("D", c - 1, 1), s)
                g_.tensor_tensor(out=gm[:], in0=P.upto[:].unsqueeze(1).broadcast_to([128, NH, CH]),
                                 in1=g[:, c, :].unsqueeze(2).broadcast_to([128, NH, CH]), op=ALU.mult).then_inc(gm_ready, 1)

            def mask_weights(s, c):
                ready(pool, ("KQ", c, len(KQ_HEADS) - 1), s)
                a = BA[:, 1, NH * c:NH * c + NH, :]
                g_.tensor_tensor(out=a, in0=a, in1=P.upto[:].unsqueeze(1).broadcast_to([128, NH, CH]),
                                 op=ALU.mult).then_inc(a_masked, 1)

            def local(s):
                for n in range(NQK):
                    halo(s, n)
                    if n == 4:
                        pool.wait_ge(g_ready, s.val(1, 1))
                        masked_g(s, 0)
                    if n >= 2:
                        square(s, n - 2)
                square(s, NQK - 2)
                ready(pool, ("sums",), s)
                g_.tensor_tensor(out=nk[:], in0=sums[:, 3 * NCHH:4 * NCHH], in1=P.phalf[:, 0:NCHH],
                                 op=ALU.pow).then_inc(nk_ready, 1)
                masked_g(s, 1)
                square(s, NQK - 1)
                for c in range(1, NCH):
                    if c + 1 < NCH:
                        masked_g(s, c + 1)
                    mask_weights(s, c - 1)
                for n in range(NQK, NBLK + 1):
                    if n < NBLK:
                        halo(s, n)
                    if n > NQK:
                        add_taps(s, n - 1)
                mask_weights(s, NCH - 1)

            s0 = At(None, 0)
            prep.constants(pool)
            ln_scale(s0)
            spill(s0)
            local(s0)
            pool.wait_ge(prep.coef_out, 12 * 16)
            g_.memset(Tbd[:], 0.0)
            g_.memset(W[:], 0.0).then_inc(prep.cleared, 1)
            with pool.Fori(0, nst - 1) as r:
                s, b = At(r, 1), At(r, 0)
                ln_scale(s)
                norm_scale(b, 0)
                norm_scale(b, 1)
                spill(s)
                for c in range(2, NCH):
                    norm_scale(b, c)
                g_.memset(W[:], 0.0)
                local(s)
            b = At(None, nst - 1)
            for c in range(NCH):
                norm_scale(b, c)

        @block.sync
        def _(sp):
            def load_x(s, b):
                if b is not None:
                    sp.wait_ge(v_conv, b.val(NV, NV))
                sp.dma_start(xb[:], x_v[s.idx()]).then_inc(x_in, 16)

            def load_residual(s, c):
                if not (s.first() and c < 2):
                    sp.wait_ge(y_out[c % 2], s.val(16 * NCH // 2, 16 * (c // 2)))
                sp.dma_start(xr[:, c % 2, :], xr_v[s.idx(), c]).then_inc(xr_in[c % 2], 16)

            def store_y(s, c):
                if c < NCH - 1:
                    ready(sp, ("WO", c), s)
                else:
                    sp.wait_ge(late_done, s.val(1, 1))
                sp.dma_start(y_v[s.idx(), c], xr[:, c % 2, :]).then_inc(y_out[c % 2], 16)

            def store_first(s):
                for c in range(NCH - 1):
                    store_y(s, c)
                    if c + 2 < NCH:
                        load_residual(s, c + 2)

            def exchange(s):
                ready(sp, ("KQ", NCH - 1, len(KQ_HEADS) - 1), s)
                for q in range(NSUB):
                    rows = slice(SUB * q, SUB * q + SUB)
                    sp.dma_start(scr.b[q].rearrange("c j i -> j c i"), BA[rows, 0, :, rows]).then_inc(b_out, 16)
                sp.wait_ge(b_out, s.val(16 * NSUB, 16 * NSUB))
                sp.dma_start(bin_[:], scr.b.rearrange("q c j i -> (q c) (j i)")).then_inc(b_in, 16)
                if s.first():
                    prep.store_coefficients(sp)
                sp.wait_ge(t32_step, s.val(T32_STEPS, T32_STEPS - 1))
                sp.dma_start(scr.t.rearrange("q c i k -> (q c) (i k)"), tin[:]).then_inc(t_out, 16)
                sp.wait_ge(t32_step, s.val(T32_STEPS, T32_STEPS))
                sp.dma_start(scr.tt.rearrange("q c k i -> (q c) (k i)"), bin_[:]).then_inc(tt_out, 16)
                sp.wait_ge(t_out, s.val(16, 16))
                if s.first():
                    sp.wait_ge(prep.cleared, 1)
                for q in range(NSUB):
                    rows = slice(SUB * q, SUB * q + SUB)
                    sp.dma_start(Tbd[rows, :, rows], scr.t[q].rearrange("c i k -> i c k")).then_inc(tbd_in, 16)
                sp.wait_ge(tt_out, s.val(16, 16))
                for q in range(NSUB):
                    rows = slice(SUB * q, SUB * q + SUB)
                    sp.dma_start(W[rows, :, rows], scr.tt[q].rearrange("c k i -> k c i")).then_inc(w_in, 16)

            s0 = At(None, 0)
            load_x(s0, None)
            prep.load_decay_weights(sp)
            prep.load_small(sp)
            prep.pad_control_points(sp)
            for i in range(NSTG, 2 * NSTG):
                prep.load_piece(sp, i)
            prep.gather_control_points(sp)
            load_residual(s0, 0)
            load_residual(s0, 1)
            exchange(s0)
            with sp.Fori(0, nst - 1) as r:
                s, b = At(r, 1), At(r, 0)
                load_x(s, b)
                store_first(b)
                exchange(s)
                load_residual(s, 0)
                store_y(b, NCH - 1)
                load_residual(s, 1)
            store_first(At(None, nst - 1))
            store_y(At(None, nst - 1), NCH - 1)
            for i in range(2):
                sp.wait_ge(y_out[i], 16 * NCH // 2 * nst)
            sp.wait_ge(spilled, 32 * nst)


CONSTANTS = 16
DVE_STEPS = 3 * NQK + 5 + 2
LN_STEPS = NCH + 6
T32_STEPS = 3 + 2 * (SUB - 1) + SUB - 2


def feed(nc, A, scr, nst=NST):
    with ExitStack() as ctx:
        def sb(name, shape, dt=F32):
            return ctx.enter_context(nc.sbuf_tensor(name, shape, dt))

        def sem(name):
            return ctx.enter_context(nc.semaphore(name))

        NM = 3
        GC = NCOL // IB
        gu_hi = sb("gu_hi", [128, 2, HB, INTER], F16)
        gu_lo = sb("gu_lo", [128, 2, HB, INTER], F16)
        d_hi = sb("d_hi", [128, IB, D], F16)
        d_lo = sb("d_lo", [128, IB, D], F16)
        x_hi = sb("fx_hi", [128, HB, ST], F16)
        x_lo = sb("fx_lo", [128, HB, ST], F16)
        it_hi = sb("it_hi", [128, IB, ST], F16)
        it_lo = sb("it_lo", [128, IB, ST], F16)
        sg = sb("sg", [128, 2, ST])
        hh = sb("hh", [128, 2, ST])
        yr = sb("yr", [128, 2, D])
        wt = sb("wt", [128, 2, GC])
        knot = sb("knot", [128, 2, GC])
        rows = sb("rows", [128, 1])
        later = sb("later", [128, 2, GC], U8)
        pow_in = sb("pow_in", [12, 128])
        coef = sb("coef", [12, 2, 2 * NM, GC], F16)
        powers = sb("powers", [12, 128], F16)
        pg = [ctx.enter_context(nc.psum_tensor(f"pg{i}", [128, 512], F32)) for i in range(2)]
        pu = [ctx.enter_context(nc.psum_tensor(f"pu{i}", [128, 512], F32)) for i in range(2)]
        pw = [ctx.enter_context(nc.psum_tensor(f"pw{i}", [128, 512], F32)) for i in range(4)]
        const_in, x_in, y_in, y_out = sem("const_in"), sem("fx_in"), [sem(f"y_in{i}") for i in range(2)], [sem(f"out{i}") for i in range(2)]
        coef_in = [sem(f"coef_in{i}") for i in range(2)]
        poly_made, first_copied, picked, w_hi_made, w_made = (
            sem("poly_made"), sem("first_copied"), sem("picked"), sem("w_hi_made"), sem("w_made"))
        gate_made, up_made, sg_ready, h_ready, hi_ready, it_ready = (
            sem("gate_made"), sem("up_made"), sem("sg_ready"), sem("h_ready"), sem("hi_ready"), sem("it_ready"))
        down_made, down_read = sem("down_made"), sem("down_read")
        later_made, powers_ready = sem("later_made"), sem("powers_ready")
        block = ctx.enter_context(nc.Block())
        y_v = scr.y.rearrange("(s t p) d -> s t p d", t=NCH, p=128)
        o_v = A.out.rearrange("(n p) d -> n p d", p=128)

        def weight_block(part, m, i):
            if m < 2:
                return (gu_hi, gu_lo)[part][:, m, :, 128 * i:128 * i + 128]
            n = GC // IB
            return (d_hi, d_lo)[part][:, :, n * i:n * i + n]

        def by_block(t, m):
            nb = HB if m < 2 else IB
            return t.rearrange("p (o b) -> p b o", b=nb)

        @block.sync
        def _(sp):

            def load_coef(i):
                if i >= 2:
                    sp.wait_ge(poly_made, NM * (i - 1))
                    sp.wait_ge(later_made, i - 1)
                sp.dma_start(knot[:, i % 2, :], A.knot[GC * i:GC * i + GC].partition_broadcast(128)).then_inc(coef_in[i % 2], 16)
                for row, part in ((0, 0), (4, 0), (8, 1)):
                    sp.dma_start(coef[row:row + 4, i % 2, :, :],
                                 scr.coef[part, :, :, :, GC * i:GC * i + GC].rearrange("k m a c -> k (m a) c")
                                 ).then_inc(coef_in[i % 2], 16)

            def store(s):
                for t in range(NCH):
                    sp.wait_ge(down_read, s.val(NCH, t + 1))
                    sp.dma_start(o_v[s.val(NCH, t)], yr[:, t % 2, :]).then_inc(y_out[t % 2], 16)

            s0 = At(None, 0)
            for i in range(IB):
                load_coef(i)
            store(s0)
            with sp.Fori(0, nst - 1) as r:
                store(At(r, 1))
            for i in range(2):
                sp.wait_ge(y_out[i], 16 * NCH // 2 * nst)

        @block.gpsimd
        def _(pool):
            def load_x(s):
                if not s.first():
                    pool.wait_ge(up_made, s.val(IB, 0))
                pool.dma_start(x_hi[:].rearrange("p b c -> p (b c)"), scr.xh[s.idx()]).then_inc(x_in, 16)
                pool.dma_start(x_lo[:].rearrange("p b c -> p (b c)"), scr.xl[s.idx()]).then_inc(x_in, 16)

            def load_y(s, t):
                if not (s.first() and t < 2):
                    pool.wait_ge(y_out[t % 2], s.val(16 * NCH // 2, 16 * (t // 2)))
                pool.dma_start(yr[:, t % 2, :], y_v[s.idx(), t]).then_inc(y_in[t % 2], 16)

            pool.wait_ge(const_in, 32)
            load_x(At(None, 0))
            for t in range(NCH):
                load_y(At(None, 0), t)
            with pool.Fori(0, nst - 1) as r:
                load_x(At(r, 1))
                for t in range(NCH):
                    load_y(At(r, 1), t)

        @block.tensor
        def _(pe):
            def polynomial(q):
                i, m = q // NM, q % NM
                if m == 0:
                    pe.wait_ge(coef_in[i % 2], 64 * (i // 2 + 1))
                if q >= 2:
                    pe.wait_ge(picked, q - 1)
                for a in range(2):
                    ins = nc.tensor.matmul(pw[2 * (q % 2) + a][:], powers[:], coef[:, i % 2, 2 * m + a, :], start=True, stop=True)
                ins.then_inc(poly_made, 1)

            def gate_up(s, i, m):
                ps, made, read = ((pg[i % 2], gate_made, sg_ready), (pu[i % 2], up_made, h_ready))[m]
                if not (s.first() and i < 2):
                    pe.wait_ge(read, s.val(IB, i - 1))
                for hb in range(HB):
                    w_h, w_l = (t[:, m, hb, 128 * i:128 * i + 128] for t in (gu_hi, gu_lo))
                    nc.tensor.matmul(ps[:], w_h, x_hi[:, hb, :], start=hb == 0, stop=False)
                    nc.tensor.matmul(ps[:], w_h, x_lo[:, hb, :], start=False, stop=False)
                    ins = nc.tensor.matmul(ps[:], w_l, x_hi[:, hb, :], start=False, stop=hb == HB - 1)
                ins.then_inc(made, 1)

            def down(s, t):
                if not (s.first() and t < 2):
                    pe.wait_ge(down_read, s.val(NCH, t - 1))
                ps, tok = pw[t % 2], slice(CH * t, CH * t + CH)
                for i in range(IB):
                    if t == 0 and i in (0, IB - 2, IB - 1):
                        pe.wait_ge(it_ready, s.val(IB, max(i + 1, IB - 2)))
                    nc.tensor.matmul(ps[:], it_hi[:, i, tok], d_hi[:, i, :], start=i == 0, stop=False)
                    nc.tensor.matmul(ps[:], it_hi[:, i, tok], d_lo[:, i, :], start=False, stop=False)
                    ins = nc.tensor.matmul(ps[:], it_lo[:, i, tok], d_hi[:, i, :], start=False, stop=i == IB - 1)
                ins.then_inc(down_made, 1)

            s0 = At(None, 0)
            pe.wait_ge(powers_ready, 1)
            for q in range(NM):
                polynomial(q)
            pe.wait_ge(x_in, 32)
            for i in range(IB):
                for m in range(NM):
                    if NM * (i + 1) + m < NM * IB:
                        polynomial(NM * (i + 1) + m)
                    if m < 2:
                        pe.wait_ge(w_made, NM * i + m + 1)
                        gate_up(s0, i, m)
            pe.wait_ge(w_made, NM * IB)
            for t in range(NCH):
                down(s0, t)
            with pe.Fori(0, nst - 1) as r:
                s = At(r, 1)
                pe.wait_ge(x_in, s.val(32, 32))
                for i in range(IB):
                    gate_up(s, i, 0)
                    gate_up(s, i, 1)
                for t in range(NCH):
                    down(s, t)

        @block.scalar
        def _(act):
            sc = nc.scalar

            act.dma_start(pow_in[:], A.powers).then_inc(const_in, 16)
            act.dma_start(rows[:], A.rows).then_inc(const_in, 16)

            def first_cubic(q):
                act.wait_ge(poly_made, q + 1)
                if q >= 2:
                    act.wait_ge(w_made, q - 1)
                sc.activation(wt[:, q % 2, :], pw[2 * (q % 2)][:], ACT.Copy).then_inc(first_copied, 1)

            def weight_hi(q):
                act.wait_ge(picked, q + 1)
                i, m = q // NM, q % NM
                sc.activation(weight_block(0, m, i), by_block(wt[:, q % 2, :], m), ACT.Copy).then_inc(w_hi_made, 1)

            def gated(s, i):
                act.wait_ge(gate_made, s.val(IB, i + 1))
                if not (s.first() and i < 2):
                    act.wait_ge(h_ready, s.val(IB, i - 1))
                sc.activation(sg[:, i % 2, :], pg[i % 2][:], ACT.Silu, scale=1.0 / W_SCALE).then_inc(sg_ready, 1)

            def inter_hi(s, i):
                act.wait_ge(h_ready, s.val(IB, i + 1))
                sc.activation(it_hi[:, i, :], hh[:, i % 2, :], ACT.Copy).then_inc(hi_ready, 1)

            s0 = At(None, 0)

            def make(q):
                if q < NM * IB:
                    first_cubic(q)
                if 1 <= q <= NM * IB:
                    weight_hi(q - 1)

            for q in range(NM):
                make(q)
            for i in range(IB):
                make(NM * (i + 1))
                gated(s0, i)
                make(NM * (i + 1) + 1)
                inter_hi(s0, i)
                make(NM * (i + 1) + 2)
            with act.Fori(0, nst - 1) as r:
                s = At(r, 1)
                for i in range(IB):
                    gated(s, i)
                    inter_hi(s, i)

        @block.vector
        def _(dve):
            v = nc.vector

            def pick(q):
                dve.wait_ge(first_copied, q + 1)
                i = q // NM
                if q % NM == 0:
                    dve.wait_ge(coef_in[i % 2], 64 * (i // 2 + 1))
                    if i >= 2:
                        dve.wait_ge(picked, NM * (i - 1))
                    v.tensor_scalar(later[:, i % 2, :], knot[:, i % 2, :], rows[:, 0:1], None, ALU.is_le).then_inc(later_made, 1)
                    dve.wait_ge(later_made, i + 1)
                v.copy_predicated(wt[:, q % 2, :], later[:, i % 2, :], pw[2 * (q % 2) + 1][:]).then_inc(picked, 1)

            def weight_lo(q):
                dve.wait_ge(w_hi_made, q + 1)
                i, m = q // NM, q % NM
                v.tensor_tensor(weight_block(1, m, i), by_block(wt[:, q % 2, :], m), weight_block(0, m, i), ALU.subtract).then_inc(w_made, 1)

            def product(s, i):
                dve.wait_ge(sg_ready, s.val(IB, i + 1))
                dve.wait_ge(up_made, s.val(IB, i + 1))
                if not (s.first() and i < 2):
                    dve.wait_ge(it_ready, s.val(IB, i - 1))
                v.tensor_tensor(hh[:, i % 2, :], sg[:, i % 2, :], pu[i % 2][:], ALU.mult).then_inc(h_ready, 1)

            def inter_lo(s, i):
                dve.wait_ge(hi_ready, s.val(IB, i + 1))
                v.tensor_tensor(it_lo[:, i, :], hh[:, i % 2, :], it_hi[:, i, :], ALU.subtract).then_inc(it_ready, 1)

            def finish(s, t):
                dve.wait_ge(down_made, s.val(NCH, t + 1))
                dve.wait_ge(y_in[t % 2], s.val(16 * NCH // 2, 16 * (t // 2 + 1)))
                v.scalar_tensor_tensor(out=yr[:, t % 2, :], in0=pw[t % 2][:], scalar=W_SCALE ** -2, in1=yr[:, t % 2, :],
                                       op0=ALU.mult, op1=ALU.add).then_inc(down_read, 1)

            s0 = At(None, 0)
            dve.wait_ge(const_in, 32)
            v.tensor_copy(powers[:], pow_in[:]).then_inc(powers_ready, 1)

            def make(q):
                if q < NM * IB:
                    pick(q)
                if 1 <= q <= NM * IB:
                    weight_lo(q - 1)

            for q in range(NM):
                make(q)
            for i in range(IB):
                make(NM * (i + 1))
                make(NM * (i + 1) + 1)
                product(s0, i)
                make(NM * (i + 1) + 2)
                inter_lo(s0, i)
            for t in range(NCH):
                finish(s0, t)
            with dve.Fori(0, nst - 1) as r:
                s = At(r, 1)
                for i in range(IB):
                    product(s, i)
                    inter_lo(s, i)
                for t in range(NCH):
                    finish(s, t)


class Arrays:

    def __init__(self, aps, out, runs):
        self.x = aps["x"].rearrange("a t d -> (a t) d")
        self.out = out.rearrange("a t d -> (a t) d")
        self.Wq, self.Wk, self.Wv, self.Wg, self.Wo = (aps[n] for n in ("Wq", "Wk", "Wv", "Wg", "Wo"))
        self.Wa, self.Wb, self.A_log, self.dt_bias, self.nw = (aps[n] for n in ("Wa", "Wb", "A_log", "dt_bias", "nw"))
        self.cwq, self.cwk, self.cwv = (aps[n] for n in ("cwq", "cwk", "cwv"))
        self.gate_cp, self.up_cp, self.down_cp = (aps[n] for n in ("gate_cp", "up_cp", "down_cp"))
        self.frac, self.knot, self.rows, self.powers = (aps[n] for n in ("frac", "knot", "rows", "powers"))
        self.runs = runs


class Scratch:

    def __init__(self, dram):
        self.pad, self.ctrl = dram("pad", [3, NCP + 3]), dram("ctrl_cols", [3, 5, NCOL])
        self.coef = dram("coef_rows", [2, 4, 3, 2, NCOL], F16)
        self.y = dram("y_attn", [T_ALL, D])
        self.xh, self.xl = dram("xn_hi", [NST, 128, HB * ST], F16), dram("xn_lo", [NST, 128, HB * ST], F16)
        self.b, self.t, self.tt = (dram(n, [NSUB, NCH * NH, SUB, SUB]) for n in ("b_blocks", "t_blocks", "tt_blocks"))


class Persistent:

    def __init__(self, sb):
        self.w_hi, self.w_lo = sb("w_hi", [128, HB, WCOLS], F16), sb("w_lo", [128, HB, WCOLS], F16)
        self.wo_hi, self.wo_lo = sb("wo_hi", [128, NH, D], F16), sb("wo_lo", [128, NH, D], F16)
        self.wab_hi, self.wab_lo = sb("wab_hi", [128, HB, 2 * NH], F16), sb("wab_lo", [128, HB, 2 * NH], F16)
        self.taps, self.dtb, self.nega = sb("taps", [128, NBLK, TAPS]), sb("dtb", [128, NH]), sb("nega", [128, NH])
        self.ident, self.ones, self.after, self.upto, self.level32 = (
            sb(n, [128, 128]) for n in ("ident", "ones", "after", "upto", "level32"))
        self.pair = sb("pair", [128, 2])
        self.mhalf, self.phalf = sb("mhalf", [128, NCH * NH]), sb("phalf", [128, NCH * NH])
        self.S, self.halo, self.zeros = (
            sb("S", [128, NPAIR, DV]), sb("halo", [128, NBLK, TAPS - 1]), sb("zeros", [128, TAPS - 1]))


def build(nc, A, nst=NST):
    def dram(name, shape, dt=F32):
        return nc.dram_tensor(name, shape, dt, kind="Internal").ap()

    scr = Scratch(dram)
    with ExitStack() as ctx:
        def sb(name, shape, dt=F32):
            return ctx.enter_context(nc.sbuf_tensor(name, shape, dt))

        P = Persistent(sb)
        attend(nc, A, scr, P, nst)
    feed(nc, A, scr, nst)


_INS = dict(x="L0_attn_hidden_states", Wq="L0_attn_Wq", Wk="L0_attn_Wk", Wv="L0_attn_Wv", Wa="L0_attn_Wa",
            Wb="L0_attn_Wb", Wg="L0_attn_Wg", Wo="L0_attn_Wo", cwq="L0_attn_conv_wq", cwk="L0_attn_conv_wk",
            cwv="L0_attn_conv_wv", A_log="L0_attn_A_log", dt_bias="L0_attn_dt_bias", nw="L0_attn_norm_weight",
            gate_cp="L0_ffn_gate_cp", up_cp="L0_ffn_up_cp", down_cp="L0_ffn_down_cp")


def kernel(**inputs):
    import concourse.bacc as bacc
    from concourse.bass_utils import run_bass_kernel_spmd

    nc = bacc.Bacc("TRN2", target_bir_lowering=False, num_devices=1)
    arrays = {short: np.ascontiguousarray(inputs[name]) for short, name in _INS.items()}
    runs, arrays["frac"], arrays["knot"], arrays["rows"], arrays["powers"] = spline_shapes()
    aps = {n: nc.dram_tensor(f"in_{n}", a.shape, mybir.dt.from_np(a.dtype), kind="ExternalInput").ap()
           for n, a in arrays.items()}
    out = nc.dram_tensor("out", [1, T_ALL, D], F32, kind="ExternalOutput").ap()
    build(nc, Arrays(aps, out, runs))
    r = run_bass_kernel_spmd(nc, [{f"in_{n}": a for n, a in arrays.items()}], core_ids=[0])
    return r.results[0]["out"]
```

```python
import concourse.bass as bass
from concourse import mybir
from contextlib import ExitStack
import numpy as np

F32 = mybir.dt.float32
F16 = mybir.dt.float16
BF16 = mybir.dt.bfloat16
U8 = mybir.dt.uint8
ALU = mybir.AluOpType
ACT = mybir.ActivationFunctionType

T_ALL, D = 2048, 512
HB = D // 128
ST = 512
NST = T_ALL // ST
CH = 128
NCH = ST // CH
NH, DK, DV = 6, 64, 128
NPAIR = NH // 2
KD, VD = NH * DK, NH * DV
TAPS = 4
NQK = 2 * KD // 128
NV = VD // 128
NBLK = NQK + NV
WCOLS = 2 * KD + 2 * VD
EPS = 1e-5
INTER = 2048
IB = INTER // 128
SUB = 32
NSUB = CH // SUB
NINST = NSUB * NCH * NH
W_SCALE = 64.0
NCP = max(16, int(INTER * D / 128.9))
NCOL = INTER * D // 128
NCR = NCOL // 128
MID = 64
NW = 8
NF = 8 + NW
NP = IB // 2
ROW = HB * 3 * 2 * 4
HALF = NH // 2 * 128
NSTG = 4
KQ_HEADS = ((0, 2), (1, 3), (4,), (5,))


def spline_shapes():
    n = NCOL * 128
    t = np.linspace(0.0, NCP - 1.0, n, dtype=np.float64)
    i = np.clip(np.floor(t).astype(np.int64), 0, NCP - 2)
    first = i.reshape(NCOL, 128)[:, 0]
    knot = (i.reshape(NCOL, 128) == first[:, None]).sum(axis=1)
    step = (NCP - 1.0) / (n - 1)
    start = t.reshape(NCOL, 128)[:, 0] - first
    frac = (start + MID * step).astype(np.float32).reshape(128, NCR)
    powers = np.stack([((np.arange(128) - MID) * step) ** k for k in range(4)])
    hi = powers.astype(np.float16)
    lo = (powers - hi).astype(np.float16)
    shift = np.arange(NCOL) - first
    cuts = [0] + [int(c) for c in np.nonzero(np.diff(shift))[0] + 1] + [NCOL]
    runs = [(a, b, int(first[a])) for a, b in zip(cuts[:-1], cuts[1:])]
    later = (np.arange(128)[:, None] >= knot[None, :]).astype(np.uint8).view(np.uint32)
    consts = dict(frac=frac, later=later, powers=np.concatenate([hi, lo, hi]).astype(np.float32))
    consts.update(group_shapes(knot, start, powers, step))
    return runs, consts


def group_shapes(knot, start, powers, step):
    kn = knot.reshape(INTER, HB)
    member = np.argsort(-start.reshape(INTER, HB)[:, 0], kind="stable").reshape(IB, 128)
    basis = np.zeros((128, HB, IB, HB, NF))
    sample, turn = np.zeros((IB, HB, NW)), np.zeros((IB, HB))
    for g in range(IB):
        for b in range(HB):
            k = kn[member[g], b]
            if k.max() - k.min() <= NW:
                low, high = (0, k.min()), (k.min() + NW, 128)
                single = range(k.min(), min(k.min() + NW, 128))
            else:
                low, high = (0, 0), (k[k < MID].max(), k[k >= MID].min())
                single = [*range(high[0]), *range(high[1], 128)]
            assert len(single) <= NW
            basis[slice(*low), b, g, b, 0:4] = powers[:, slice(*low)].T
            basis[slice(*high), b, g, b, 4:8] = powers[:, slice(*high)].T
            for e, j in enumerate(single):
                basis[j, b, g, b, 8 + e], sample[g, b, e] = 1.0, j
            turn[g, b] = high[0]
    basis = basis.reshape(128, HB, NP, 128).transpose(0, 2, 1, 3).reshape(128, NP * HB * 128) * W_SCALE
    hi = basis.astype(np.float16)
    tables = np.concatenate([sample.ravel(), ((sample - MID) * step).ravel(), turn.ravel()])
    return dict(basis_hi=hi, basis_lo=(basis - hi).astype(np.float16), tables=tables.astype(np.float32),
                gknot=np.ascontiguousarray(kn[member].transpose(1, 0, 2)).astype(np.float32).reshape(128, IB * HB),
                member=np.ascontiguousarray(member.T).astype(np.uint32))


class At:

    def __init__(self, reg, off):
        self.reg, self.off = reg, off

    def val(self, per, n):
        assert self.first() or self.off * per + n > 0
        return self.off * per + n if self.reg is None else self.reg * per + (self.off * per + n)

    def idx(self):
        return self.off if self.reg is None else self.reg + self.off

    def first(self):
        return self.reg is None and self.off == 0


class Steps:

    def __init__(self, per):
        self.per, self.n = per, 0

    def start(self, at):
        assert self.n in (0, self.per), (self.n, self.per)
        self.at, self.n = at, 0

    def next(self):
        self.n += 1
        return self.at.val(self.per, self.n)


def bank_uses():
    order = []
    ring = [("ln", t) for t in range(NCH)]
    gates = [("gate", c, h) for c in range(NCH) for h in range(2)]
    ring += [("blk", n) for n in range(NQK)] + gates[:2] + [("ktr", c) for c in range(NCH)]
    for n in range(NV):
        ring += [("blk", NQK + n)] + gates[2 + n:3 + n]
    ring += [("vtr", n) for n in range(NV)]
    order += [(i % 2, u) for i, u in enumerate(ring)] + [(2, ("sums",)), (4, ("ab",))]
    for c in range(NCH):
        order += [(2, ("D", c, 0)), (3, ("D", c, 1))] + [(4 + p, ("KQ", c, p)) for p in range(len(KQ_HEADS))]
    order += [(2, ("qsums",))]
    for k in range(NCH + 3):
        if k < NCH:
            order += [(2, ("X", k, 0)), (3, ("X", k, 1))]
        if 0 <= k - 1 < NCH:
            order += [(4, ("Y", k - 1)), (5, ("Z", k - 1, 0)), (6, ("Z", k - 1, 1))]
        if 0 <= k - 2 < NCH:
            order += [(7, ("X2", k - 2))]
        if 0 <= k - 3 < NCH:
            order += [(4, ("Z2", k - 3))]
    for c in range(NCH + 2):
        if c < NCH:
            order += [(2, ("KS", c, 0)), (3, ("KS", c, 1))]
        if 2 <= c <= NCH:
            order += [(7, ("WO", c - 2))]
        if c < NCH:
            order += [(4, ("U", c, 0)), (5, ("U", c, 1)), (6, ("QS", c, 0)), (7, ("QS", c, 1))]
        if 1 <= c <= NCH:
            order += [(5, ("OT", c - 1, 0)), (6, ("OT", c - 1, 1))]
        if c < NCH:
            order += [(4, ("dS", c)), (2, ("AU", c, 0)), (3, ("AU", c, 1))]
    per, table = [0] * 8, {}
    for bank, u in order:
        table[u] = (bank, per[bank])
        per[bank] += 1
    return table, per


class Preparation:

    def __init__(self, nc, A, scr, P, sb, sem, stage, spline, split):
        self.nc, self.A, self.scr, self.P = nc, A, scr, P
        self.stage = stage
        self.ab_stage = sb("ab_stage", [128, HB, 2 * NH])
        self.nw, self.nw_s = sb("nw", [128, 1]), sb("nw_s", [128, 1])
        n, k = 3 * NCR, 0

        def part(width):
            nonlocal k
            k += width
            return spline[:, k - width:k]
        self.ctrl = part(5 * n).rearrange("p (m k r) -> p m k r", m=3, k=5)
        self.co = part(6 * n).rearrange("p (k m a r) -> p k m a r", k=3, m=3, a=2)
        self.t1, self.t2 = (part(2 * n).rearrange("p (m a r) -> p m a r", m=3, a=2) for _ in range(2))
        self.frac = part(2 * NCR).rearrange("p (a r) -> p a r", a=2)
        self.rows = split[:, 0:8 * n]
        self.dcf = self.rows.rearrange("p (r m a k) -> p k m a r", k=4, m=3, a=2)
        self.dsp = split[:, 8 * n:8 * n + 8 * NCR].bitcast(F16).rearrange("p (h a k r) -> p h (a k) r", h=2, k=4, a=2)
        self.staged = [sem(f"staged{i}") for i in range(NSTG)]
        self.ab_in, self.small_in, self.hi_done, self.lo_done = sem("ab_in"), sem("small_in"), sem("hi_done"), sem("lo_done")
        self.const_made, self.padded, self.gathered = sem("const_made"), sem("padded"), sem("gathered")
        self.ctrl_in, self.sp_step, self.coef_out = sem("ctrl_in"), sem("sp_step"), sem("coef_out")
        self.nw_ready, self.nega_ready, self.coef_hi, self.coef_lo = (
            sem("nw_ready"), sem("nega_ready"), sem("coef_hi"), sem("coef_lo"))
        self.cleared = sem("cleared")
        self.pieces = [(A.Wk, 0, 0), (A.Wq, 0, KD)]
        self.pieces += [(A.Wg, 384 * i, 2 * KD + VD + 384 * i) for i in range(2)]
        self.pieces += [(A.Wv, 384 * i, 2 * KD + 384 * i) for i in range(2)]

    def parts(self, i):
        P = self.P
        if i < len(self.pieces):
            col = self.pieces[i][2]
            return (self.stage[i % NSTG].rearrange("p (b n) -> p b n", b=HB),
                    P.w_hi[:, :, col:col + 384], P.w_lo[:, :, col:col + 384])
        h0 = 3 * (i - len(self.pieces))
        return (self.stage[i % NSTG].rearrange("p (h n) -> p h n", h=3),
                P.wo_hi[:, h0:h0 + 3, :], P.wo_lo[:, h0:h0 + 3, :])

    @staticmethod
    def count(i):
        return i + 1 if i < 2 else i + 2

    def load_piece(self, eng, i):
        if i >= NSTG:
            eng.wait_ge(self.lo_done, self.count(i - NSTG))
        if i < len(self.pieces):
            w, c0, _ = self.pieces[i]
            src = w.rearrange("(b p) n -> p b n", p=128)[:, :, c0:c0 + 384]
        else:
            h0 = 3 * (i - len(self.pieces))
            src = self.A.Wo.rearrange("(h p) n -> p h n", p=128)[:, h0:h0 + 3, :]
        eng.dma_start(self.parts(i)[0], src).then_inc(self.staged[i % NSTG], 16)

    def load_decay_weights(self, sp):
        sp.dma_start(self.ab_stage[:, :, 0:NH], self.A.Wa.rearrange("(b p) n -> p b n", p=128)).then_inc(self.ab_in, 16)
        sp.dma_start(self.ab_stage[:, :, NH:2 * NH], self.A.Wb.rearrange("(b p) n -> p b n", p=128)).then_inc(self.ab_in, 16)

    def load_small(self, sp):
        A, P, small_in = self.A, self.P, self.small_in
        sp.dma_start(P.dtb[:], A.dt_bias.partition_broadcast(128)).then_inc(small_in, 16)
        sp.dma_start(P.nega[:], A.A_log.partition_broadcast(128)).then_inc(small_in, 16)
        for b in range(NPAIR):
            for which, w in enumerate((A.cwk, A.cwq)):
                sp.dma_start(P.taps[:, NPAIR * which + b, :], w[128 * b:128 * b + 128, :]).then_inc(small_in, 16)
        sp.dma_start(P.taps[:, NQK:NBLK, :], A.cwv.rearrange("(b p) t -> p b t", p=128)).then_inc(small_in, 16)
        sp.dma_start(self.nw[:], A.nw.rearrange("(p a) -> p a", a=1)).then_inc(small_in, 16)
        sp.dma_start(self.frac[:, 0, :], A.frac).then_inc(small_in, 16)

    SMALL = 16 * (2 + 2 * NPAIR + 3)

    def pad_control_points(self, sp):
        A, scr, padded = self.A, self.scr, self.padded
        for m, cp in enumerate((A.gate_cp, A.up_cp, A.down_cp)):
            row = cp.rearrange("(a n) -> a n", a=1)
            sp.dma_start(scr.pad[m:m + 1, 1:1 + NCP], row).then_inc(padded, 16)
            sp.dma_start(scr.pad[m:m + 1, 0:1], row[:, 0:1]).then_inc(padded, 16)
            for e in range(2):
                sp.dma_start(scr.pad[m:m + 1, 1 + NCP + e:2 + NCP + e], row[:, NCP - 1:NCP]).then_inc(padded, 16)

    def gather_control_points(self, sp):
        scr, runs = self.scr, self.A.runs
        sp.wait_ge(self.padded, 12 * 16)
        for c0, c1, j0 in runs:
            src = bass.AP(tensor=scr.pad.tensor, offset=scr.pad.offset + j0,
                          ap=[[NCP + 3, 3], [1, 5], [1, c1 - c0]])
            sp.dma_start(scr.ctrl[:, :, c0:c1], src, allow_slow_non_contiguous=c1 - c0 == 1).then_inc(self.gathered, 16)
        sp.wait_ge(self.gathered, 16 * len(runs))
        for m in range(3):
            sp.dma_start(self.ctrl[:, m, :, :], scr.ctrl[m].rearrange("k (q r) -> q k r", r=NCR)).then_inc(self.ctrl_in, 16)

    def store_coefficients(self, sp):
        sp.wait_ge(self.coef_lo, 1)
        sp.dma_start(self.scr.rows.rearrange("(q i) n -> q (i n)", q=128), self.rows).then_inc(self.coef_out, 16)
        for a in range(2):
            for part in range(2):
                sp.dma_start(self.scr.coef[part, :, a, :].rearrange("k (q r) -> q k r", r=NCR),
                             self.dsp[:, part, 4 * a:4 * a + 4, :]).then_inc(self.coef_out, 16)

    COEF_OUT = 16 * (1 + 4)

    def decay_weights_high(self, act):
        act.wait_ge(self.ab_in, 32)
        self.nc.scalar.activation(self.P.wab_hi[:], self.ab_stage[:], ACT.Copy, scale=W_SCALE).then_inc(self.hi_done, 1)

    def piece_high(self, act, i):
        act.wait_ge(self.staged[i % NSTG], 16 * (i // NSTG + 1))
        src, hi, _ = self.parts(i)
        if i == len(self.pieces):
            act.wait_ge(self.small_in, self.SMALL)
            self.nc.scalar.activation(self.nw_s[:], self.nw[:], ACT.Copy, scale=W_SCALE).then_inc(self.nw_ready, 1)
            act.wait_ge(self.nw_ready, 1)
        scale = W_SCALE if i < len(self.pieces) else self.nw_s[:]
        self.nc.scalar.activation(hi, src, ACT.Copy, scale=scale).then_inc(self.hi_done, 1)

    def decay_rates(self, act):
        P = self.P
        act.wait_ge(self.small_in, self.SMALL)
        self.nc.scalar.activation(P.nega[:], P.nega[:], ACT.Exp).then_inc(self.nega_ready, 1)
        act.wait_ge(self.nega_ready, 1)
        self.nc.scalar.activation(P.nega[:], P.nega[:], ACT.Copy, scale=-1.0).then_inc(self.nega_ready, 1)

    def decay_weights_low(self, dve):
        dve.wait_ge(self.hi_done, 3)
        self.nc.vector.scalar_tensor_tensor(out=self.P.wab_lo[:], in0=self.ab_stage[:], scalar=W_SCALE, in1=self.P.wab_hi[:],
                                            op0=ALU.mult, op1=ALU.subtract).then_inc(self.lo_done, 1)

    def piece_low(self, dve, i):
        dve.wait_ge(self.hi_done, self.count(i))
        src, hi, lo = self.parts(i)
        scale = W_SCALE if i < len(self.pieces) else self.nw_s[:]
        self.nc.vector.scalar_tensor_tensor(out=lo, in0=src, scalar=scale, in1=hi,
                                            op0=ALU.mult, op1=ALU.subtract).then_inc(self.lo_done, 1)

    def spline_coefficients(self, dve):
        nc, ctrl, co, t1, t2, dcf, dsp = self.nc, self.ctrl, self.co, self.t1, self.t2, self.dcf, self.dsp
        step = [0]

        def link(ins):
            step[0] += 1
            ins.then_inc(self.sp_step, 1)
            dve.wait_ge(self.sp_step, step[0])

        dve.wait_ge(self.small_in, self.SMALL)
        link(nc.vector.tensor_scalar(self.frac[:, 1, :], self.frac[:, 0, :], -1.0, None, ALU.add))
        dve.wait_ge(self.ctrl_in, 48)
        stt = nc.vector.scalar_tensor_tensor
        p0, p1, p2, p3 = (ctrl[:, :, k:k + 2, :] for k in range(4))
        u = self.frac.unsqueeze(1).broadcast_to([128, 3, 2, NCR])
        c1, c2, c3 = (co[:, k, :, :, :] for k in range(3))
        d0, d1, d2, d3 = (dcf[:, k, :, :, :] for k in range(4))
        link(nc.vector.tensor_tensor(t1, p1, p2, ALU.subtract))
        link(nc.vector.tensor_tensor(t2, p3, p0, ALU.subtract))
        link(nc.vector.tensor_scalar(t2, t2, 0.5, None, ALU.mult))
        link(stt(out=c3, in0=t1, scalar=1.5, in1=t2, op0=ALU.mult, op1=ALU.add))
        link(nc.vector.tensor_tensor(t2, p2, p0, ALU.subtract))
        link(nc.vector.tensor_scalar(c1, t2, 0.5, None, ALU.mult))
        link(stt(out=t1, in0=p1, scalar=-2.5, in1=p0, op0=ALU.mult, op1=ALU.add))
        link(stt(out=t1, in0=p2, scalar=2.0, in1=t1, op0=ALU.mult, op1=ALU.add))
        link(stt(out=c2, in0=p3, scalar=-0.5, in1=t1, op0=ALU.mult, op1=ALU.add))
        link(nc.vector.tensor_tensor(t1, c3, u, ALU.mult))
        link(stt(out=d2, in0=t1, scalar=3.0, in1=c2, op0=ALU.mult, op1=ALU.add))
        link(nc.vector.tensor_tensor(t2, d2, c2, ALU.add))
        link(nc.vector.tensor_tensor(t2, t2, u, ALU.mult))
        link(nc.vector.tensor_tensor(d1, t2, c1, ALU.add))
        link(nc.vector.tensor_tensor(t1, t1, c2, ALU.add))
        link(nc.vector.tensor_tensor(t1, t1, u, ALU.mult))
        link(nc.vector.tensor_tensor(t1, t1, c1, ALU.add))
        link(nc.vector.tensor_copy(d3, c3))
        link(nc.vector.tensor_tensor(t1, t1, u, ALU.mult))
        link(nc.vector.tensor_tensor(d0, t1, p1, ALU.add))
        exact, hi, lo = self.rows.rearrange("p (r m x) -> p m x r", m=3, x=8)[:, 2], dsp[:, 0], dsp[:, 1]
        nc.vector.tensor_scalar(hi, exact, W_SCALE, None, ALU.mult).then_inc(self.coef_hi, 1)
        dve.wait_ge(self.coef_hi, 1)
        stt(out=lo, in0=exact, scalar=W_SCALE, in1=hi, op0=ALU.mult, op1=ALU.subtract).then_inc(self.coef_lo, 1)

    def constants(self, pool):
        P, const_made = self.P, self.const_made
        n = [0]

        def made(ins):
            n[0] += 1
            ins.then_inc(const_made, 1)
            pool.wait_ge(const_made, n[0])

        g = self.nc.gpsimd
        made(g.memset(P.ident[:], 0.0))
        made(g.affine_select(out=P.ident[:], in_=P.ident[:], compare_op=ALU.not_equal, fill=1.0, base=0,
                             pattern=[[-1, 128]], channel_multiplier=1))
        made(g.memset(P.ones[:], 1.0))
        made(g.affine_select(out=P.after[:], in_=P.ones[:], compare_op=ALU.is_gt, fill=0.0, base=0,
                             pattern=[[-1, 128]], channel_multiplier=1))
        made(g.affine_select(out=P.upto[:], in_=P.ones[:], compare_op=ALU.is_ge, fill=0.0, base=0,
                             pattern=[[1, 128]], channel_multiplier=-1))
        made(g.memset(P.level32[:], 0.0))
        for b in (1, 3):
            made(g.memset(P.level32[SUB * b:SUB * b + SUB, SUB * (b - 1):SUB * b], 1.0))
        made(g.memset(P.pair[:], 0.0))
        for b in range(2):
            made(g.memset(P.pair[DK * b:DK * b + DK, b:b + 1], 1.0))
        made(g.memset(P.mhalf[:], -0.5))
        made(g.memset(P.phalf[:], 0.5))
        made(g.memset(P.S[:], 0.0))
        made(g.memset(P.halo[:], 0.0))
        made(g.memset(P.zeros[:], 0.0))
        assert n[0] == CONSTANTS


def attend(nc, A, scr, P, nst=NST):
    uses, per = bank_uses()
    with ExitStack() as ctx:
        def sb(name, shape, dt=F32):
            return ctx.enter_context(nc.sbuf_tensor(name, shape, dt))

        def sem(name):
            return ctx.enter_context(nc.semaphore(name))

        NCHH = NCH * NH
        xb = sb("xb", [128, NCH, D])
        x_hi = sb("x_hi", [128, HB, ST], F16)
        x_lo = sb("x_lo", [128, HB, ST], F16)
        raw = sb("raw", [128, 3, ST + TAPS - 1])
        cv = sb("cv", [128, 2, ST])
        kq = sb("kq", [128, NPAIR, 2, ST])
        vT = sb("vT", [128, 3, ST])
        V = sb("V", [128, NCH, NH, DV])
        gate = sb("gate", [128, NCH, VD])
        ktok = sb("ktok", [128, NCH, KD])
        BA = sb("BA", [128, 2, NCHH, CH])
        eg = sb("eg", [128, 2, NH, CH])
        Tbd = sb("Tbd", [128, NCHH, CH])
        W = sb("W", [128, NCHH, CH])
        T1 = sb("T1", [64, 2, NH, 64])
        X2s = sb("X2s", [128, 2, NH, 64])
        og_hi = sb("og_hi", [128, NH, CH], F16)
        og_lo = sb("og_lo", [128, NH, CH], F16)
        xr = sb("xr", [128, 2, D])
        junk = sb("junk", [128, NH, DV], BF16)
        bin_ = sb("bin", [NINST, SUB * SUB])
        tin = sb("tin", [NINST, SUB * SUB])
        tmp = sb("tmp", [NINST, 5 * SUB * SUB // 16])
        mv = sb("mv", [128, NCH, 2])
        stats = sb("stats", [128, NCH, 6])
        rstd = sb("rstd", [128, NCH])
        ln_d = sb("ln_d", [128, NCH])
        ab = sb("ab", [128, NCH, 2 * NH])
        z, az, nb, e1, ln1, beta, g = (sb(n, [128, NCH, NH]) for n in ("z", "az", "nb", "e1", "ln1", "beta", "g"))
        eb = sb("eb", [128, NCH, NH])
        sums = sb("sums", [128, 4 * NCHH])
        rk2, cj, eq, nk, gam, ngam, suf, ks = (sb(n, [128, NCHH]) for n in
                                               ("rk2", "cj", "eq", "nk", "gam", "ngam", "suf", "ks"))
        gC = sb("gC", [128, NCH, NPAIR])
        ss = sb("ss", [128, 2, NH])
        t6 = sb("t6", [128, 2, NH])
        rn = sb("rn", [128, 2, NH])
        rb = BA[:, 0, :, :]
        Rr, U = rb[:, 0:NH, :], rb[:, NH:2 * NH, :]
        O = rb[:, 2 * NH:4 * NH, :].rearrange("p (r h) d -> p r h d", r=2)
        sq = BA[:, 1, :, :].rearrange("p (n a) c -> p n (a c)", n=NQK)
        E, gm = eg[:, 0], eg[:, 1]
        tap_products = (eg[:].rearrange("p a h c -> p (a h c)").rearrange("p (t n) -> p t n", t=TAPS - 1), xb[:, 0:TAPS - 1, :])
        bank = [ctx.enter_context(nc.psum_tensor(f"bank{i}", [128, 512], F32)) for i in range(8)]
        full = [sem(f"full{i}") for i in range(8)]
        done = [sem(f"done{i}") for i in range(8)]
        x_in, ln_step, ln_stats, ln_rstd, xn_ready = sem("x_in"), sem("ln_step"), sem("ln_stats"), sem("ln_rstd"), sem("xn_ready")
        xhi_ready, spilled = sem("xhi_ready"), sem("spilled")
        ab_ready, ab_exp, ab_ln, g_ready = sem("ab_ready"), sem("ab_exp"), sem("ab_ln"), sem("g_ready")
        dve_step, t32_step = sem("dve_step"), sem("t32_step")
        halo_used, raw_ready, cv_ready, silu_done, sq_ready = (
            sem("halo_used"), sem("raw_ready"), sem("cv_ready"), sem("silu_done"), sem("sq_ready"))
        dec_ready, nk_ready, ks_ready = sem("dec_ready"), sem("nk_ready"), sem("ks_ready")
        gm_ready, a_masked = sem("gm_ready"), sem("a_masked")
        taps_ready, tap_step, v_conv = sem("taps_ready"), sem("tap_step"), sem("v_conv")
        b_out, b_in, t_out, tt_out, tbd_in, w_in = (sem(n) for n in ("b_out", "b_in", "t_out", "tt_out", "tbd_in", "w_in"))
        ss_ready, t6_ready, rn_ready, og_ready, oghi_ready = (
            sem("ss_ready"), sem("t6_ready"), sem("rn_ready"), sem("og_ready"), sem("oghi_ready"))
        xr_in = [sem(f"xr_in{i}") for i in range(2)]
        y_out = [sem(f"y_out{i}") for i in range(2)]
        prep = Preparation(nc, A, scr, P, sb, sem,
                           [BA[:, 0, NCHH // 2 * i:NCHH // 2 * (i + 1), :].rearrange("p i c -> p (i c)") for i in range(2)]
                           + [V[:, NCH // 2 * i:NCH // 2 * (i + 1), :, :].rearrange("p c h d -> p (c h d)") for i in range(2)],
                           Tbd[:].rearrange("p i c -> p (i c)"), W[:].rearrange("p i c -> p (i c)"))
        late_full, late_done = sem("late_full"), sem("late_done")
        LATE_BANK = uses[("X2", 0)][0]
        block = ctx.enter_context(nc.Block())

        def square_of(n):
            return sq[:, n, :] if n < NPAIR else xb[:, n - NPAIR, :]

        x_v = A.x.rearrange("(s t p) d -> s p t d", t=NCH, p=128)
        y_v = scr.y.rearrange("(s t p) d -> s t p d", t=NCH, p=128)
        xr_v = A.x.rearrange("(s t p) d -> s t p d", t=NCH, p=128)

        def filled(eng, u, s):
            b, n = uses[u]
            eng.wait_ge(full[b], s.val(per[b], n + 1))

        def ready(eng, u, s):
            b, n = uses[u]
            eng.wait_ge(done[b], s.val(per[b], n + 1))

        def out_of(u):
            return bank[uses[u][0]], done[uses[u][0]]

        def ch(c, h):
            return NH * c + h

        @block.tensor
        def _(pe):
            def claim(u, s):
                b, n = uses[u]
                if not (s.first() and n == 0):
                    pe.wait_ge(done[b], s.val(per[b], n))
                return bank[b], full[b]

            def split_product(out, w_hi, w_lo, x_hi_, x_lo_, swap, first=True, last=True):
                todo = ((w_hi, x_hi_), (w_hi, x_lo_), (w_lo, x_hi_))
                for i, (w, xx) in enumerate(todo):
                    a, b = (xx, w) if swap else (w, xx)
                    ins = nc.tensor.matmul(out, a, b, start=first and i == 0, stop=last and i == 2)
                return ins

            def ln_transposes(s, tiles):
                for t in tiles:
                    pe.wait_ge(xn_ready, s.val(NCH, t + 1))
                    ps, f = claim(("ln", t), s)
                    for hb in range(HB):
                        ins = nc.tensor.transpose(ps[:, 128 * hb:128 * hb + 128], xb[:, t, 128 * hb:128 * hb + 128], P.ident[:])
                    ins.then_inc(f, 1)

            def decay_products(s):
                ps, f = claim(("ab",), s)
                for c in range(NCH):
                    for hb in range(HB):
                        ins = split_product(ps[:, 2 * NH * c:2 * NH * (c + 1)], P.wab_hi[:, hb, :], P.wab_lo[:, hb, :],
                                            x_hi[:, hb, CH * c:CH * c + CH], x_lo[:, hb, CH * c:CH * c + CH], True,
                                            hb == 0, hb == HB - 1)
                ins.then_inc(f, 1)

            def gate_products(s, c, h):
                ps, f = claim(("gate", c, h), s)
                col = 2 * KD + VD + 384 * h
                for hb in range(HB):
                    ins = split_product(ps[:, 0:384], P.w_hi[:, hb, col:col + 384], P.w_lo[:, hb, col:col + 384],
                                        x_hi[:, hb, CH * c:CH * c + CH], x_lo[:, hb, CH * c:CH * c + CH], True,
                                        hb == 0, hb == HB - 1)
                ins.then_inc(f, 1)

            def block_products(s, n):
                ps, f = claim(("blk", n), s)
                if n == 0:
                    for t in (NCH - 2, NCH - 1):
                        ready(pe, ("ln", t), s)
                for hb in range(HB):
                    ins = split_product(ps[:], P.w_hi[:, hb, 128 * n:128 * n + 128], P.w_lo[:, hb, 128 * n:128 * n + 128],
                                        x_hi[:, hb, :], x_lo[:, hb, :], False, hb == 0, hb == HB - 1)
                ins.then_inc(f, 1)

            def norms(ps, col, s, which):
                for n in range(NPAIR * which, NPAIR * which + NPAIR):
                    pe.wait_ge(sq_ready, s.val(NQK, n + 1))
                    for c in range(NCH):
                        at = col + NH * c + 2 * (n % NPAIR)
                        ins = nc.tensor.matmul(ps[:, at:at + 2], square_of(n)[:, CH * c:CH * c + CH], P.pair[:], start=True, stop=True)
                return ins

            def token_sums(s):
                ps, f = claim(("sums",), s)
                pe.wait_ge(g_ready, s.val(1, 1))
                gv = g[:].rearrange("p c h -> p (c h)")
                for i, mask in enumerate((P.upto, P.after, P.ones)):
                    nc.tensor.matmul(ps[:, NCHH * i:NCHH * (i + 1)], mask[:], gv, start=True, stop=True)
                norms(ps, 3 * NCHH, s, 0).then_inc(f, 1)

            def query_sums(s):
                ps, f = claim(("qsums",), s)
                norms(ps, 0, s, 1).then_inc(f, 1)

            def k_transposes(s, c):
                ps, f = claim(("ktr", c), s)
                for b in range(NPAIR):
                    ins = nc.tensor.transpose(ps[:, 128 * b:128 * b + 128], kq[:, b, 0, CH * c:CH * c + CH], P.ident[:])
                ins.then_inc(f, 1)

            def chunk_scores(s, c):
                pe.wait_ge(gm_ready, s.val(NCH, c + 1))
                for hf in range(2):
                    ps, f = claim(("D", c, hf), s)
                    nc.tensor.matmul(ps[:, 0:HALF], P.after[:], gm[:, hf:NH:2, :], start=True, stop=True).then_inc(f, 1)
                if c == 0:
                    pe.wait_ge(silu_done, s.val(NBLK, NQK))
                for p, heads in enumerate(KQ_HEADS):
                    ps, f = claim(("KQ", c, p), s)
                    for k, h in enumerate(heads):
                        rows = slice(DK * (h % 2), DK * (h % 2) + DK)
                        ins = nc.tensor.matmul(ps[:, 256 * k:256 * k + 256], kq[rows, h // 2, 0, CH * c:CH * c + CH],
                                               kq[rows, h // 2, :, CH * c:CH * c + CH], start=True, stop=True)
                    ins.then_inc(f, 1)

            def v_transposes(s, n):
                ps, f = claim(("vtr", n), s)
                pe.wait_ge(silu_done, s.val(NBLK, NQK + n + 1))
                for c in range(NCH):
                    ins = nc.tensor.transpose(ps[:, 128 * c:128 * c + 128], vT[:, n % 3, CH * c:CH * c + CH], P.ident[:])
                ins.then_inc(f, 1)

            def solve(s):
                pe.wait_ge(tbd_in, s.val(16 * NSUB, 16 * NSUB))
                for k in range(NCH + 3):
                    if 1 <= k < NV - 1:
                        v_transposes(s, k + 1)
                    if k < NCH:
                        for hf in range(2):
                            ps, f = claim(("X", k, hf), s)
                            for h in range(3):
                                i = ch(k, 2 * h + hf)
                                ins = nc.tensor.matmul(ps[:, 128 * h:128 * h + 128], BA[:, 0, i, :], Tbd[:, i, :], start=True, stop=True)
                            ins.then_inc(f, 1)
                    c = k - 1
                    if 0 <= c < NCH:
                        if c == 0:
                            pe.wait_ge(w_in, s.val(16 * NSUB, 16 * NSUB))
                        ps, f = claim(("Y", c), s)
                        for hf in range(2):
                            ready(pe, ("X", c, hf), s)
                        for h in range(NH):
                            ins = nc.tensor.matmul(ps[0:64, 64 * h:64 * h + 64], W[:, ch(c, h), 0:64],
                                                   eg[:, c % 2, h, 0:64], start=True, stop=True)
                        ins.then_inc(f, 1)
                        for hf in range(2):
                            ps, f = claim(("Z", c, hf), s)
                            for h in range(3):
                                i = 2 * h + hf
                                ins = nc.tensor.matmul(ps[:, 128 * h:128 * h + 128], eg[:, c % 2, i, :], W[:, ch(c, i), :], start=True, stop=True)
                            ins.then_inc(f, 1)
                    c = k - 2
                    if 0 <= c < NCH:
                        if c == 0 and not s.first():
                            pe.wait_ge(late_done, s.val(1, 0))
                        ps, f = claim(("X2", c), s)
                        ready(pe, ("Y", c), s)
                        for h in range(NH):
                            ins = nc.tensor.matmul(ps[:, 64 * h:64 * h + 64], BA[0:64, 0, ch(c, h), :],
                                                   T1[:, c % 2, h, :], start=True, stop=True)
                        ins.then_inc(f, 1)
                    c = k - 3
                    if 0 <= c < NCH:
                        ps, f = claim(("Z2", c), s)
                        ready(pe, ("X2", c), s)
                        for hf in range(2):
                            ready(pe, ("Z", c, hf), s)
                        for h in range(NH):
                            ins = nc.tensor.matmul(ps[0:64, 64 * h:64 * h + 64], X2s[:, c % 2, h, :],
                                                   W[:, ch(c, h), 64:128], start=True, stop=True)
                        ins.then_inc(f, 1)

            def state_product(s, c, name, which, hf):
                ps, f = claim((name, c, hf), s)
                for h in range(hf, NH, 2):
                    rows = slice(DK * (h % 2), DK * (h % 2) + DK)
                    ins = nc.tensor.matmul(ps[:, 128 * (h // 2):128 * (h // 2) + 128], kq[rows, h // 2, which, CH * c:CH * c + CH],
                                           P.S[rows, h // 2, :], start=True, stop=True)
                ins.then_inc(f, 1)

            def recur(s, c):
                if c >= 1:
                    ready(pe, ("dS", c - 1), s)
                for hf in range(2):
                    state_product(s, c, "KS", 0, hf)
                if c >= 2:
                    project_out(s, c - 2)
                ready(pe, ("Z2", c), s)
                for hf in range(2):
                    ps, f = claim(("U", c, hf), s)
                    ready(pe, ("KS", c, hf), s)
                    for h in range(hf, NH, 2):
                        ins = nc.tensor.matmul(ps[:, 128 * (h // 2):128 * (h // 2) + 128], W[:, ch(c, h), :], Rr[:, h, :], start=True, stop=True)
                    ins.then_inc(f, 1)
                for hf in range(2):
                    state_product(s, c, "QS", 1, hf)
                if c >= 1:
                    transpose_out(s, c - 1)
                ps, f = claim(("dS", c), s)
                for hf in range(2):
                    ready(pe, ("U", c, hf), s)
                for h in range(NH):
                    r = DK * (h % 2)
                    ins = nc.tensor.matmul(ps[r:r + DK, 128 * (h // 2):128 * (h // 2) + 128], ktok[:, c, DK * h:DK * h + DK],
                                           U[:, h, :], start=True, stop=True)
                ins.then_inc(f, 1)
                pe.wait_ge(a_masked, s.val(NCH, c + 1))
                for hf in range(2):
                    ps, f = claim(("AU", c, hf), s)
                    for h in range(hf, NH, 2):
                        ins = nc.tensor.matmul(ps[:, 128 * (h // 2):128 * (h // 2) + 128], BA[:, 1, ch(c, h), :], U[:, h, :], start=True, stop=True)
                    ins.then_inc(f, 1)

            def transpose_out(s, c):
                pe.wait_ge(og_ready, s.val(NCH, c + 1))
                for hf in range(2):
                    ps, f = claim(("OT", c, hf), s)
                    for h in range(3):
                        ins = nc.tensor.transpose(ps[:, 128 * h:128 * h + 128], O[:, c % 2, 2 * h + hf, :], P.ident[:])
                    ins.then_inc(f, 1)

            def project_out(s, c):
                if c < NCH - 1:
                    ps, f = claim(("WO", c), s)
                else:
                    ps, f = bank[LATE_BANK], late_full
                for hf in range(2):
                    ready(pe, ("OT", c, hf), s)
                for h in range(NH):
                    ins = split_product(ps[:], P.wo_hi[:, h, :], P.wo_lo[:, h, :], og_hi[:, h, :], og_lo[:, h, :], True,
                                        h == 0, h == NH - 1)
                ins.then_inc(f, 1)

            def outputs_end(s, between):
                project_out(s, NCH - 2)
                between(0)
                transpose_out(s, NCH - 1)
                between(1)

            def local(s, blocks, before=None):
                for n in blocks:
                    block_products(s, n)
                if s.first():
                    pe.wait_ge(prep.lo_done, 5)
                for i in range(2):
                    gate_products(s, i // 2, i % 2)
                token_sums(s)
                for c in range(NCH):
                    chunk_scores(s, c)
                    if c < NCH // 2:
                        k_transposes(s, 2 * c)
                        k_transposes(s, 2 * c + 1)
                if s.first():
                    pe.wait_ge(prep.lo_done, 7)
                for n in range(NV):
                    block_products(s, NQK + n)
                    if n == 0:
                        query_sums(s)
                    gate_products(s, (n + 2) // 2, n % 2)
                v_transposes(s, 0)
                if before is not None:
                    ready(pe, ("KQ", NCH - 1, LATE_BANK - 4), s)
                    project_out(before, NCH - 1)
                v_transposes(s, 1)
                solve(s)

            s0 = At(None, 0)
            pe.wait_ge(prep.const_made, CONSTANTS)
            ln_transposes(s0, range(NCH))
            pe.wait_ge(prep.lo_done, 1)
            for n in range(NPAIR):
                block_products(s0, n)
            pe.wait_ge(prep.lo_done, 3)
            decay_products(s0)
            local(s0, range(NPAIR, NQK))
            pe.wait_ge(prep.lo_done, 9)
            with pe.Fori(0, nst - 1) as r:
                s, b = At(r, 1), At(r, 0)
                for c in range(NCH):
                    recur(b, c)
                    if c == 1:
                        ln_transposes(s, range(0, NCH // 2))
                    if c == 2:
                        ln_transposes(s, range(NCH // 2, NCH))
                for t in (NCH - 2, NCH - 1):
                    ready(pe, ("ln", t), s)
                decay_products(s)
                outputs_end(b, lambda n: block_products(s, n))
                local(s, range(2, NQK), b)
            b = At(None, nst - 1)
            for c in range(NCH):
                recur(b, c)
            outputs_end(b, lambda n: None)
            ready(pe, ("WO", NCH - 2), b)
            project_out(b, NCH - 1)

        @block.vector
        def _(dve):
            steps = Steps(DVE_STEPS)
            t32 = Steps(T32_STEPS)
            v = nc.vector

            def ln_tile_stats(s):
                dve.wait_ge(x_in, s.val(16, 16))
                for t in range(NCH):
                    v.bn_stats(stats[:, t, :], xb[:, t, :]).then_inc(ln_step, 1)

            def ln_moments(s):
                dve.wait_ge(ln_step, s.val(LN_STEPS, NCH))

                def link_ln(ins, n):
                    ins.then_inc(ln_step, 1)
                    dve.wait_ge(ln_step, s.val(LN_STEPS, NCH + n))
                link_ln(v.tensor_tensor(mv[:, :, 0], stats[:, :, 1], stats[:, :, 4], ALU.add), 1)
                link_ln(v.tensor_tensor(ln_d[:], stats[:, :, 1], stats[:, :, 4], ALU.subtract), 2)
                link_ln(v.tensor_tensor(mv[:, :, 1], stats[:, :, 2], stats[:, :, 5], ALU.add), 3)
                link_ln(v.tensor_scalar(mv[:, :, 0], mv[:, :, 0], 0.5, None, ALU.mult), 4)
                link_ln(v.tensor_tensor(ln_d[:], ln_d[:], ln_d[:], ALU.mult), 5)
                link_ln(v.tensor_scalar(mv[:, :, 1], mv[:, :, 1], 1.0 / D, EPS, ALU.mult, ALU.add), 6)
                v.scalar_tensor_tensor(out=mv[:, :, 1], in0=ln_d[:], scalar=0.25, in1=mv[:, :, 1],
                                       op0=ALU.mult, op1=ALU.add).then_inc(ln_stats, 1)

            def ln_apply(s):
                dve.wait_ge(ln_rstd, s.val(1, 1))
                for t in range(NCH):
                    v.tensor_scalar(xb[:, t, :], xb[:, t, :], mv[:, t, 0:1], rstd[:, t:t + 1],
                                    ALU.subtract, ALU.mult).then_inc(xn_ready, 1)

            def xn_parts(s, tiles):
                for t in tiles:
                    ps, d = out_of(("ln", t))
                    dve.wait_ge(xhi_ready, s.val(NCH, t + 1))
                    cols = slice(CH * t, CH * t + CH)
                    v.tensor_tensor(x_lo[:, :, cols], ps[:].rearrange("p (b c) -> p b c", b=HB), x_hi[:, :, cols],
                                    ALU.subtract).then_inc(d, 1)

            def link(ins):
                n = steps.next()
                ins.then_inc(dve_step, 1)
                dve.wait_ge(dve_step, n)

            def decays(s):
                filled(dve, ("ab",), s)
                ps, d = out_of(("ab",))
                v.tensor_copy(ab[:].rearrange("p c n -> p (c n)"), ps[:, 0:2 * NCHH]).then_inc(d, 1)
                ready(dve, ("ab",), s)
                link(v.scalar_tensor_tensor(out=z[:], in0=ab[:, :, 0:NH], scalar=1.0 / W_SCALE,
                                            in1=P.dtb[:].unsqueeze(1).broadcast_to([128, NCH, NH]), op0=ALU.mult, op1=ALU.add))
                link(v.tensor_scalar(nb[:], ab[:, :, NH:2 * NH], -1.0 / W_SCALE, None, ALU.mult))
                v.scalar_tensor_tensor(out=az[:], in0=z[:], scalar=-1.0, in1=z[:], op0=ALU.mult, op1=ALU.max).then_inc(ab_ready, 1)

            def decays_end(s):
                dve.wait_ge(ab_exp, s.val(2, 2))
                link(v.tensor_scalar(eb[:], eb[:], 1.0, None, ALU.add))
                link(v.reciprocal(beta[:], eb[:]))
                dve.wait_ge(ab_ln, s.val(1, 1))
                link(v.scalar_tensor_tensor(out=z[:], in0=z[:], scalar=0.0, in1=ln1[:], op0=ALU.max, op1=ALU.add))
                v.tensor_tensor(g[:], z[:], P.nega[:].unsqueeze(1).broadcast_to([128, NCH, NH]), ALU.mult).then_inc(g_ready, 1)

            def convolve(s, blocks):
                for i in range(TAPS):
                    for n in blocks:
                        if i == 0:
                            dve.wait_ge(raw_ready, s.val(NBLK, n + 1))
                            if not (s.first() and n < 2):
                                dve.wait_ge(silu_done, s.val(NBLK, n - 1))
                        src = raw[:, n % 3, i:i + ST]
                        out = cv[:, n % 2, :]
                        w = P.taps[:, n, i:i + 1]
                        if i == 0:
                            ins = v.tensor_scalar(out, src, w, None, ALU.mult)
                        else:
                            dve.wait_ge(dve_step, last[n])
                            ins = v.scalar_tensor_tensor(out=out, in0=src, scalar=w, in1=out, op0=ALU.mult, op1=ALU.add)
                        if i < TAPS - 1:
                            last[n] = steps.next()
                            ins.then_inc(dve_step, 1)
                        else:
                            ins.then_inc(cv_ready, 1)

            last = {}

            def token_scales(s):
                filled(dve, ("sums",), s)
                ps, d = out_of(("sums",))
                v.tensor_copy(sums[:], ps[:, 0:4 * NCHH]).then_inc(d, 1)
                ready(dve, ("sums",), s)
                link(v.reciprocal(rk2[:], sums[:, 3 * NCHH:4 * NCHH]))
                link(v.tensor_tensor(cj[:], rk2[:], beta[:].rearrange("p c h -> p (c h)"), ALU.mult))
                dve.wait_ge(dec_ready, s.val(4, 4))
                v.tensor_scalar(ngam[:], gam[:], -1.0, None, ALU.mult).then_inc(ks_ready, 1)
                v.tensor_tensor(ks[:], cj[:], suf[:], ALU.mult).then_inc(ks_ready, 1)
                dve.wait_ge(ks_ready, s.val(2, 2))

            def query_scales(s):
                u = ("qsums",)
                filled(dve, u, s)
                ps, d = out_of(u)
                v.tensor_scalar(eq[:], ps[:, 0:NCHH], DK * EPS / W_SCALE ** 2, None, ALU.mult).then_inc(d, 1)

            def k_tokens(s, c):
                filled(dve, ("ktr", c), s)
                ps, d = out_of(("ktr", c))
                v.tensor_tensor(ktok[:, c, :].rearrange("p (h k) -> p h k", h=NH), ps[:, 0:KD].rearrange("p (h k) -> p h k", h=NH),
                                ks[:, NH * c:NH * c + NH].unsqueeze(2).broadcast_to([128, NH, DK]), ALU.mult).then_inc(d, 1)

            def scores(s, c):
                for hf in range(2):
                    ready(dve, ("D", c, hf), s)
                for p, heads in enumerate(KQ_HEADS):
                    u = ("KQ", c, p)
                    filled(dve, u, s)
                    ps, d = out_of(u)
                    for k, h in enumerate(heads):
                        ins = v.scalar_tensor_tensor(out=BA[:, :, ch(c, h), :],
                                                     in0=ps[:, 256 * k:256 * k + 256].rearrange("p (k c) -> p k c", k=2),
                                                     scalar=cj[:, ch(c, h):ch(c, h) + 1],
                                                     in1=E[:, h, :].unsqueeze(1).broadcast_to([128, 2, CH]),
                                                     op0=ALU.mult, op1=ALU.mult)
                    ins.then_inc(d, 1)

            def invert_blocks(s):
                t32.start(s)

                def step(ins):
                    ins.then_inc(t32_step, 1)
                    return t32.next()

                if not s.first():
                    dve.wait_ge(t_out, s.val(16, 0))
                    dve.wait_ge(tt_out, s.val(16, 0))
                dve.wait_ge(t32_step, step(v.memset(tin[:], 0.0)))
                ones = step(v.memset(tin[:, 0:SUB * SUB:SUB + 1], 1.0))
                dve.wait_ge(b_in, s.val(16, 16))
                tv = tin[:].rearrange("p (i c) -> p i c", i=SUB)
                half = SUB // 2
                done_to = [ones, ones]
                for j in range(SUB - 1):
                    n = SUB - 1 - j
                    todo = []
                    for k in range(2):
                        c0, c1 = half * k, min(half * (k + 1), j + 1)
                        if c0 < c1:
                            prod = tmp[:, half * half * k:half * half * k + n * (c1 - c0)]
                            todo.append((k, c0, c1, prod.rearrange("p (i c) -> p i c", i=n)))
                    for k, c0, c1, prod in todo:
                        dve.wait_ge(t32_step, done_to[k])
                        done_to[k] = step(v.tensor_tensor(
                            prod, bin_[:, SUB * j + j + 1:SUB * j + SUB].unsqueeze(2).broadcast_to([NINST, n, c1 - c0]),
                            tv[:, j, c0:c1].unsqueeze(1).broadcast_to([NINST, n, c1 - c0]), ALU.mult))
                    for k, c0, c1, prod in todo:
                        dve.wait_ge(t32_step, done_to[k])
                        rest = tv[:, j + 1:SUB, c0:c1]
                        done_to[k] = step(v.tensor_tensor(rest, rest, prod, ALU.subtract))
                dve.wait_ge(t32_step, done_to[0])
                dve.wait_ge(t32_step, done_to[1])
                step(v.tensor_copy(bin_[:].rearrange("p (c i) -> p c i", c=SUB), tin[:].rearrange("p (i c) -> p c i", i=SUB)))

            def heads3(ps):
                return ps[:, 0:HALF].rearrange("p (h d) -> p h d", h=3)

            def heads64(ps, lo_):
                return ps[lo_:lo_ + 64, 0:64 * NH].rearrange("p (h d) -> p h d", h=NH)

            def solve(s):
                dve.wait_ge(v_conv, s.val(NV, NV - 1))
                for k in range(NCH + 3):
                    if k < NCH:
                        for hf in range(2):
                            filled(dve, ("X", k, hf), s)
                            ps, d = out_of(("X", k, hf))
                            v.tensor_tensor(eg[:, k % 2, hf:NH:2, :], heads3(ps),
                                            P.level32[:].unsqueeze(1).broadcast_to([128, 3, CH]), ALU.mult).then_inc(d, 1)
                    c = k - 1
                    if 0 <= c < NCH:
                        filled(dve, ("Y", c), s)
                        ps, d = out_of(("Y", c))
                        v.tensor_tensor(T1[:, c % 2, :, :], Tbd[0:64, NH * c:NH * c + NH, 0:64], heads64(ps, 0),
                                        ALU.subtract).then_inc(d, 1)
                        for hf in range(2):
                            filled(dve, ("Z", c, hf), s)
                            ps, d = out_of(("Z", c, hf))
                            ws = W[:, NH * c + hf:NH * c + NH:2, :]
                            v.tensor_tensor(ws, ws, heads3(ps), ALU.subtract).then_inc(d, 1)
                    c = k - 3
                    if 0 <= c < NCH:
                        filled(dve, ("Z2", c), s)
                        ps, d = out_of(("Z2", c))
                        for hf in range(2):
                            ready(dve, ("Z", c, hf), s)
                        w = W[0:64, NH * c:NH * c + NH, 64:128]
                        v.tensor_tensor(w, w, heads64(ps, 0), ALU.subtract).then_inc(d, 1)

            def right_sides(s, c):
                for hf in range(2):
                    u = ("KS", c, hf)
                    filled(dve, u, s)
                    ps, d = out_of(u)
                    for h in range(hf, NH, 2):
                        ins = v.scalar_tensor_tensor(out=Rr[:, h, :], in0=ps[:, 128 * (h // 2):128 * (h // 2) + 128],
                                                     scalar=ngam[:, ch(c, h):ch(c, h) + 1], in1=V[:, c, h, :],
                                                     op0=ALU.mult, op1=ALU.add)
                    ins.then_inc(d, 1)

            def state(s, c):
                u = ("dS", c)
                filled(dve, u, s)
                ps, d = out_of(u)
                for b in range(NPAIR):
                    ins = v.scalar_tensor_tensor(out=P.S[:, b, :], in0=P.S[:, b, :], scalar=gC[:, c, b:b + 1],
                                                 in1=ps[:, 128 * b:128 * b + 128], op0=ALU.mult, op1=ALU.add)
                ins.then_inc(d, 1)

            def outputs(s, c):
                for hf in range(2):
                    ready(dve, ("QS", c, hf), s)
                    u = ("AU", c, hf)
                    filled(dve, u, s)
                    ps, d = out_of(u)
                    o = O[:, c % 2, hf:NH:2, :]
                    v.tensor_tensor(o, heads3(ps), o, ALU.add).then_inc(d, 1)

            def mean_squares(s, c):
                dve.wait_ge(ss_ready, s.val(NCH, c + 1))
                v.scalar_tensor_tensor(out=t6[:, c % 2, :], in0=ss[:, c % 2, :], scalar=1.0 / (DV * W_SCALE ** 2),
                                       in1=eq[:, NH * c:NH * c + NH], op0=ALU.mult, op1=ALU.add).then_inc(t6_ready, 1)

            def gated(s, c):
                dve.wait_ge(rn_ready, s.val(NCH, c + 1))
                for h in range(NH):
                    o = O[:, c % 2, h, :]
                    ins = v.scalar_tensor_tensor(out=o, in0=o, scalar=rn[:, c % 2, h:h + 1],
                                                 in1=gate[:, c, DV * h:DV * h + DV], op0=ALU.mult, op1=ALU.mult)
                ins.then_inc(og_ready, 1)

            def og_part(s, c):
                for hf in range(2):
                    dve.wait_ge(oghi_ready, s.val(2 * NCH, 2 * c + hf + 1))
                    ps, d = out_of(("OT", c, hf))
                    hs = slice(hf, NH, 2)
                    v.tensor_tensor(og_lo[:, hs, :], heads3(ps), og_hi[:, hs, :], ALU.subtract).then_inc(d, 1)

            def residual(s, c):
                if c < NCH - 1:
                    filled(dve, ("WO", c), s)
                    ps, d = out_of(("WO", c))
                else:
                    dve.wait_ge(late_full, s.val(1, 1))
                    ps, d = bank[LATE_BANK], late_done
                dve.wait_ge(xr_in[c % 2], s.val(16 * NCH // 2, 16 * (c // 2 + 1)))
                v.scalar_tensor_tensor(out=xr[:, c % 2, :], in0=ps[:], scalar=W_SCALE ** -2, in1=xr[:, c % 2, :],
                                       op0=ALU.mult, op1=ALU.add).then_inc(d, 1)

            def local(s, first, before=None):
                for n in range(first, NQK, 2):
                    convolve(s, (n, n + 1))
                token_scales(s)
                for c in range(NCH):
                    scores(s, c)
                    if s.first() and c < NSTG - 1:
                        prep.piece_low(dve, NSTG + 1 + c)
                    if c < NCH // 2:
                        k_tokens(s, 2 * c)
                        k_tokens(s, 2 * c + 1)
                if s.first():
                    prep.spline_coefficients(dve)
                query_scales(s)
                invert_blocks(s)
                if before is not None:
                    residual(before, NCH - 1)
                solve(s)

            def recur(b, c, following=None):
                right_sides(b, c)
                if following is not None and c == 0:
                    ln_tile_stats(following)
                if c >= 1:
                    mean_squares(b, c - 1)
                if following is not None and c == 1:
                    ln_apply(following)
                if c >= 2:
                    residual(b, c - 2)
                if c >= 1:
                    gated(b, c - 1)
                state(b, c)
                if following is not None and c == 0:
                    ln_moments(following)
                if c >= 1:
                    og_part(b, c - 1)
                outputs(b, c)

            def outputs_end(b):
                mean_squares(b, NCH - 1)
                gated(b, NCH - 1)
                residual(b, NCH - 2)
                og_part(b, NCH - 1)

            s0 = At(None, 0)
            steps.start(s0)
            ln_tile_stats(s0)
            ln_moments(s0)
            ln_apply(s0)
            prep.piece_low(dve, 0)
            xn_parts(s0, range(NCH))
            prep.piece_low(dve, 1)
            prep.decay_weights_low(dve)
            prep.piece_low(dve, 2)
            prep.piece_low(dve, 3)
            dve.wait_ge(prep.small_in, prep.SMALL)
            dve.wait_ge(prep.nega_ready, 2)
            dve.wait_ge(prep.const_made, CONSTANTS)
            convolve(s0, (0, 1))
            decays(s0)
            convolve(s0, (2, 3))
            decays_end(s0)
            convolve(s0, (4, 5))
            prep.piece_low(dve, NSTG)
            local(s0, NQK)
            with dve.Fori(0, nst - 1) as r:
                s, b = At(r, 1), At(r, 0)
                steps.start(s)
                recur(b, 0, s)
                recur(b, 1, s)
                xn_parts(s, range(0, NCH // 2))
                recur(b, 2)
                xn_parts(s, range(NCH // 2, NCH))
                recur(b, 3)
                decays(s)
                outputs_end(b)
                convolve(s, (0, 1))
                decays_end(s)
                local(s, 2, b)
            b = At(None, nst - 1)
            for c in range(NCH):
                recur(b, c)
            outputs_end(b)
            residual(b, NCH - 1)

        @block.scalar
        def _(act):
            sc = nc.scalar

            def xn_high(s, tiles):
                if not s.first() and tiles[0] == 0:
                    act.wait_ge(spilled, s.val(32, 0))
                for t in tiles:
                    filled(act, ("ln", t), s)
                    ps, _ = out_of(("ln", t))
                    sc.activation(x_hi[:, :, CH * t:CH * t + CH], ps[:].rearrange("p (b c) -> p b c", b=HB),
                                  ACT.Copy).then_inc(xhi_ready, 1)

            def decays(s):
                act.wait_ge(ab_ready, s.val(1, 1))
                sc.activation(e1[:], az[:], ACT.Exp, scale=-1.0).then_inc(ab_exp, 1)
                sc.activation(eb[:], nb[:], ACT.Exp).then_inc(ab_exp, 1)
                act.wait_ge(ab_exp, s.val(2, 1))
                sc.activation(ln1[:], e1[:], ACT.Ln, bias=P.ones[:, 0:1]).then_inc(ab_ln, 1)

            def gates(s, c, h):
                if not s.first():
                    act.wait_ge(og_ready, s.val(NCH, 0))
                u = ("gate", c, h)
                filled(act, u, s)
                ps, d = out_of(u)
                sc.activation(gate[:, c, 384 * h:384 * h + 384], ps[:, 0:384], ACT.Silu, scale=1.0 / W_SCALE).then_inc(d, 1)

            def raw_out(s, n):
                u = ("blk", n)
                filled(act, u, s)
                ps, d = out_of(u)
                if not (s.first() and n < 3):
                    act.wait_ge(raw_ready, s.val(NBLK, n - 2))
                    if 3 <= n < NQK + 3:
                        act.wait_ge(cv_ready, s.val(NQK, n - 2))
                    else:
                        act.wait_ge(v_conv, s.val(NV, (n - 2 if n < 3 else n - NQK - 2)))
                sc.activation(raw[:, n % 3, TAPS - 1:], ps[:], ACT.Copy, scale=1.0 / W_SCALE).then_inc(d, 1)

            def v_taps(s, n):
                i = n - NQK
                act.wait_ge(raw_ready, s.val(NBLK, n + 1))
                act.wait_ge(silu_done, s.val(NBLK, n - 1))
                if i >= 2:
                    act.wait_ge(v_conv, s.val(NV, i - 1))
                else:
                    filled(act, ("D", NCH - 1, 1), s)
                    ready(act, ("KQ", NCH - 1, len(KQ_HEADS) - 1), s)
                    if i == 1:
                        filled(act, ("qsums",), s)
                for t in range(TAPS):
                    dst = cv[:, n % 2, :] if t == 0 else tap_products[i % 2][:, t - 1, :]
                    ins = sc.activation(dst, raw[:, n % 3, t:t + ST], ACT.Copy, scale=P.taps[:, n, t:t + 1])
                ins.then_inc(taps_ready, 1)

            def v_tokens(s, n):
                u = ("vtr", n)
                filled(act, u, s)
                ps, d = out_of(u)
                if n == 0:
                    act.wait_ge(nk_ready, s.val(1, 1))
                for c in range(NCH):
                    ins = sc.activation(V[:, c, n, :], ps[:, 128 * c:128 * c + 128], ACT.Copy, scale=nk[:, ch(c, n):ch(c, n) + 1])
                ins.then_inc(d, 1)

            def silu(s, n):
                if n < NQK:
                    act.wait_ge(cv_ready, s.val(NQK, n + 1))
                    dst = kq[:, n % NPAIR, n // NPAIR, :]
                else:
                    act.wait_ge(v_conv, s.val(NV, n - NQK + 1))
                    dst = vT[:, n % 3, :]
                    if n - NQK >= 3:
                        filled(act, ("vtr", n - NQK - 3), s)
                sc.activation(dst, cv[:, n % 2, :], ACT.Silu).then_inc(silu_done, 1)

            def decay_exps(s):
                ready(act, ("sums",), s)
                tot = sums[:, 2 * NCHH:3 * NCHH].rearrange("p (c b r) -> p c b r", c=NCH, r=2)
                sc.activation(gam[:], sums[:, 0:NCHH], ACT.Exp).then_inc(dec_ready, 1)
                sc.activation(suf[:], sums[:, NCHH:2 * NCHH], ACT.Exp).then_inc(dec_ready, 1)
                for r in range(2):
                    rows = slice(DK * r, DK * r + DK)
                    sc.activation(gC[rows, :, :], tot[rows, :, :, r], ACT.Exp).then_inc(dec_ready, 1)

            def pair_exps(s, c):
                if c:
                    ready(act, ("KQ", c - 1, len(KQ_HEADS) - 1), s)
                for hf in range(2):
                    u = ("D", c, hf)
                    filled(act, u, s)
                    ps, d = out_of(u)
                    sc.activation(E[:, hf:NH:2, :], ps[:, 0:HALF].rearrange("p (h c) -> p h c", h=3), ACT.Exp).then_inc(d, 1)

            def local(s):
                for n in range(NQK):
                    raw_out(s, n)
                    if n == 1 and not s.first():
                        decays(s)
                    if n == 1 and s.first():
                        prep.piece_high(act, NSTG)
                    if n >= 2:
                        silu(s, n - 2)
                    if n == 3 and s.first():
                        decays(s)
                gates(s, 0, 0)
                gates(s, 0, 1)
                silu(s, NQK - 2)
                silu(s, NQK - 1)
                decay_exps(s)
                for c in range(NCH):
                    pair_exps(s, c)
                    if s.first() and c < NSTG - 1:
                        prep.piece_high(act, NSTG + 1 + c)
                for n in range(NV):
                    raw_out(s, NQK + n)
                    if n == NV - 1:
                        silu(s, NQK + n - 2)
                    v_taps(s, NQK + n)
                    gates(s, (n + 2) // 2, n % 2)
                    if n in (1, 2, 3, NV - 1):
                        silu(s, NQK + n - 1)
                v_tokens(s, 0)
                v_tokens(s, 1)
                silu(s, NBLK - 1)
                for c in range(NCH):
                    v_tokens(s, c + 2)
                    u = ("X2", c)
                    filled(act, u, s)
                    ps, d = out_of(u)
                    sc.activation(X2s[:, c % 2, :, :], ps[:, 0:64 * NH].rearrange("p (h c) -> p h c", h=NH), ACT.Copy).then_inc(d, 1)

            def q_state(s, c):
                for hf in range(2):
                    u = ("QS", c, hf)
                    filled(act, u, s)
                    ps, d = out_of(u)
                    for h in range(hf, NH, 2):
                        ins = sc.activation(O[:, c % 2, h, :], ps[:, 128 * (h // 2):128 * (h // 2) + 128], ACT.Copy,
                                            scale=gam[:, ch(c, h):ch(c, h) + 1])
                    ins.then_inc(d, 1)

            def updates(s, c):
                for hf in range(2):
                    u = ("U", c, hf)
                    filled(act, u, s)
                    ps, d = out_of(u)
                    sc.activation(U[:, hf:NH:2, :], ps[:, 0:HALF].rearrange("p (h d) -> p h d", h=3), ACT.Copy).then_inc(d, 1)

            def squares(s, c):
                if c:
                    act.wait_ge(ss_ready, s.val(NCH, c))
                for h in range(NH):
                    if h < 2:
                        ready(act, ("AU", c, h), s)
                    ins = sc.activation(junk[:, h, :], O[:, c % 2, h, :], ACT.Square, accum_out=ss[:, c % 2, h:h + 1])
                ins.then_inc(ss_ready, 1)

            def og_high(s, c):
                for hf in range(2):
                    u = ("OT", c, hf)
                    filled(act, u, s)
                    ps, _ = out_of(u)
                    sc.activation(og_hi[:, hf:NH:2, :], ps[:, 0:HALF].rearrange("p (h c) -> p h c", h=3),
                                  ACT.Copy).then_inc(oghi_ready, 1)

            def recur(b, c):
                updates(b, c)
                q_state(b, c)
                if c >= 1:
                    og_high(b, c - 1)
                squares(b, c)

            def outputs_end(b):
                og_high(b, NCH - 1)
                act.wait_ge(ss_ready, b.val(NCH, NCH))

            s0 = At(None, 0)
            for i in range(NSTG):
                prep.load_piece(act, i)
            prep.piece_high(act, 0)
            act.wait_ge(prep.const_made, CONSTANTS)
            xn_high(s0, range(NCH))
            prep.piece_high(act, 1)
            prep.decay_weights_high(act)
            prep.piece_high(act, 2)
            prep.piece_high(act, 3)
            prep.decay_rates(act)
            local(s0)
            with act.Fori(0, nst - 1) as r:
                s, b = At(r, 1), At(r, 0)
                for c in range(NCH):
                    recur(b, c)
                    if c == 1:
                        xn_high(s, range(0, NCH // 2))
                    if c == 2:
                        xn_high(s, range(NCH // 2, NCH))
                outputs_end(b)
                local(s)
            b = At(None, nst - 1)
            for c in range(NCH):
                recur(b, c)
            outputs_end(b)

        @block.gpsimd
        def _(pool):
            g_ = nc.gpsimd

            def ln_scale(s):
                pool.wait_ge(ln_stats, s.val(1, 1))
                g_.tensor_tensor(out=rstd[:], in0=mv[:, :, 1], in1=P.mhalf[:, 0:NCH], op=ALU.pow).then_inc(ln_rstd, 1)

            def spill(s):
                for t in (NCH - 2, NCH - 1):
                    ready(pool, ("ln", t), s)
                pool.dma_start(scr.xh[s.idx()], x_hi[:].rearrange("p b c -> p (b c)")).then_inc(spilled, 16)
                pool.dma_start(scr.xl[s.idx()], x_lo[:].rearrange("p b c -> p (b c)")).then_inc(spilled, 16)

            def norm_scale(s, c):
                pool.wait_ge(t6_ready, s.val(NCH, c + 1))
                g_.tensor_tensor(out=rn[:, c % 2, :], in0=t6[:, c % 2, :], in1=P.mhalf[:, 0:NH], op=ALU.pow).then_inc(rn_ready, 1)

            def halo(s, n):
                ready(pool, ("blk", n), s)
                g_.tensor_tensor(out=raw[:, n % 3, 0:TAPS - 1], in0=P.halo[:, n, :], in1=P.zeros[:], op=ALU.add).then_inc(halo_used, 1)
                pool.wait_ge(halo_used, s.val(NBLK, n + 1))
                g_.tensor_tensor(out=P.halo[:, n, :], in0=raw[:, n % 3, ST:ST + TAPS - 1], in1=P.zeros[:], op=ALU.add).then_inc(raw_ready, 1)

            def add_taps(s, n):
                i = n - NQK
                tp, c = tap_products[i % 2], cv[:, n % 2, :]
                pool.wait_ge(taps_ready, s.val(NV, i + 1))
                g_.tensor_tensor(out=c, in0=c, in1=tp[:, 0, :], op=ALU.add).then_inc(tap_step, 1)
                g_.tensor_tensor(out=tp[:, 1, :], in0=tp[:, 1, :], in1=tp[:, 2, :], op=ALU.add).then_inc(tap_step, 1)
                pool.wait_ge(tap_step, s.val(2 * NV, 2 * i + 2))
                g_.tensor_tensor(out=c, in0=c, in1=tp[:, 1, :], op=ALU.add).then_inc(v_conv, 1)

            def square(s, n):
                pool.wait_ge(silu_done, s.val(NBLK, n + 1))
                src = kq[:, n % NPAIR, n // NPAIR, :]
                g_.tensor_tensor(out=square_of(n), in0=src, in1=src, op=ALU.mult).then_inc(sq_ready, 1)

            def masked_g(s, c):
                if c:
                    filled(pool, ("D", c - 1, 1), s)
                g_.tensor_tensor(out=gm[:], in0=P.upto[:].unsqueeze(1).broadcast_to([128, NH, CH]),
                                 in1=g[:, c, :].unsqueeze(2).broadcast_to([128, NH, CH]), op=ALU.mult).then_inc(gm_ready, 1)

            def mask_weights(s, c):
                ready(pool, ("KQ", c, len(KQ_HEADS) - 1), s)
                a = BA[:, 1, NH * c:NH * c + NH, :]
                g_.tensor_tensor(out=a, in0=a, in1=P.upto[:].unsqueeze(1).broadcast_to([128, NH, CH]),
                                 op=ALU.mult).then_inc(a_masked, 1)

            def local(s):
                for n in range(NQK):
                    halo(s, n)
                    if n == 4:
                        pool.wait_ge(g_ready, s.val(1, 1))
                        masked_g(s, 0)
                    if n >= 2:
                        square(s, n - 2)
                square(s, NQK - 2)
                ready(pool, ("sums",), s)
                g_.tensor_tensor(out=nk[:], in0=sums[:, 3 * NCHH:4 * NCHH], in1=P.phalf[:, 0:NCHH],
                                 op=ALU.pow).then_inc(nk_ready, 1)
                masked_g(s, 1)
                square(s, NQK - 1)
                for c in range(1, NCH):
                    if c + 1 < NCH:
                        masked_g(s, c + 1)
                    mask_weights(s, c - 1)
                for n in range(NQK, NBLK + 1):
                    if s.first() and n == NBLK - 2:
                        pool.wait_ge(prep.coef_out, prep.COEF_OUT)
                        g_.memset(Tbd[:], 0.0)
                        g_.memset(W[:], 0.0).then_inc(prep.cleared, 1)
                    if n < NBLK:
                        halo(s, n)
                    if n > NQK:
                        add_taps(s, n - 1)
                mask_weights(s, NCH - 1)

            s0 = At(None, 0)
            prep.constants(pool)
            ln_scale(s0)
            spill(s0)
            local(s0)
            with pool.Fori(0, nst - 1) as r:
                s, b = At(r, 1), At(r, 0)
                ln_scale(s)
                norm_scale(b, 0)
                norm_scale(b, 1)
                spill(s)
                for c in range(2, NCH):
                    norm_scale(b, c)
                g_.memset(W[:], 0.0)
                local(s)
            b = At(None, nst - 1)
            for c in range(NCH):
                norm_scale(b, c)

        @block.sync
        def _(sp):
            def load_x(s, b):
                if b is not None:
                    sp.wait_ge(v_conv, b.val(NV, NV))
                sp.dma_start(xb[:], x_v[s.idx()]).then_inc(x_in, 16)

            def load_residual(s, c):
                if not (s.first() and c < 2):
                    sp.wait_ge(y_out[c % 2], s.val(16 * NCH // 2, 16 * (c // 2)))
                sp.dma_start(xr[:, c % 2, :], xr_v[s.idx(), c]).then_inc(xr_in[c % 2], 16)

            def store_y(s, c):
                if c < NCH - 1:
                    ready(sp, ("WO", c), s)
                else:
                    sp.wait_ge(late_done, s.val(1, 1))
                sp.dma_start(y_v[s.idx(), c], xr[:, c % 2, :]).then_inc(y_out[c % 2], 16)

            def store_first(s):
                for c in range(NCH - 1):
                    store_y(s, c)
                    if c + 2 < NCH:
                        load_residual(s, c + 2)

            def exchange(s):
                ready(sp, ("KQ", NCH - 1, len(KQ_HEADS) - 1), s)
                for q in range(NSUB):
                    rows = slice(SUB * q, SUB * q + SUB)
                    sp.dma_start(scr.b[q].rearrange("c j i -> j c i"), BA[rows, 0, :, rows]).then_inc(b_out, 16)
                sp.wait_ge(b_out, s.val(16 * NSUB, 16 * NSUB))
                sp.dma_start(bin_[:], scr.b.rearrange("q c j i -> (q c) (j i)")).then_inc(b_in, 16)
                if s.first():
                    prep.store_coefficients(sp)
                sp.wait_ge(t32_step, s.val(T32_STEPS, T32_STEPS - 1))
                sp.dma_start(scr.t.rearrange("q c i k -> (q c) (i k)"), tin[:]).then_inc(t_out, 16)
                sp.wait_ge(t32_step, s.val(T32_STEPS, T32_STEPS))
                sp.dma_start(scr.tt.rearrange("q c k i -> (q c) (k i)"), bin_[:]).then_inc(tt_out, 16)
                sp.wait_ge(t_out, s.val(16, 16))
                if s.first():
                    sp.wait_ge(prep.cleared, 1)
                for q in range(NSUB):
                    rows = slice(SUB * q, SUB * q + SUB)
                    sp.dma_start(Tbd[rows, :, rows], scr.t[q].rearrange("c i k -> i c k")).then_inc(tbd_in, 16)
                sp.wait_ge(tt_out, s.val(16, 16))
                for q in range(NSUB):
                    rows = slice(SUB * q, SUB * q + SUB)
                    sp.dma_start(W[rows, :, rows], scr.tt[q].rearrange("c k i -> k c i")).then_inc(w_in, 16)

            s0 = At(None, 0)
            load_x(s0, None)
            prep.load_decay_weights(sp)
            prep.load_small(sp)
            prep.pad_control_points(sp)
            for i in range(NSTG, 2 * NSTG):
                prep.load_piece(sp, i)
            prep.gather_control_points(sp)
            load_residual(s0, 0)
            load_residual(s0, 1)
            exchange(s0)
            with sp.Fori(0, nst - 1) as r:
                s, b = At(r, 1), At(r, 0)
                load_x(s, b)
                store_first(b)
                exchange(s)
                load_residual(s, 0)
                store_y(b, NCH - 1)
                load_residual(s, 1)
            store_first(At(None, nst - 1))
            store_y(At(None, nst - 1), NCH - 1)
            for i in range(2):
                sp.wait_ge(y_out[i], 16 * NCH // 2 * nst)
            sp.wait_ge(spilled, 32 * nst)


CONSTANTS = 16
DVE_STEPS = 3 * NQK + 5 + 2
LN_STEPS = NCH + 6
T32_STEPS = 3 + 2 * (SUB - 1) + SUB - 2


def feed(nc, A, scr, nst=NST):
    with ExitStack() as ctx:
        def sb(name, shape, dt=F32):
            return ctx.enter_context(nc.sbuf_tensor(name, shape, dt))

        def sem(name):
            return ctx.enter_context(nc.semaphore(name))

        GC = NCOL // IB
        NG = IB * HB
        pg = [ctx.enter_context(nc.psum_tensor(f"pg{i}", [128, 512], F32)) for i in range(2)]
        pu = [ctx.enter_context(nc.psum_tensor(f"pu{i}", [128, 512], F32)) for i in range(2)]
        pf = [ctx.enter_context(nc.psum_tensor(f"pf{i}", [128, 512], F32)) for i in range(2)]
        pd = [ctx.enter_context(nc.psum_tensor(f"pd{i}", [128, 512], F32)) for i in range(2)]
        pairs = [(pg[0], pu[0]), (pg[1], pu[1]), (pd[0], pd[1])]
        b_hi = sb("b_hi", [128, NP, HB, 128], F16)
        b_lo = sb("b_lo", [128, NP, HB, 128], F16)
        c_hi = sb("c_hi", [128, 2, IB, 128], F16)
        c_lo = sb("c_lo", [128, 2, IB, 128], F16)
        dn = sb("dn", [128, IB, 2, D], F16)
        dw = sb("dw", [128, IB, 2, D], F16)
        x_hi = sb("fx_hi", [128, HB, ST], F16)
        x_lo = sb("fx_lo", [128, HB, ST], F16)
        f = sb("f", [128, IB, ST], F16)
        it = sb("it", [128, 2, IB, ST], F16)
        it_hi, it_lo = it[:, 0], it[:, 1]
        room = it[:].rearrange("p a i c -> p (a i c)").bitcast(F32)
        used = 0

        def part(width):
            nonlocal used
            used += width
            return room[:, used - width:used]
        cg = part(IB * ROW)
        cf = part(2 * NG * NF).rearrange("p (m c f) -> p m c f", m=2, f=NF)
        early = part(2 * NG * NW).rearrange("p (m c e) -> p m c e", m=2, e=NW)
        tables = part(NG * (2 * NW + 1))
        gknot = part(NG)
        past = part(NG * NW // 4).bitcast(U8).rearrange("p (c e) -> p c e", e=NW)
        before = part(NG * NW // 4).bitcast(U8).rearrange("p (c e) -> p c e", e=NW)
        cubic = cg.rearrange("p (c m a k) -> p c m a k", m=3, a=2, k=4)
        sample, offset = (tables[:, NG * NW * i:NG * NW * (i + 1)].rearrange("p (c e) -> p c e", e=NW) for i in range(2))
        turn = tables[:, 2 * NG * NW:]
        sg = sb("sg", [128, 2, ST])
        hh = sb("hh", [128, 2, ST])
        yr = sb("yr", [128, 2, D])
        wt = sb("wt", [128, len(pairs), GC])
        later_in = sb("later_in", [128, NCOL // 4], mybir.dt.uint32)
        later = later_in[:].bitcast(U8).rearrange("p (i c) -> p i c", c=GC)
        member = sb("member", [128, IB], mybir.dt.uint32)
        ident = sb("fident", [128, 128])
        pow_in = sb("pow_in", [12, 128])
        coef = dw[0:12].rearrange("p i a d -> p (i a d)").rearrange("p (a i c) -> p a i c", a=2, c=GC)
        powers = sb("powers", [12, 128], F16)
        const_in, member_in, tables_in = sem("const_in"), sem("member_in"), sem("tables_in")
        basis_in = [sem(f"basis_in{k}") for k in range(4)]
        x_in, y_in, y_out = sem("fx_in"), [sem(f"y_in{i}") for i in range(2)], [sem(f"out{i}") for i in range(2)]
        coef_in = [sem(f"coef_in{k}") for k in range(4)]
        poly_made, first_copied, picked, w_hi_made, w_made = (
            sem("poly_made"), sem("first_copied"), sem("picked"), sem("w_hi_made"), sem("w_made"))
        down_stored, down_in = sem("down_stored"), sem("down_in")
        cubics_in, early_step, single_step, turned_made, ident_made = (
            sem("cubics_in"), sem("early_step"), sem("single_step"), sem("turned_made"), sem("ident_made"))
        turned_hi, turned_lo, hi_copied, lo_copied = sem("turned_hi"), sem("turned_lo"), sem("hi_copied"), sem("lo_copied")
        feat_made, feat_hi, feat_lo, feat_ready = sem("feat_made"), sem("feat_hi"), sem("feat_lo"), sem("feat_ready")
        gate_made, up_made, sg_ready, h_ready, hi_ready, it_ready = (
            sem("gate_made"), sem("up_made"), sem("sg_ready"), sem("h_ready"), sem("hi_ready"), sem("it_ready"))
        down_made, down_read = sem("down_made"), sem("down_read")
        powers_ready = sem("powers_ready")
        block = ctx.enter_context(nc.Block())
        y_v = scr.y.rearrange("(s t p) d -> s t p d", t=NCH, p=128)
        o_v = A.out.rearrange("(n p) d -> n p d", p=128)
        HORNER = 6
        EARLY_STEPS = 2 * (1 + HORNER) + HORNER
        SINGLE_STEPS = 2 + 2 * 3 + HORNER
        TURNS = 2 * NP // 4
        LOW, HIGH = slice(0, 64), slice(64, 128)
        HALVES = ((LOW, HIGH), (HIGH, LOW))

        def turned(part, n, e, half):
            return part[half, n % 2, 8 * (n // 2) + e:8 * (n // 2) + 8:2, :]

        def turned_from(n, e):
            return pd[n % 2][HALVES[e][0], :].rearrange("p (k r) -> p k r", r=128)

        PN = GC // IB

        def down_block(part, i):
            return dn[:, :, part, PN * i:PN * i + PN]

        def by_block(t):
            return t.rearrange("p (o b) -> p b o", b=IB)

        def at_samples(out, m, a, ops, k, link):
            c = [cubic[:, :, m, a, n:n + 1].broadcast_to([128, NG, NW]) for n in range(4)]
            link(ops.tensor_tensor(out, c[3] if k == 0 else out, offset, ALU.mult))
            link(ops.tensor_tensor(out, out, c[2 - k], ALU.add))

        @block.sync
        def _(sp):

            def load_coef(k):
                cols, blocks = slice(NCOL // 4 * k, NCOL // 4 * (k + 1)), slice(IB // 4 * k, IB // 4 * (k + 1))
                for row, part in ((0, 0), (4, 0), (8, 1)):
                    sp.dma_start(coef[row:row + 4, :, blocks, :].rearrange("k a i c -> k a (i c)"),
                                 scr.coef[part, :, :, cols]).then_inc(coef_in[k], 16)
                words = slice(NCOL // 16 * k, NCOL // 16 * (k + 1))
                sp.dma_start(later_in[:, words], A.later[:, words]).then_inc(coef_in[k], 16)

            def load_x(s):
                if not s.first():
                    sp.wait_ge(feat_made, s.val(NP, 0))
                sp.dma_start(x_hi[:].rearrange("p b c -> p (b c)"), scr.xh[s.idx()]).then_inc(x_in, 16)
                sp.dma_start(x_lo[:].rearrange("p b c -> p (b c)"), scr.xl[s.idx()]).then_inc(x_in, 16)

            def store(s):
                for t in range(NCH):
                    sp.wait_ge(down_read, s.val(NCH, t + 1))
                    sp.dma_start(o_v[s.val(NCH, t)], yr[:, t % 2, :]).then_inc(y_out[t % 2], 16)

            load_coef(0)
            load_x(At(None, 0))
            for k in range(1, 4):
                load_coef(k)
            load_x(At(None, 1))
            sp.wait_ge(w_made, IB)
            for k in range(4):
                bs = slice(IB // 4 * k, IB // 4 * (k + 1))
                sp.dma_start(scr.down.rearrange("(b p) n -> p b n", p=128)[:, bs, :],
                             dn[:, bs].rearrange("p b a n -> p b (a n)")).then_inc(down_stored, 16)
            load_x(At(None, 2))
            store(At(None, 0))
            with sp.Fori(0, nst - 3) as r:
                load_x(At(r, 3))
                store(At(r, 1))
            store(At(None, nst - 2))
            store(At(None, nst - 1))
            for i in range(2):
                sp.wait_ge(y_out[i], 16 * NCH // 2 * nst)

        @block.gpsimd
        def _(pool):
            g_ = nc.gpsimd

            def load_y(s, t):
                if not (s.first() and t < 2):
                    pool.wait_ge(y_out[t % 2], s.val(16 * NCH // 2, 16 * (t // 2)))
                pool.dma_start(yr[:, t % 2, :], y_v[s.idx(), t]).then_inc(y_in[t % 2], 16)

            def gather(out, g, src, arrived):
                pool.indirect_dma_start(out, None, src, bass.IndirectOffsetOnAxis(ap=member[:, g:g + 1], axis=0)
                                        ).then_inc(arrived, 16)

            pool.wait_ge(member_in, 16)
            for g in range(IB):
                gather(cg[:, ROW * g:ROW * (g + 1)], g, scr.rows, cubics_in)
            g_.memset(ident[:], 0.0).then_inc(ident_made, 1)
            pool.wait_ge(ident_made, 1)
            g_.affine_select(out=ident[:], in_=ident[:], compare_op=ALU.not_equal, fill=1.0, base=0,
                             pattern=[[-1, 128]], channel_multiplier=1).then_inc(ident_made, 1)
            pool.wait_ge(tables_in, 32)
            pool.wait_ge(cubics_in, 16 * IB)
            step = 0

            def link(ins):
                nonlocal step
                step += 1
                ins.then_inc(early_step, 1)
                pool.wait_ge(early_step, step)

            for m in range(2):
                link(g_.tensor_copy(cf[:, m, :, 0:4], cubic[:, :, m, 0, :]))
                for k in range(3):
                    at_samples(early[:, m], m, 0, g_, k, link)
            for k in range(3):
                at_samples(cf[:, 1, :, 8:NF], 1, 1, g_, k, link)
            assert step == EARLY_STEPS
            pool.wait_ge(down_stored, 4 * 16)
            for g in range(IB):
                gather(dw[:, g].rearrange("p a n -> p (a n)"), g, scr.down, down_in)
            for t in range(NCH):
                load_y(At(None, 0), t)
            with pool.Fori(0, nst - 2) as r:
                for t in range(NCH):
                    load_y(At(r, 1), t)
            for t in range(NCH):
                load_y(At(None, nst - 1), t)

        @block.tensor
        def _(pe):
            def polynomial(q):
                if q % 4 == 0:
                    pe.wait_ge(coef_in[q // 4], 64)
                if q >= 3:
                    pe.wait_ge(picked, q - 2)
                for a, ps in enumerate(pairs[q % 3]):
                    ins = nc.tensor.matmul(ps[:], powers[:], coef[:, a, q, :], start=True, stop=True)
                ins.then_inc(poly_made, 1)

            def features(s, k):
                if not (s.first() and k < 2):
                    pe.wait_ge(feat_ready, s.val(NP, k - 1))
                if s.first() and k % 2 == 0:
                    pe.wait_ge(basis_in[k // 2], 32)
                ps = pf[k % 2]
                for hb in range(HB):
                    f_h, f_l = b_hi[:, k, hb, :], b_lo[:, k, hb, :]
                    nc.tensor.matmul(ps[:], f_h, x_hi[:, hb, :], start=hb == 0, stop=False)
                    nc.tensor.matmul(ps[:], f_h, x_lo[:, hb, :], start=False, stop=False)
                    ins = nc.tensor.matmul(ps[:], f_l, x_hi[:, hb, :], start=False, stop=hb == HB - 1)
                ins.then_inc(feat_made, 1)

            def turn_coefficients(n):
                if n >= 2:
                    pe.wait_ge(turned_lo, 2 * (n - 1))
                m, k0 = n % 2, 4 * (n // 2)
                flat = cf[:, m].rearrange("p c f -> p (c f)")
                for k in range(4):
                    ins = nc.tensor.transpose(pd[n % 2][:, 128 * k:128 * k + 128],
                                              flat[:, 128 * (k0 + k):128 * (k0 + k + 1)], ident[:])
                ins.then_inc(turned_made, 1)

            def gate_up(s, i, m):
                ps, made, read = ((pg[i % 2], gate_made, sg_ready), (pu[i % 2], up_made, h_ready))[m]
                if not (s.first() and i < 2):
                    pe.wait_ge(read, s.val(IB, i - 1))
                if s.first() and i % 8 == 0 and m == 0:
                    pe.wait_ge(hi_copied, 4 * (i // 8 + 1))
                    pe.wait_ge(lo_copied, 4 * (i // 8 + 1))
                if m == 0 and i % 2 == 0:
                    pe.wait_ge(feat_ready, s.val(NP, i // 2 + 1))
                nc.tensor.matmul(ps[:], c_hi[:, m, i, :], f[:, i, :], start=True, stop=False)
                nc.tensor.matmul(ps[:], c_lo[:, m, i, :], f[:, i, :], start=False, stop=True).then_inc(made, 1)

            def down(s, t):
                if not (s.first() and t < 2):
                    pe.wait_ge(down_read, s.val(NCH, t - 1))
                ps, tok = pd[t % 2], slice(CH * t, CH * t + CH)
                for i in range(IB):
                    if t == 0 and i in (0, IB - 2, IB - 1):
                        pe.wait_ge(it_ready, s.val(IB, max(i + 1, IB - 2)))
                    nc.tensor.matmul(ps[:], it_hi[:, i, tok], dw[:, i, 0, :], start=i == 0, stop=False)
                    nc.tensor.matmul(ps[:], it_hi[:, i, tok], dw[:, i, 1, :], start=False, stop=False)
                    ins = nc.tensor.matmul(ps[:], it_lo[:, i, tok], dw[:, i, 0, :], start=False, stop=i == IB - 1)
                ins.then_inc(down_made, 1)

            def groups(s, following):
                if following is not None:
                    pe.wait_ge(x_in, following.val(32, 32))
                for k in range(NP):
                    for i in (2 * k, 2 * k + 1):
                        gate_up(s, i, 0)
                        gate_up(s, i, 1)
                    if following is not None:
                        features(following, k)

            s0 = At(None, 0)
            pe.wait_ge(powers_ready, 1)
            for q in range(5):
                polynomial(q)
            pe.wait_ge(x_in, 32)
            for k in range(NP):
                features(s0, k)
                for q in (2 * k + 5, 2 * k + 6):
                    if q < IB:
                        polynomial(q)
            pe.wait_ge(ident_made, 2)
            pe.wait_ge(early_step, EARLY_STEPS)
            pe.wait_ge(single_step, SINGLE_STEPS)
            pe.wait_ge(picked, IB)
            for n in range(TURNS):
                turn_coefficients(n)
            groups(s0, At(None, 1))
            pe.wait_ge(down_in, 16 * IB)
            for t in range(NCH):
                down(s0, t)
            with pe.Fori(0, nst - 2) as r:
                groups(At(r, 1), At(r, 2))
                for t in range(NCH):
                    down(At(r, 1), t)
            last = At(None, nst - 1)
            groups(last, None)
            for t in range(NCH):
                down(last, t)

        @block.scalar
        def _(act):
            sc = nc.scalar

            act.dma_start(member[:], A.member).then_inc(member_in, 16)
            act.dma_start(pow_in[:], A.powers).then_inc(const_in, 16)

            def load_functions(k):
                cols = slice(2 * HB * 128 * k, 2 * HB * 128 * (k + 1))
                for functions, src in ((b_hi, A.basis_hi), (b_lo, A.basis_lo)):
                    act.dma_start(functions[:, 2 * k:2 * k + 2].rearrange("p k b f -> p (k b f)"), src[:, cols]
                                  ).then_inc(basis_in[k], 16)

            load_functions(0)

            def first_cubic(q):
                act.wait_ge(poly_made, q + 1)
                if q >= 3:
                    act.wait_ge(w_made, q - 2)
                sc.activation(wt[:, q % 3, :], pairs[q % 3][0][:], ACT.Copy).then_inc(first_copied, 1)

            def weight_hi(q):
                act.wait_ge(picked, q + 1)
                sc.activation(down_block(0, q), by_block(wt[:, q % 3, :]), ACT.Copy).then_inc(w_hi_made, 1)

            def feature_hi(s, k):
                act.wait_ge(feat_made, s.val(NP, k + 1))
                if not s.first():
                    act.wait_ge(up_made, s.val(IB, 2 * k + 2 - IB))
                sc.activation(f[LOW, 2 * k, :], pf[k % 2][LOW, :], ACT.Copy, scale=1.0 / W_SCALE).then_inc(feat_hi, 1)
                sc.activation(f[HIGH, 2 * k + 1, :], pf[k % 2][HIGH, :], ACT.Copy, scale=1.0 / W_SCALE).then_inc(feat_hi, 1)

            def turned_high(n):
                act.wait_ge(turned_made, n + 1)
                for e, (own, other) in enumerate(HALVES):
                    sc.activation(turned(c_hi, n, e, own), turned_from(n, e), ACT.Copy, scale=W_SCALE).then_inc(turned_hi, 1)
                for e, (own, other) in enumerate(HALVES):
                    act.wait_ge(turned_hi, 2 * n + e + 1)
                    sc.activation(turned(c_hi, n, e, other), turned(c_hi, n, e, own), ACT.Copy).then_inc(hi_copied, 1)

            def gated(s, i):
                act.wait_ge(gate_made, s.val(IB, i + 1))
                if not (s.first() and i < 2):
                    act.wait_ge(h_ready, s.val(IB, i - 1))
                sc.activation(sg[:, i % 2, :], pg[i % 2][:], ACT.Silu, scale=1.0 / W_SCALE).then_inc(sg_ready, 1)

            def inter_hi(s, i):
                act.wait_ge(h_ready, s.val(IB, i + 1))
                sc.activation(it_hi[:, i, :], hh[:, i % 2, :], ACT.Copy).then_inc(hi_ready, 1)

            def groups(s, following):
                for k in range(NP):
                    for i in (2 * k, 2 * k + 1):
                        gated(s, i)
                        if i >= 1:
                            inter_hi(s, i - 1)
                    if following is not None and k >= 1:
                        feature_hi(following, k - 1)
                inter_hi(s, IB - 1)
                if following is not None:
                    feature_hi(following, NP - 1)

            def make(q):
                if q < IB:
                    first_cubic(q)
                if 1 <= q <= IB:
                    weight_hi(q - 1)

            s0 = At(None, 0)
            for k in range(NP):
                make(2 * k)
                make(2 * k + 1)
                if k == 0:
                    act.dma_start(tables, A.tables.partition_broadcast(128)).then_inc(tables_in, 16)
                    act.dma_start(gknot, A.gknot).then_inc(tables_in, 16)
                if k < 3:
                    load_functions(k + 1)
                if k >= 1:
                    feature_hi(s0, k - 1)
            make(IB)
            feature_hi(s0, NP - 1)
            for n in range(TURNS):
                turned_high(n)
            groups(s0, At(None, 1))
            with act.Fori(0, nst - 2) as r:
                groups(At(r, 1), At(r, 2))
            groups(At(None, nst - 1), None)

        @block.vector
        def _(dve):
            v = nc.vector

            def pick(q):
                dve.wait_ge(first_copied, q + 1)
                if q % 4 == 0:
                    dve.wait_ge(coef_in[q // 4], 64)
                v.copy_predicated(wt[:, q % 3, :], later[:, q, :], pairs[q % 3][1][:]).then_inc(picked, 1)

            def weight_lo(q):
                dve.wait_ge(w_hi_made, q + 1)
                v.tensor_tensor(down_block(1, q), by_block(wt[:, q % 3, :]), down_block(0, q), ALU.subtract).then_inc(w_made, 1)

            def feature_lo(s, k):
                dve.wait_ge(feat_hi, s.val(2 * NP, 2 * k + 1))
                v.scalar_tensor_tensor(out=f[HIGH, 2 * k, :], in0=pf[k % 2][LOW, :], scalar=1.0 / W_SCALE,
                                       in1=f[LOW, 2 * k, :], op0=ALU.mult, op1=ALU.subtract).then_inc(feat_lo, 1)
                dve.wait_ge(feat_hi, s.val(2 * NP, 2 * k + 2))
                v.scalar_tensor_tensor(out=f[LOW, 2 * k + 1, :], in0=pf[k % 2][HIGH, :], scalar=1.0 / W_SCALE,
                                       in1=f[HIGH, 2 * k + 1, :], op0=ALU.mult, op1=ALU.subtract).then_inc(feat_ready, 1)

            step = 0

            def link(ins):
                nonlocal step
                step += 1
                ins.then_inc(single_step, 1)
                dve.wait_ge(single_step, step)

            def sample_masks():
                dve.wait_ge(tables_in, 32)
                wide = gknot.unsqueeze(2).broadcast_to([128, NG, NW])
                link(v.tensor_tensor(before, wide, sample, ALU.is_gt))
                link(v.tensor_tensor(past, wide, turn.unsqueeze(2).broadcast_to([128, NG, NW]), ALU.is_gt))

            def next_cubic(m):
                link(v.tensor_copy(cf[:, m, :, 4:8], cubic[:, :, m, 1, :]))
                link(v.copy_predicated(cf[:, m, :, 4:8], past[:, :, 0:4], cubic[:, :, m, 0, :]))

            def first_samples(m):
                dve.wait_ge(early_step, (1 + HORNER, EARLY_STEPS)[m])
                link(v.copy_predicated(cf[:, m, :, 8:NF], before, early[:, m]))

            def turned_low(n):
                for e, (own, other) in enumerate(HALVES):
                    dve.wait_ge(turned_hi, 2 * n + e + 1)
                    v.scalar_tensor_tensor(out=turned(c_lo, n, e, own), in0=turned_from(n, e), scalar=W_SCALE,
                                           in1=turned(c_hi, n, e, own), op0=ALU.mult, op1=ALU.subtract).then_inc(turned_lo, 1)
                for e, (own, other) in enumerate(HALVES):
                    dve.wait_ge(turned_lo, 2 * n + e + 1)
                    v.tensor_copy(turned(c_lo, n, e, other), turned(c_lo, n, e, own)).then_inc(lo_copied, 1)

            def product(s, i):
                dve.wait_ge(sg_ready, s.val(IB, i + 1))
                dve.wait_ge(up_made, s.val(IB, i + 1))
                if not (s.first() and i < 2):
                    dve.wait_ge(it_ready, s.val(IB, i - 1))
                v.tensor_tensor(hh[:, i % 2, :], sg[:, i % 2, :], pu[i % 2][:], ALU.mult).then_inc(h_ready, 1)

            def inter_lo(s, i):
                dve.wait_ge(hi_ready, s.val(IB, i + 1))
                v.tensor_tensor(it_lo[:, i, :], hh[:, i % 2, :], it_hi[:, i, :], ALU.subtract).then_inc(it_ready, 1)

            def finish(s, t):
                dve.wait_ge(down_made, s.val(NCH, t + 1))
                dve.wait_ge(y_in[t % 2], s.val(16 * NCH // 2, 16 * (t // 2 + 1)))
                v.scalar_tensor_tensor(out=yr[:, t % 2, :], in0=pd[t % 2][:], scalar=W_SCALE ** -2, in1=yr[:, t % 2, :],
                                       op0=ALU.mult, op1=ALU.add).then_inc(down_read, 1)

            def groups(s, following):
                for k in range(NP):
                    for i in (2 * k, 2 * k + 1):
                        product(s, i)
                        if i >= 1:
                            inter_lo(s, i - 1)
                    if following is not None and k >= 1:
                        feature_lo(following, k - 1)
                inter_lo(s, IB - 1)
                if following is not None:
                    feature_lo(following, NP - 1)

            def finish_all(s):
                for t in range(NCH):
                    finish(s, t)

            def make(q):
                if q < IB:
                    pick(q)
                if 1 <= q <= IB:
                    weight_lo(q - 1)

            s0 = At(None, 0)
            dve.wait_ge(const_in, 16)
            v.tensor_copy(powers[:], pow_in[:]).then_inc(powers_ready, 1)
            for k in range(NP):
                make(2 * k)
                make(2 * k + 1)
                if k >= 1:
                    feature_lo(s0, k - 1)
                if k == 1:
                    sample_masks()
                if k == 2:
                    dve.wait_ge(cubics_in, 16 * IB)
                if 2 <= k < 5:
                    at_samples(cf[:, 0, :, 8:NF], 0, 1, v, k - 2, link)
                if k in (5, 6):
                    next_cubic(k - 5)
                if k == 7:
                    first_samples(0)
            make(IB)
            first_samples(1)
            feature_lo(s0, NP - 1)
            assert step == SINGLE_STEPS
            for n in range(TURNS):
                turned_low(n)
            groups(s0, At(None, 1))
            finish_all(s0)
            with dve.Fori(0, nst - 2) as r:
                groups(At(r, 1), At(r, 2))
                finish_all(At(r, 1))
            groups(At(None, nst - 1), None)
            finish_all(At(None, nst - 1))


class Arrays:

    def __init__(self, aps, out, runs):
        self.x = aps["x"].rearrange("a t d -> (a t) d")
        self.out = out.rearrange("a t d -> (a t) d")
        self.Wq, self.Wk, self.Wv, self.Wg, self.Wo = (aps[n] for n in ("Wq", "Wk", "Wv", "Wg", "Wo"))
        self.Wa, self.Wb, self.A_log, self.dt_bias, self.nw = (aps[n] for n in ("Wa", "Wb", "A_log", "dt_bias", "nw"))
        self.cwq, self.cwk, self.cwv = (aps[n] for n in ("cwq", "cwk", "cwv"))
        self.gate_cp, self.up_cp, self.down_cp = (aps[n] for n in ("gate_cp", "up_cp", "down_cp"))
        self.frac, self.later, self.powers = (aps[n] for n in ("frac", "later", "powers"))
        self.basis_hi, self.basis_lo, self.tables, self.gknot, self.member = (
            aps[n] for n in ("basis_hi", "basis_lo", "tables", "gknot", "member"))
        self.runs = runs


class Scratch:

    def __init__(self, dram):
        self.pad, self.ctrl = dram("pad", [3, NCP + 3]), dram("ctrl_cols", [3, 5, NCOL])
        self.rows = dram("coef_rows", [INTER, ROW])
        self.coef = dram("coef_down", [2, 4, 2, NCOL], F16)
        self.down = dram("down_rows", [INTER, 2 * D], F16)
        self.y = dram("y_attn", [T_ALL, D])
        self.xh, self.xl = dram("xn_hi", [NST, 128, HB * ST], F16), dram("xn_lo", [NST, 128, HB * ST], F16)
        self.b, self.t, self.tt = (dram(n, [NSUB, NCH * NH, SUB, SUB]) for n in ("b_blocks", "t_blocks", "tt_blocks"))


class Persistent:

    def __init__(self, sb):
        self.w_hi, self.w_lo = sb("w_hi", [128, HB, WCOLS], F16), sb("w_lo", [128, HB, WCOLS], F16)
        self.wo_hi, self.wo_lo = sb("wo_hi", [128, NH, D], F16), sb("wo_lo", [128, NH, D], F16)
        self.wab_hi, self.wab_lo = sb("wab_hi", [128, HB, 2 * NH], F16), sb("wab_lo", [128, HB, 2 * NH], F16)
        self.taps, self.dtb, self.nega = sb("taps", [128, NBLK, TAPS]), sb("dtb", [128, NH]), sb("nega", [128, NH])
        self.ident, self.ones, self.after, self.upto, self.level32 = (
            sb(n, [128, 128]) for n in ("ident", "ones", "after", "upto", "level32"))
        self.pair = sb("pair", [128, 2])
        self.mhalf, self.phalf = sb("mhalf", [128, NCH * NH]), sb("phalf", [128, NCH * NH])
        self.S, self.halo, self.zeros = (
            sb("S", [128, NPAIR, DV]), sb("halo", [128, NBLK, TAPS - 1]), sb("zeros", [128, TAPS - 1]))


def build(nc, A, nst=NST):
    def dram(name, shape, dt=F32):
        return nc.dram_tensor(name, shape, dt, kind="Internal").ap()

    scr = Scratch(dram)
    with ExitStack() as ctx:
        def sb(name, shape, dt=F32):
            return ctx.enter_context(nc.sbuf_tensor(name, shape, dt))

        P = Persistent(sb)
        attend(nc, A, scr, P, nst)
    feed(nc, A, scr, nst)


_INS = dict(x="L0_attn_hidden_states", Wq="L0_attn_Wq", Wk="L0_attn_Wk", Wv="L0_attn_Wv", Wa="L0_attn_Wa",
            Wb="L0_attn_Wb", Wg="L0_attn_Wg", Wo="L0_attn_Wo", cwq="L0_attn_conv_wq", cwk="L0_attn_conv_wk",
            cwv="L0_attn_conv_wv", A_log="L0_attn_A_log", dt_bias="L0_attn_dt_bias", nw="L0_attn_norm_weight",
            gate_cp="L0_ffn_gate_cp", up_cp="L0_ffn_up_cp", down_cp="L0_ffn_down_cp")


def kernel(**inputs):
    import concourse.bacc as bacc
    from concourse.bass_utils import run_bass_kernel_spmd

    nc = bacc.Bacc("TRN2", target_bir_lowering=False, num_devices=1)
    arrays = {short: np.ascontiguousarray(inputs[name]) for short, name in _INS.items()}
    runs, consts = spline_shapes()
    arrays.update(consts)
    aps = {n: nc.dram_tensor(f"in_{n}", a.shape, mybir.dt.from_np(a.dtype), kind="ExternalInput").ap()
           for n, a in arrays.items()}
    out = nc.dram_tensor("out", [1, T_ALL, D], F32, kind="ExternalOutput").ap()
    build(nc, Arrays(aps, out, runs))
    r = run_bass_kernel_spmd(nc, [{f"in_{n}": a for n, a in arrays.items()}], core_ids=[0])
    return r.results[0]["out"]
```
